# Optimizing a Trainium2 kernel written in Bass

```python
import numpy as np
import jax
import jax.numpy as jnp

def _softmax(x, axis=-1):
    return jax.nn.softmax(x, axis=axis)

def _gelu(x):
    return jax.nn.gelu(x, approximate=True)

def _silu(x):
    return jax.nn.silu(x)

def _sigmoid(x):
    return jax.nn.sigmoid(x)

def _layernorm(x, axis=-1, eps=1e-05):
    m = jnp.mean(x, axis=axis, keepdims=True)
    v = jnp.var(x, axis=axis, keepdims=True)
    return (x - m) / jnp.sqrt(v + eps)

def _scatter_add(tgt, idx, src, axis=0):
    return tgt.at[idx].add(src)

def _segment_sum(src, seg, n):
    return jax.ops.segment_sum(src, seg, n)
kernel_name = 'mk_decoder_preln_d2_seqx_r8_5d44d4'

def setup_inputs(seed: int=0):
    np.random.seed(seed)
    _w = jnp.asarray

    def _rec_inputs():
        import jax
        import jax.numpy as jnp
        _rk = jax.random.key(seed)
        x = -0.0002928 + 1 * jax.random.normal(jax.random.fold_in(_rk, 1), (128, 64, 128), jnp.float32)
        _lenS = 64 - jax.random.randint(jax.random.fold_in(_rk, 7), (128,), 0, max(1, 64 // 4) + 1, jnp.int32)
        _lenS2 = 64 - jax.random.randint(jax.random.fold_in(_rk, 8), (128,), 0, max(1, 64 // 4) + 1, jnp.int32)
        _ctx_1024P = jax.random.normal(jax.random.fold_in(_rk, 11), (128, 16, 128), jnp.float32)
        _ctx_1024c = jax.random.dirichlet(jax.random.fold_in(_rk, 511), 0.3 * jnp.ones((16,), jnp.float32), (128, 64))
        _ctx_1024t = jnp.einsum('bsk,bkd->bsd', _ctx_1024c, _ctx_1024P)
        _ctx_1024t = _ctx_1024t * jax.lax.rsqrt(jnp.mean(jnp.square(_ctx_1024t)) + 1e-12) * 0.953939
        ctx_1024 = -1.39393e-06 + 0.999914 * (_ctx_1024t + 0.3 * jax.random.normal(jax.random.fold_in(_rk, 611), (128, 64, 128), jnp.float32))
        return (x, ctx_1024)
    x, ctx_1024 = _rec_inputs()

    def _L0_attn_setup():
        import jax, jax.numpy as jnp
        import numpy as np
        D_MODEL = 128
        N_HEADS = 16
        HEAD_DIM = D_MODEL // N_HEADS
        ROPE_THETA = 10000.0
        EPS = 1e-06
        PAD_VAL = 1.0

        def _rope(x, cos, sin):
            x1 = x[..., 0::2]
            x2 = x[..., 1::2]
            r1 = x1 * cos - x2 * sin
            r2 = x1 * sin + x2 * cos
            return jnp.stack([r1, r2], axis=-1).reshape(x.shape)
        key = jax.random.key(seed)
        ks = jax.random.split(key, 5)
        w_scale = 1.0 / np.sqrt(D_MODEL)
        return {'x': jax.random.normal(ks[0], (4, 512, D_MODEL), jnp.float32), 'Wq': jax.random.normal(ks[1], (D_MODEL, D_MODEL), jnp.float32) * w_scale, 'Wk': jax.random.normal(ks[2], (D_MODEL, D_MODEL), jnp.float32) * w_scale, 'Wv': jax.random.normal(ks[3], (D_MODEL, D_MODEL), jnp.float32) * w_scale, 'Wo': jax.random.normal(ks[4], (D_MODEL, D_MODEL), jnp.float32) * w_scale}
    _L0_attn_all = _L0_attn_setup()
    _L0_attn_in = {k: v for k, v in _L0_attn_all.items() if k in ('Wq', 'Wk', 'Wv', 'Wo')}
    del _L0_attn_all

    def _L0_xattn_setup():
        import jax, jax.numpy as jnp
        import numpy as np
        B, S, D, NH = (2, 256, 128, 8)
        DH = D // NH
        EPS = 1e-06
        LN_EPS = 1e-05

        def _mlstm_cell(q, k, v, igate_w, igate_b, fgate_w, fgate_b, ln_scale):
            Slen = q.shape[0]
            ifg = jnp.concatenate([q, k, v], axis=-1)
            ig = (ifg @ igate_w.T + igate_b).T
            fg = (ifg @ fgate_w.T + fgate_b).T
            qh = q.reshape(Slen, NH, DH).transpose(1, 0, 2)
            kh = k.reshape(Slen, NH, DH).transpose(1, 0, 2)
            vh = v.reshape(Slen, NH, DH).transpose(1, 0, 2)
            log_f = jax.nn.log_sigmoid(fg)
            cs = jnp.cumsum(log_f, axis=1)
            fg_mat = cs[:, :, None] - cs[:, None, :]
            mask = jnp.tril(jnp.ones((Slen, Slen), dtype=bool))
            log_fg_mat = jnp.where(mask, fg_mat, -jnp.inf)
            log_D = log_fg_mat + ig[:, None, :]
            max_log_D = jnp.max(log_D, axis=-1, keepdims=True)
            D_mat = jnp.exp(log_D - max_log_D)
            qk = jnp.einsum('hsd,htd->hst', qh, kh) / np.sqrt(DH)
            C = qk * D_mat
            normalizer = jnp.maximum(jnp.abs(C.sum(axis=-1, keepdims=True)), jnp.exp(-max_log_D))
            h = jnp.einsum('hst,htd->hsd', C / (normalizer + EPS), vh)
            h = h.transpose(1, 0, 2).reshape(Slen, D)
            mu = h.mean(axis=-1, keepdims=True)
            var = h.var(axis=-1, keepdims=True)
            return (h - mu) / jnp.sqrt(var + LN_EPS) * ln_scale
        key = jax.random.key(seed)
        ks = jax.random.split(key, 8)
        rnd = lambda k, sh, s=1.0: jax.random.normal(k, sh, dtype=jnp.float32) * s
        return {'q': rnd(ks[0], (B, S, D)), 'k': rnd(ks[1], (B, S, D)), 'v': rnd(ks[2], (B, S, D)), 'igate_w': rnd(ks[3], (NH, 3 * D), 0.02), 'igate_b': jnp.linspace(3.0, 6.0, NH, dtype=jnp.float32), 'fgate_w': rnd(ks[4], (NH, 3 * D), 0.02), 'fgate_b': rnd(ks[5], (NH,), 0.3162278), 'ln_scale': jnp.ones((D,), dtype=jnp.float32)}
    _L0_xattn_all = _L0_xattn_setup()
    _L0_xattn_in = {k: v for k, v in _L0_xattn_all.items() if k in ('igate_w', 'igate_b', 'fgate_w', 'fgate_b', 'ln_scale')}
    del _L0_xattn_all

    def _L0_ffn_setup():
        import jax, jax.numpy as jnp
        import numpy as np
        D = 128
        H = 96
        E = 8
        K = 2
        NS = 2
        ROUTE_SCALE = 1.0

        def _gated_mlp(x, w1, w2):
            h = x @ w1.T
            y, g = jnp.split(h, 2, axis=-1)
            return y * jax.nn.silu(g) @ w2.T
        key = jax.random.key(seed)
        ks = jax.random.split(key, 6)
        s = 0.02
        return {'x': jax.random.normal(ks[0], (2, 128, D), jnp.float32), 'gate_w': jax.random.normal(ks[1], (E, D), jnp.float32) * s, 'W1': jax.random.normal(ks[2], (E, 2 * H, D), jnp.float32) * s, 'W2': jax.random.normal(ks[3], (E, D, H), jnp.float32) * s, 'Ws1': jax.random.normal(ks[4], (2 * NS * H, D), jnp.float32) * s, 'Ws2': jax.random.normal(ks[5], (D, NS * H), jnp.float32) * s}
    _L0_ffn_all = _L0_ffn_setup()
    _L0_ffn_in = {k: v for k, v in _L0_ffn_all.items() if k in ('gate_w', 'W1', 'W2', 'Ws1', 'Ws2')}
    del _L0_ffn_all

    def _L1_attn_setup():
        import jax, jax.numpy as jnp
        import numpy as np
        D_MODEL = 128
        NUM_HEADS = 16
        D_HEAD = D_MODEL // NUM_HEADS
        LN_EPS = 1e-05

        def apply_rope(x):
            L = x.shape[2]
            inv_freq = 1.0 / 10000.0 ** (jnp.arange(0, D_HEAD, 2, dtype=jnp.float32) / D_HEAD)
            freqs = jnp.arange(L, dtype=jnp.float32)[:, None] * inv_freq[None, :]
            sin = jnp.sin(freqs)[None, None]
            cos = jnp.cos(freqs)[None, None]
            x1 = x[..., ::2]
            x2 = x[..., 1::2]
            rot = jnp.stack([x1 * cos - x2 * sin, x1 * sin + x2 * cos], axis=-1)
            return rot.reshape(x.shape)
        key = jax.random.key(seed)
        ks = jax.random.split(key, 10)
        B, L = (4, 256)
        s = 1.0 / np.sqrt(D_MODEL)
        inp = {'x': jax.random.normal(ks[0], (B, L, D_MODEL), dtype=jnp.float32), 'ln_gamma': jnp.ones((D_MODEL,), jnp.float32), 'ln_beta': jnp.zeros((D_MODEL,), jnp.float32), 'Wq': jax.random.normal(ks[1], (D_MODEL, D_MODEL), jnp.float32) * s, 'bq': jnp.zeros((D_MODEL,), jnp.float32), 'Wk': jax.random.normal(ks[2], (D_MODEL, D_MODEL), jnp.float32) * s, 'bk': jnp.zeros((D_MODEL,), jnp.float32), 'Wv': jax.random.normal(ks[3], (D_MODEL, D_MODEL), jnp.float32) * s, 'bv': jnp.zeros((D_MODEL,), jnp.float32), 'Wo': jax.random.normal(ks[4], (D_MODEL, D_MODEL), jnp.float32) * s, 'bo': jnp.zeros((D_MODEL,), jnp.float32)}
        return inp
    _L1_attn_all = _L1_attn_setup()
    _L1_attn_in = {k: v for k, v in _L1_attn_all.items() if k in ('ln_gamma', 'ln_beta', 'Wq', 'bq', 'Wk', 'bk', 'Wv', 'bv', 'Wo', 'bo')}
    del _L1_attn_all

    def _L1_xattn_setup():
        import jax, jax.numpy as jnp
        import numpy as np
        D_MODEL = 128
        NUM_HEADS = 16
        D_K = D_MODEL // NUM_HEADS
        key = jax.random.key(seed)
        ks = jax.random.split(key, 11)
        B, S = (4, 256)
        s = 1.0 / np.sqrt(D_MODEL)
        inp = {'Q': jax.random.normal(ks[0], (B, S, D_MODEL), jnp.float32), 'K': jax.random.normal(ks[1], (B, S, D_MODEL), jnp.float32), 'V': jax.random.normal(ks[2], (B, S, D_MODEL), jnp.float32), 'Wq': jax.random.normal(ks[3], (D_MODEL, D_MODEL), jnp.float32) * s, 'bq': jax.random.normal(ks[4], (D_MODEL,), jnp.float32) * s, 'Wk': jax.random.normal(ks[5], (D_MODEL, D_MODEL), jnp.float32) * s, 'bk': jax.random.normal(ks[6], (D_MODEL,), jnp.float32) * s, 'Wv': jax.random.normal(ks[7], (D_MODEL, D_MODEL), jnp.float32) * s, 'bv': jax.random.normal(ks[8], (D_MODEL,), jnp.float32) * s, 'Wo': jax.random.normal(ks[9], (D_MODEL, D_MODEL), jnp.float32) * s, 'bo': jax.random.normal(ks[10], (D_MODEL,), jnp.float32) * s}
        return inp
    _L1_xattn_all = _L1_xattn_setup()
    _L1_xattn_in = {k: v for k, v in _L1_xattn_all.items() if k in ('Wq', 'bq', 'Wk', 'bk', 'Wv', 'bv', 'Wo', 'bo')}
    del _L1_xattn_all

    def _L1_ffn_setup():
        import jax, jax.numpy as jnp
        import numpy as np
        B, S, D, DO = (4, 256, 128, 128)
        E, K = (20, 2)
        key = jax.random.key(seed)
        ks = jax.random.split(key, 6)
        sc_d = 1.0 / np.sqrt(D)
        sc_h = 1.0 / np.sqrt(D // 4)
        return {'x': jax.random.normal(ks[0], (B, S, D), jnp.float32), 'wg1': jax.random.normal(ks[1], (D, D // 4), jnp.float32) * sc_d, 'bg1': jnp.zeros((D // 4,), jnp.float32), 'wg2': jax.random.normal(ks[2], (D // 4, 2 * E), jnp.float32) * sc_h, 'bg2': jnp.zeros((2 * E,), jnp.float32), 'We': jax.random.normal(ks[3], (E, D, DO), jnp.float32) * sc_d, 'be': jnp.zeros((E, DO), jnp.float32)}
    _L1_ffn_all = _L1_ffn_setup()
    _L1_ffn_in = {k: v for k, v in _L1_ffn_all.items() if k in ('wg1', 'bg1', 'wg2', 'bg2', 'We', 'be')}
    del _L1_ffn_all
    return {'x': x, 'ctx_1024': ctx_1024, 'L0_attn_Wq': _L0_attn_in['Wq'], 'L0_attn_Wk': _L0_attn_in['Wk'], 'L0_attn_Wv': _L0_attn_in['Wv'], 'L0_attn_Wo': _L0_attn_in['Wo'], 'L0_xattn_igate_w': _L0_xattn_in['igate_w'], 'L0_xattn_igate_b': _L0_xattn_in['igate_b'], 'L0_xattn_fgate_w': _L0_xattn_in['fgate_w'], 'L0_xattn_fgate_b': _L0_xattn_in['fgate_b'], 'L0_xattn_ln_scale': _L0_xattn_in['ln_scale'], 'L0_ffn_gate_w': _L0_ffn_in['gate_w'], 'L0_ffn_W1': _L0_ffn_in['W1'], 'L0_ffn_W2': _L0_ffn_in['W2'], 'L0_ffn_Ws1': _L0_ffn_in['Ws1'], 'L0_ffn_Ws2': _L0_ffn_in['Ws2'], 'L1_attn_ln_gamma': _L1_attn_in['ln_gamma'], 'L1_attn_ln_beta': _L1_attn_in['ln_beta'], 'L1_attn_Wq': _L1_attn_in['Wq'], 'L1_attn_bq': _L1_attn_in['bq'], 'L1_attn_Wk': _L1_attn_in['Wk'], 'L1_attn_bk': _L1_attn_in['bk'], 'L1_attn_Wv': _L1_attn_in['Wv'], 'L1_attn_bv': _L1_attn_in['bv'], 'L1_attn_Wo': _L1_attn_in['Wo'], 'L1_attn_bo': _L1_attn_in['bo'], 'L1_xattn_Wq': _L1_xattn_in['Wq'], 'L1_xattn_bq': _L1_xattn_in['bq'], 'L1_xattn_Wk': _L1_xattn_in['Wk'], 'L1_xattn_bk': _L1_xattn_in['bk'], 'L1_xattn_Wv': _L1_xattn_in['Wv'], 'L1_xattn_bv': _L1_xattn_in['bv'], 'L1_xattn_Wo': _L1_xattn_in['Wo'], 'L1_xattn_bo': _L1_xattn_in['bo'], 'L1_ffn_wg1': _L1_ffn_in['wg1'], 'L1_ffn_bg1': _L1_ffn_in['bg1'], 'L1_ffn_wg2': _L1_ffn_in['wg2'], 'L1_ffn_bg2': _L1_ffn_in['bg2'], 'L1_ffn_We': _L1_ffn_in['We'], 'L1_ffn_be': _L1_ffn_in['be']}

def reference(x, ctx_1024, L0_attn_Wq, L0_attn_Wk, L0_attn_Wv, L0_attn_Wo, L0_xattn_igate_w, L0_xattn_igate_b, L0_xattn_fgate_w, L0_xattn_fgate_b, L0_xattn_ln_scale, L0_ffn_gate_w, L0_ffn_W1, L0_ffn_W2, L0_ffn_Ws1, L0_ffn_Ws2, L1_attn_ln_gamma, L1_attn_ln_beta, L1_attn_Wq, L1_attn_bq, L1_attn_Wk, L1_attn_bk, L1_attn_Wv, L1_attn_bv, L1_attn_Wo, L1_attn_bo, L1_xattn_Wq, L1_xattn_bq, L1_xattn_Wk, L1_xattn_bk, L1_xattn_Wv, L1_xattn_bv, L1_xattn_Wo, L1_xattn_bo, L1_ffn_wg1, L1_ffn_bg1, L1_ffn_wg2, L1_ffn_bg2, L1_ffn_We, L1_ffn_be):
    import jax
    import jax.numpy as jnp

    def _L0_attn_ref(x, Wq, Wk, Wv, Wo):
        import jax, jax.numpy as jnp
        import numpy as np
        D_MODEL = 128
        N_HEADS = 16
        HEAD_DIM = D_MODEL // N_HEADS
        ROPE_THETA = 10000.0
        EPS = 1e-06
        PAD_VAL = 1.0

        def _rope(x, cos, sin):
            x1 = x[..., 0::2]
            x2 = x[..., 1::2]
            r1 = x1 * cos - x2 * sin
            r2 = x1 * sin + x2 * cos
            return jnp.stack([r1, r2], axis=-1).reshape(x.shape)
        B, S, D = x.shape

        def split_heads(t):
            return t.reshape(B, S, N_HEADS, HEAD_DIM).transpose(0, 2, 1, 3)
        q = split_heads(x @ Wq)
        k = split_heads(x @ Wk)
        v = split_heads(x @ Wv)
        freqs = 1.0 / ROPE_THETA ** (jnp.arange(0, HEAD_DIM, 2, dtype=jnp.float32) / HEAD_DIM)
        ang = jnp.arange(S, dtype=jnp.float32)[:, None] * freqs[None, :]
        cos = jnp.cos(ang)[None, None]
        sin = jnp.sin(ang)[None, None]
        q = _rope(q, cos, sin)
        k = _rope(k, cos, sin)
        q = jax.nn.relu(q)
        k = jax.nn.relu(k)
        v_pad = jnp.pad(v, ((0, 0), (0, 0), (0, 0), (0, 1)), constant_values=PAD_VAL)
        vk = jnp.einsum('bhke,bhkd->bhed', v_pad, k)
        num = jnp.einsum('bhed,bhld->bhle', vk, q)
        attn = num[..., :-1] / (num[..., -1:] + EPS)
        out = attn.transpose(0, 2, 1, 3).reshape(B, S, D)
        return out @ Wo

    def _L0_xattn_ref(q, k, v, igate_w, igate_b, fgate_w, fgate_b, ln_scale):
        import jax, jax.numpy as jnp
        import numpy as np
        B, S, D, NH = (2, 256, 128, 8)
        DH = D // NH
        EPS = 1e-06
        LN_EPS = 1e-05

        def _mlstm_cell(q, k, v, igate_w, igate_b, fgate_w, fgate_b, ln_scale):
            Slen = q.shape[0]
            ifg = jnp.concatenate([q, k, v], axis=-1)
            ig = (ifg @ igate_w.T + igate_b).T
            fg = (ifg @ fgate_w.T + fgate_b).T
            qh = q.reshape(Slen, NH, DH).transpose(1, 0, 2)
            kh = k.reshape(Slen, NH, DH).transpose(1, 0, 2)
            vh = v.reshape(Slen, NH, DH).transpose(1, 0, 2)
            log_f = jax.nn.log_sigmoid(fg)
            cs = jnp.cumsum(log_f, axis=1)
            fg_mat = cs[:, :, None] - cs[:, None, :]
            mask = jnp.tril(jnp.ones((Slen, Slen), dtype=bool))
            log_fg_mat = jnp.where(mask, fg_mat, -jnp.inf)
            log_D = log_fg_mat + ig[:, None, :]
            max_log_D = jnp.max(log_D, axis=-1, keepdims=True)
            D_mat = jnp.exp(log_D - max_log_D)
            qk = jnp.einsum('hsd,htd->hst', qh, kh) / np.sqrt(DH)
            C = qk * D_mat
            normalizer = jnp.maximum(jnp.abs(C.sum(axis=-1, keepdims=True)), jnp.exp(-max_log_D))
            h = jnp.einsum('hst,htd->hsd', C / (normalizer + EPS), vh)
            h = h.transpose(1, 0, 2).reshape(Slen, D)
            mu = h.mean(axis=-1, keepdims=True)
            var = h.var(axis=-1, keepdims=True)
            return (h - mu) / jnp.sqrt(var + LN_EPS) * ln_scale
        return jax.vmap(lambda qq, kk, vv: _mlstm_cell(qq, kk, vv, igate_w, igate_b, fgate_w, fgate_b, ln_scale))(q, k, v)

    def _L0_ffn_ref(x, gate_w, W1, W2, Ws1, Ws2):
        import jax, jax.numpy as jnp
        import numpy as np
        D = 128
        H = 96
        E = 8
        K = 2
        NS = 2
        ROUTE_SCALE = 1.0

        def _gated_mlp(x, w1, w2):
            h = x @ w1.T
            y, g = jnp.split(h, 2, axis=-1)
            return y * jax.nn.silu(g) @ w2.T
        x_shape = x.shape
        xf = x.reshape(-1, D)
        T = xf.shape[0]
        scores = jax.nn.softmax((xf @ gate_w.T).astype(jnp.float32), axis=-1)
        top_vals, top_idx = jax.lax.top_k(scores, K)
        weights = (top_vals * ROUTE_SCALE).astype(x.dtype)
        w_dense = jnp.zeros((T, E), x.dtype).at[jnp.arange(T)[:, None], top_idx].set(weights)
        h = jnp.einsum('td,ehd->teh', xf, W1)
        y, g = jnp.split(h, 2, axis=-1)
        eo = jnp.einsum('teh,edh->ted', y * jax.nn.silu(g), W2)
        z = jnp.einsum('te,ted->td', w_dense, eo)
        z = z + _gated_mlp(xf, Ws1, Ws2)
        return z.reshape(x_shape)

    def _L1_attn_ref(x, ln_gamma, ln_beta, Wq, bq, Wk, bk, Wv, bv, Wo, bo):
        import jax, jax.numpy as jnp
        import numpy as np
        D_MODEL = 128
        NUM_HEADS = 16
        D_HEAD = D_MODEL // NUM_HEADS
        LN_EPS = 1e-05

        def apply_rope(x):
            L = x.shape[2]
            inv_freq = 1.0 / 10000.0 ** (jnp.arange(0, D_HEAD, 2, dtype=jnp.float32) / D_HEAD)
            freqs = jnp.arange(L, dtype=jnp.float32)[:, None] * inv_freq[None, :]
            sin = jnp.sin(freqs)[None, None]
            cos = jnp.cos(freqs)[None, None]
            x1 = x[..., ::2]
            x2 = x[..., 1::2]
            rot = jnp.stack([x1 * cos - x2 * sin, x1 * sin + x2 * cos], axis=-1)
            return rot.reshape(x.shape)
        B, L, _ = x.shape
        mu = jnp.mean(x, axis=-1, keepdims=True)
        var = jnp.mean(jnp.square(x - mu), axis=-1, keepdims=True)
        xn = (x - mu) * jax.lax.rsqrt(var + LN_EPS) * ln_gamma + ln_beta

        def heads(t):
            return t.reshape(B, L, NUM_HEADS, D_HEAD).transpose(0, 2, 1, 3)
        q = heads(xn @ Wq + bq)
        k = heads(xn @ Wk + bk)
        v = heads(xn @ Wv + bv)
        q = apply_rope(q)
        k = apply_rope(k)
        scores = jnp.einsum('bhid,bhjd->bhij', q, k) / jnp.sqrt(jnp.float32(D_HEAD))
        mask = jnp.tril(jnp.ones((L, L), jnp.float32))[None, None]
        scores = scores * mask + (1.0 - mask) * -1000000000.0
        probs = jax.nn.softmax(scores, axis=-1)
        out = jnp.einsum('bhij,bhjd->bhid', probs, v)
        out = out.transpose(0, 2, 1, 3).reshape(B, L, D_MODEL)
        out = out @ Wo + bo
        return x + out

    def _L1_xattn_ref(Q, K, V, Wq, bq, Wk, bk, Wv, bv, Wo, bo):
        import jax, jax.numpy as jnp
        import numpy as np
        D_MODEL = 128
        NUM_HEADS = 16
        D_K = D_MODEL // NUM_HEADS
        B, S, _ = Q.shape
        q = Q @ Wq + bq
        k = K @ Wk + bk
        v = V @ Wv + bv
        q = q.reshape(B, S, NUM_HEADS, D_K).transpose(0, 2, 1, 3)
        k = k.reshape(B, S, NUM_HEADS, D_K).transpose(0, 2, 1, 3)
        v = v.reshape(B, S, NUM_HEADS, D_K).transpose(0, 2, 1, 3)
        scale = 1.0 / jnp.sqrt(jnp.float32(D_K))
        scores = jnp.einsum('bhqd,bhkd->bhqk', q, k) * scale
        attn = jax.nn.softmax(scores, axis=-1)
        out = jnp.einsum('bhqk,bhkd->bhqd', attn, v)
        out = out.transpose(0, 2, 1, 3).reshape(B, S, D_MODEL)
        return out @ Wo + bo

    def _L1_ffn_ref(x, wg1, bg1, wg2, bg2, We, be):
        import jax, jax.numpy as jnp
        import numpy as np
        B, S, D, DO = (4, 256, 128, 128)
        E, K = (20, 2)
        Bv, Sv, Dv = x.shape
        xf = x.reshape(-1, Dv)
        h = jax.nn.gelu(xf @ wg1 + bg1, approximate=False)
        logits = (xf @ 0.0 + (h @ wg2 + bg2))[:, :E] if False else (h @ wg2 + bg2)[:, :E]
        probs = jax.nn.softmax(logits, axis=-1)
        top_vals, top_idx = jax.lax.top_k(probs, K)
        N = xf.shape[0]
        gates = jnp.zeros((N, E), xf.dtype).at[jnp.arange(N)[:, None], top_idx].set(top_vals)

        def body(y, eb):
            We_e, be_e, g_e = eb
            return (y + g_e[:, None] * (xf @ We_e + be_e), None)
        y0 = jnp.zeros((N, be.shape[-1]), xf.dtype)
        y, _ = jax.lax.scan(body, y0, (We, be, gates.T))
        return y.reshape(Bv, Sv, -1)
    x = x + _L0_attn_ref(_layernorm(x, axis=-1), L0_attn_Wq, L0_attn_Wk, L0_attn_Wv, L0_attn_Wo)
    x = x + _L0_xattn_ref(_layernorm(x, axis=-1), ctx_1024, ctx_1024, L0_xattn_igate_w, L0_xattn_igate_b, L0_xattn_fgate_w, L0_xattn_fgate_b, L0_xattn_ln_scale)
    x = x + _L0_ffn_ref(_layernorm(x, axis=-1), L0_ffn_gate_w, L0_ffn_W1, L0_ffn_W2, L0_ffn_Ws1, L0_ffn_Ws2)
    x = x + _L1_attn_ref(_layernorm(x, axis=-1), L1_attn_ln_gamma, L1_attn_ln_beta, L1_attn_Wq, L1_attn_bq, L1_attn_Wk, L1_attn_bk, L1_attn_Wv, L1_attn_bv, L1_attn_Wo, L1_attn_bo)
    x = x + _L1_xattn_ref(_layernorm(x, axis=-1), ctx_1024, ctx_1024, L1_xattn_Wq, L1_xattn_bq, L1_xattn_Wk, L1_xattn_bk, L1_xattn_Wv, L1_xattn_bv, L1_xattn_Wo, L1_xattn_bo)
    x = x + _L1_ffn_ref(_layernorm(x, axis=-1), L1_ffn_wg1, L1_ffn_bg1, L1_ffn_wg2, L1_ffn_bg2, L1_ffn_We, L1_ffn_be)
    return x

_drawn_inputs = setup_inputs


def setup_inputs(seed=0):
    import zlib

    import numpy as np

    out = dict(_drawn_inputs(seed))
    spreads = {'L0_xattn_ln_scale': (1.0, 0.2),
     'L1_attn_ln_gamma': (1.0, 0.6),
     'L1_attn_ln_beta': (0.0, 0.449),
     'L1_attn_bq': (0.0, 0.681),
     'L1_attn_bk': (0.0, 2.0),
     'L1_attn_bv': (0.0, 0.468),
     'L1_attn_bo': (0.0, 0.533),
     'L1_ffn_bg1': (0.0, 1.313),
     'L1_ffn_bg2': (0.0, 0.482),
     'L1_ffn_be': (0.0, 2.0)}
    factors = {'L0_ffn_gate_w': 8.0,
     'L0_ffn_W1': 8.0,
     'L0_ffn_W2': 8.0,
     'L0_ffn_Ws1': 8.0,
     'L0_ffn_Ws2': 8.0,
     'L1_xattn_bq': 16.157,
     'L1_xattn_bk': 64.0,
     'L1_xattn_bv': 3.618,
     'L1_xattn_bo': 3.583}
    for name, (base, spread) in spreads.items():
        noise = np.random.default_rng([zlib.crc32(name.encode()), seed]).standard_normal(out[name].shape)
        drawn = base * np.exp(spread * noise) if base else spread * noise
        out[name] = jnp.asarray(drawn.astype(out[name].dtype))
    for name, factor in factors.items():
        out[name] = (out[name] * factor).astype(out[name].dtype)
    return out
```

```python
import concourse.bass as bass
from concourse import mybir
from contextlib import ExitStack

fp32 = mybir.dt.float32
bf16 = mybir.dt.bfloat16
ALU = mybir.AluOpType
ACT = mybir.ActivationFunctionType
AX = mybir.AxisListType

P = 128
SEQ = 64
BPT = P // SEQ
D = 128
LN_EPS = 1e-5
STREAMS = 4


class Arena:

    def __init__(self, nc, stage):
        self.nc, self.stage, self.ctx, self.held = nc, stage, ExitStack(), []

    def __enter__(self):
        return self

    def __exit__(self, *a):
        self.ctx.__exit__(*a)
        if self.held:
            self.nc.clear_and_free_semaphores(self.held)
            self.nc.all_engine_barrier()

    def sb(self, name, shape, dt=fp32):
        return self.ctx.enter_context(self.nc.sbuf_tensor(f"{self.stage}_{name}", shape, dt))

    def ps(self, name, shape, dt=fp32):
        return self.ctx.enter_context(self.nc.psum_tensor(f"{self.stage}_{name}", shape, dt))

    def sem(self, name):
        self.held.append(self.nc.alloc_semaphore(f"{self.stage}_{name}"))
        return self.held[-1]

    def sems(self, name, n):
        return [self.sem(f"{name}{i}") for i in range(n)]


def wait_apart(eng, sem, value, mark):
    eng.wait_ge(sem, value)
    eng.sem_inc(mark, 1)


def ln_moments(dve, st, work, moments_step, done):
    even, odd = st[:, :, 1], st[:, :, 4]
    mean, var, diff = work[:, 0, :], work[:, 1, :], work[:, 2, :]
    dve.tensor_tensor(mean, even, odd, ALU.add).then_inc(moments_step, 1)
    dve.tensor_tensor(diff, even, odd, ALU.subtract).then_inc(moments_step, 1)
    dve.tensor_tensor(var, st[:, :, 2], st[:, :, 5], ALU.add).then_inc(moments_step, 1)
    dve.wait_ge(moments_step, done + 3)
    dve.tensor_scalar(mean, mean, 0.5, None, ALU.mult).then_inc(moments_step, 1)
    dve.scalar_tensor_tensor(out=diff, in0=diff, scalar=D / 4.0, in1=diff, op0=ALU.mult,
                             op1=ALU.mult).then_inc(moments_step, 1)
    dve.wait_ge(moments_step, done + 5)
    dve.tensor_tensor(var, var, diff, ALU.add).then_inc(moments_step, 1)


def linear_attention(nc, g, w, x_dram):
    N = g.tiles // STREAMS
    HD = 8
    NH = D // HD
    KVW = D + NH
    with Arena(nc, "la") as a:
        wqkv = a.sb("wqkv", [D, 3 * D])
        wo = a.sb("wo", [D, D])
        rope_c = a.sb("rope_c", [P, 2 * D])
        rope_s = a.sb("rope_s", [P, 2 * D])
        kv_mask = a.sb("kv_mask", [D, KVW])
        U = range(STREAMS)
        st0 = a.sb("st0", [P, STREAMS, 6])
        mom = a.sb("mom", [P, 3, STREAMS])
        lnv = a.sb("lnv", [P, 2, STREAMS])
        xn = a.sb("xn", [P, STREAMS, D])
        xnT = a.sb("xnT", [D, STREAMS, P])
        ra = a.sb("ra", [P, STREAMS, 2 * D])
        rb = a.sb("rb", [P, STREAMS, 2 * D])
        qk = a.sb("qk", [P, STREAMS, 2 * D])
        vo = a.sb("vo", [P, STREAMS, BPT, KVW])
        qT = a.sb("qT", [D, STREAMS, P])
        kvm = a.sb("kvm", [D, STREAMS, BPT, KVW])
        den = a.sb("den", [P, STREAMS, NH])
        at = a.sb("at", [P, STREAMS, D])
        atT = a.sb("atT", [D, STREAMS, P])
        bank_a = [a.ps(f"bank_a{u}", [P, 512]) for u in U]
        bank_b = [a.ps(f"bank_b{u}", [P, 512]) for u in U]
        qkv_ps = [b[:, 0:3 * D] for b in bank_a]
        tr_ps = [b[:, 3 * D:4 * D] for b in bank_a]
        kv_ps = [b[:, 0:BPT * KVW].rearrange("p (b n) -> p b n", b=BPT) for b in bank_b]
        y_ps = [b[:, 0:D] for b in bank_b]
        o_ps = [b[:, 2 * KVW:3 * KVW] for b in bank_b]

        consts = a.sem("consts")
        x_in = a.sems("x_in", STREAMS)
        bn_done = a.sem("bn_done")
        moments_step = a.sem("moments_step")
        ln_done = a.sem("ln_done")
        rstd_done = a.sem("rstd_done")
        ones_set = a.sem("ones_set")
        xn_done = a.sems("xn_done", STREAMS)
        xnT_ps = a.sems("xnT_ps", STREAMS)
        xnT_done = a.sems("xnT_done", STREAMS)
        qkv_done = a.sems("qkv_done", STREAMS)
        rope_ab = a.sems("rope_ab", STREAMS)
        rope_sum = a.sems("rope_sum", STREAMS)
        v_done = a.sems("v_done", STREAMS)
        qk_done = a.sems("qk_done", STREAMS)
        kv_sum = a.sems("kv_sum", STREAMS)
        kvm_done = a.sems("kvm_done", STREAMS)
        qT_ps = a.sems("qT_ps", STREAMS)
        qT_done = a.sems("qT_done", STREAMS)
        o_done = a.sems("o_done", STREAMS)
        den_done = a.sems("den_done", STREAMS)
        at_done = a.sems("at_done", STREAMS)
        atT_ps = a.sems("atT_ps", STREAMS)
        atT_done = a.sems("atT_done", STREAMS)
        y_done = a.sems("y_done", STREAMS)
        x_new = a.sems("x_new", STREAMS)
        bn2_done = a.sem("bn2_done")
        blk = a.ctx.enter_context(nc.Block())

        @blk.sync
        def _(sp):
            with sp.Fori(0, N) as i:
                for u in U:
                    sp.wait_ge(x_in[u], i * 16)
                    n = i * STREAMS + u
                    sp.dma_start(g.x[:, n, :], x_dram[:, n, :]).then_inc(x_in[u], 16)
            for u in U:
                sp.wait_ge(x_in[u], 16 * N)

        @blk.scalar
        def _(act):
            loads = [(wqkv[:, :], w["la_wqkv"]), (wo[:, :], w["la_wo"]), (g.ident[:, :], w["ident"]),
                     (rope_c[:, :], w["rope_c"]), (rope_s[:, :], w["rope_s"]), (kv_mask[:, :], w["kv_mask"])]
            for dst, src in loads:
                act.dma_start(dst, src).then_inc(consts, 16)
            act.wait_ge(consts, 16 * len(loads))
            act.wait_ge(ones_set, 2 + BPT)
            act.preload_act_table_set("natural_log_exp_and_others")
            with act.Fori(0, N) as i:
                act.wait_ge(moments_step, i * 6 + 6)
                act.activation(lnv[:, 0, :], mom[:, 1, :], ACT.Ln, bias=g.ln_eps[:, :], scale=1.0 / D).then_inc(ln_done, 1)
                act.wait_ge(ln_done, i + 1)
                act.activation(lnv[:, 1, :], lnv[:, 0, :], ACT.Exp, scale=-0.5).then_inc(rstd_done, 1)
                for u in U:
                    act.wait_ge(xnT_ps[u], i + 1)
                    act.activation(xnT[:, u, :], tr_ps[u], ACT.Copy).then_inc(xnT_done[u], 1)
                for u in U:
                    act.wait_ge(rope_ab[u], 2 * i + 2)
                    for b in range(BPT):
                        r = slice(SEQ * b, SEQ * b + SEQ)
                        act.activation(vo[r, u, b, 0:D], qkv_ps[u][r, 2 * D:3 * D], ACT.Copy).then_inc(v_done[u], 1)
                    act.wait_ge(rope_sum[u], i + 1)
                    act.activation(qk[:, u, :], ra[:, u, :], ACT.Relu).then_inc(qk_done[u], 1)
                for u in U:
                    act.wait_ge(qT_ps[u], i + 1)
                    act.activation(qT[:, u, :], tr_ps[u], ACT.Copy).then_inc(qT_done[u], 1)
                for u in U:
                    act.wait_ge(atT_ps[u], i + 1)
                    act.activation(atT[:, u, :], tr_ps[u], ACT.Copy).then_inc(atT_done[u], 1)

        @blk.tensor
        def _(pe):
            pe.wait_ge(ones_set, 2 + BPT)
            pe.wait_ge(consts, 16 * 6)
            with pe.Fori(0, N) as i:
                for u in U:
                    pe.wait_ge(xn_done[u], i + 1)
                    pe.transpose(tr_ps[u], xn[:, u, :], g.ident[:, :]).then_inc(xnT_ps[u], 1)
                for u in U:
                    pe.wait_ge(xnT_done[u], i + 1)
                    pe.matmul(qkv_ps[u], xnT[:, u, :], wqkv[:, :], start=True, stop=True).then_inc(qkv_done[u], 1)
                for u in U:
                    pe.wait_ge(qk_done[u], i + 1)
                    pe.transpose(tr_ps[u], qk[:, u, 0:D], g.ident[:, :]).then_inc(qT_ps[u], 1)
                    pe.wait_ge(v_done[u], BPT * (i + 1))
                    pe.matmul(kv_ps[u], qk[:, u, D:2 * D], vo[:, u, :, :], start=True, stop=True).then_inc(kv_sum[u], 1)
                for u in U:
                    pe.wait_ge(qT_done[u], i + 1)
                    pe.wait_ge(kvm_done[u], i + 1)
                    for b in range(BPT):
                        r = slice(SEQ * b, SEQ * b + SEQ)
                        mm = pe.matmul(o_ps[u][r, :], qT[:, u, r], kvm[:, u, b, :], start=True, stop=True)
                    mm.then_inc(o_done[u], 1)
                for u in U:
                    pe.wait_ge(at_done[u], i + 1)
                    pe.transpose(tr_ps[u], at[:, u, :], g.ident[:, :]).then_inc(atT_ps[u], 1)
                for u in U:
                    pe.wait_ge(atT_done[u], i + 1)
                    pe.matmul(y_ps[u], atT[:, u, :], wo[:, :], start=True, stop=True).then_inc(y_done[u], 1)

        @blk.gpsimd
        def _(pool):
            pool.memset(g.ln_eps[:, :], LN_EPS).then_inc(ones_set, 1)
            pool.memset(vo[:, :, :, :], 0.0).then_inc(ones_set, 1)
            pool.wait_ge(ones_set, 2)
            for b in range(BPT):
                pool.memset(vo[SEQ * b:SEQ * b + SEQ, :, b, D:KVW], 1.0).then_inc(ones_set, 1)

        @blk.vector
        def _(dve):
            dve.wait_ge(consts, 16 * 6)
            dve.wait_ge(ones_set, 2 + BPT)
            with dve.Fori(0, N) as i:
                for u in U:
                    dve.wait_ge(x_in[u], i * 16 + 16)
                    dve.wait_ge(consts, 16)
                    dve.bn_stats(st0[:, u, :], g.x[:, i * STREAMS + u, :]).then_inc(bn_done, 1)
                dve.wait_ge(bn_done, i * STREAMS + STREAMS)
                ln_moments(dve, st0, mom, moments_step, i * 6)
                dve.wait_ge(rstd_done, i + 1)
                for u in U:
                    dve.tensor_scalar(xn[:, u, :], g.x[:, i * STREAMS + u, :], mom[:, 0, u:u + 1], lnv[:, 1, u:u + 1],
                                      ALU.subtract, ALU.mult).then_inc(xn_done[u], 1)
                for u in U:
                    dve.wait_ge(qkv_done[u], i + 1)
                    dve.tensor_tensor(ra[:, u, :], qkv_ps[u][:, 0:2 * D], rope_c[:, :], ALU.mult).then_inc(rope_ab[u], 1)
                    dve.tensor_tensor(rb[:, u, :], qkv_ps[u][:, 0:2 * D], rope_s[:, :], ALU.mult).then_inc(rope_ab[u], 1)
                for u in U:
                    dve.wait_ge(rope_ab[u], 2 * i + 2)
                    av = ra[:, u, :].rearrange("p (n two) -> p n two", two=2)
                    bv = rb[:, u, :].rearrange("p (n two) -> p n two", two=2)
                    dve.tensor_tensor(av, av, bv[:, :, ::-1], ALU.add).then_inc(rope_sum[u], 1)
                for u in U:
                    dve.wait_ge(kv_sum[u], i + 1)
                    dve.tensor_tensor(kvm[:, u, :, :], kv_ps[u], kv_mask[:, :].unsqueeze(1).to_broadcast([D, BPT, KVW]),
                                      ALU.mult).then_inc(kvm_done[u], 1)
                for u in U:
                    dve.wait_ge(o_done[u], i + 1)
                    dve.tensor_scalar(den[:, u, :], o_ps[u][:, D:KVW], 1e-6, None, ALU.add).then_inc(den_done[u], 1)
                for u in U:
                    dve.wait_ge(den_done[u], 2 * i + 1)
                    dve.reciprocal(den[:, u, :], den[:, u, :]).then_inc(den_done[u], 1)
                for u in U:
                    dve.wait_ge(den_done[u], 2 * i + 2)
                    dve.tensor_tensor(at[:, u, :].rearrange("p (h e) -> p h e", h=NH),
                                      o_ps[u][:, 0:D].rearrange("p (h e) -> p h e", h=NH),
                                      den[:, u, :].unsqueeze(2).to_broadcast([P, NH, HD]), ALU.mult).then_inc(at_done[u], 1)
                for u in U:
                    n = i * STREAMS + u
                    dve.wait_ge(y_done[u], i + 1)
                    dve.tensor_tensor(g.x[:, n, :], g.x[:, n, :], y_ps[u], ALU.add).then_inc(x_new[u], 1)
                for u in U:
                    dve.wait_ge(x_new[u], i + 1)
                    dve.wait_ge(consts, 16)
                    dve.bn_stats(g.st[:, i * STREAMS + u, :], g.x[:, i * STREAMS + u, :]).then_inc(bn2_done, 1)
            dve.wait_ge(bn2_done, g.tiles)


def mlstm(nc, g, w, ctx_rows):
    TG = STREAMS
    TOK = TG * P
    NB = TG * BPT
    N = g.tiles // TG
    NH, HD = 8, 16
    HP = NH // 2
    VW = HD + 1
    T = range(TG)
    B = range(NB)
    with Arena(nc, "ml") as a:
        wg = a.sb("wg", [D, 3, 40])
        wgc = a.sb("wgc", [D, 40])
        gate_b = a.sb("gate_b", [40, 2])
        lns = a.sb("lns", [P, D])
        m_h2 = a.sb("m_h2", [D, 2])
        m_pair = a.sb("m_pair", [D, HP])
        keep = a.sb("keep", [NH, TOK])
        restart = a.sb("restart", [NH, TOK])
        m_par = a.sb("m_par", [NH, 2])
        m_hp = a.sb("m_hp", [NH, HP])
        causal = a.sb("causal", [P, SEQ], bf16)
        causal32 = a.sb("causal32", [P, SEQ])
        ident16 = a.sb("ident16", [P, P], bf16)
        xvar = a.sb("xvar", [P, 3, g.tiles])
        xr = a.sb("xr", [P, 2, g.tiles])
        q_tok = a.sb("q_tok", [P, TG, D])
        qT = a.sb("qT", [D, TOK])
        qG = a.sb("qG", [D, HP, TOK])
        cx = a.sb("cx", [P, NB, D])
        kE = a.sb("kE", [D, NB, 2, SEQ])
        vB = a.sb("vB", [P, NB, HP, 2, VW])
        f_abs = a.sb("f_abs", [NH, TOK])
        f_min = a.sb("f_min", [NH, TOK])
        cs = a.sb("cs", [NH, TOK])
        gg = a.sb("gg", [NH, TOK])
        cm = a.sb("cm", [NH, TOK])
        floor = a.sb("floor", [NH, TOK])
        argL = a.sb("argL", [40, NB, 2, SEQ])
        argR = a.sb("argR", [40, NB, HP, SEQ])
        dE = a.sb("dE", [P, 3, HP, SEQ])
        cT = a.sb("cT", [P, 3, HP, SEQ])
        fl = a.sb("fl", [P, TG, NH])
        den = a.sb("den", [P, TG, NH])
        h = a.sb("h", [P, TG, D])
        st = a.sb("st", [P, TG, 6])
        mom = a.sb("mom", [P, 3, TG])
        hr = a.sb("hr", [P, 2, TG])
        hn = a.sb("hn", [P, TG, D])
        banks = [a.ps(f"bank{n}", [P, 512]) for n in range(8)]
        qT_ps, kT_ps, gate_ps = banks[0], banks[1], banks[2]
        out_ps = [banks[n][:, 0:NH * VW] for n in range(4)]
        fl_ps = banks[7][:, 0:TG * NH].rearrange("p (t h) -> p t h", t=TG)
        s_ps = [banks[4 + n][:, 0:HP * SEQ].rearrange("p (h s) -> p h s", h=HP) for n in range(3)]
        e_ps = [banks[4 + n][:, HP * SEQ:2 * HP * SEQ].rearrange("p (h s) -> p h s", h=HP) for n in range(3)]

        consts = a.sem("consts")
        cx_in = a.sem("cx_in")
        setup = a.sem("setup")
        casts_done = a.sem("casts_done")
        pool_mark = a.sem("pool_mark")
        sp_mark = a.sem("sp_mark")
        moments_step = a.sem("moments_step")
        xr_done = a.sem("xr_done")
        q_done = a.sem("q_done")
        qT_in_ps = a.sem("qT_in_ps")
        kT_in_ps = a.sem("kT_in_ps")
        qT_done = a.sem("qT_done")
        qG_done = a.sem("qG_done")
        kE_done = a.sem("kE_done")
        vB_done = a.sem("vB_done")
        gates_ready = a.sem("gates_ready")
        f_step = a.sem("f_step")
        gate_step = a.sem("gate_step")
        arg_done = a.sem("arg_done")
        scores_ready = a.sem("scores_ready")
        exps_done = a.sem("exps_done")
        c_done = a.sem("c_done")
        fl_ready = a.sem("fl_ready")
        out_ready = a.sem("out_ready")
        fl_done = a.sem("fl_done")
        den_step = a.sem("den_step")
        h_done = a.sem("h_done")
        bn_done = a.sem("bn_done")
        hmom_step = a.sem("hmom_step")
        hr_done = a.sem("hr_done")
        hn_done = a.sem("hn_done")
        hs_done = a.sem("hs_done")
        x_new = a.sem("x_new")
        st_done = a.sem("st_done")
        blk = a.ctx.enter_context(nc.Block())
        loads = [(wg[:, :, :], w["ml_wg"]), (gate_b[:, :], w["ml_gate_b"]), (lns[:, :], w["ml_scale"]),
                 (m_h2[:, :], w["ml_m_h2"]), (m_pair[:, :], w["ml_m_pair"]), (keep[:, :], w["ml_keep"]),
                 (restart[:, :], w["ml_restart"]), (m_par[:, :], w["ml_m_par"]), (m_hp[:, :], w["ml_m_hp"]),
                 (causal32[:, :], w["ml_causal"]), (argL[32:40, :, :, :], w["ml_argL"]),
                 (argR[0:8, :, :, :], w["ml_argR"])]
        LOADED = 16 * len(loads)

        @blk.sync
        def _(sp):
            sp.wait_ge(setup, 3)
            for dst, src in loads:
                sp.dma_start(dst, src).then_inc(consts, 16)
            with sp.Fori(0, N) as i:
                wait_apart(sp, cx_in, i * 32, sp_mark)
                wait_apart(sp, kT_in_ps, i, sp_mark)
                wait_apart(sp, vB_done, i * 2, sp_mark)
                for h2 in range(2):
                    sp.dma_start(cx[SEQ * h2:SEQ * h2 + SEQ, :, :],
                                 ctx_rows[:, bass.ds(i * NB, NB), :]).then_inc(cx_in, 16)
            sp.wait_ge(cx_in, 32 * N)

        @blk.gpsimd
        def _(pool):
            pool.memset(vB[:, :, :, :, :], 0.0).then_inc(setup, 1)
            pool.memset(argL[:, :, :, :], 0.0).then_inc(setup, 1)
            pool.memset(argR[:, :, :, :], 0.0).then_inc(setup, 1)
            pool.wait_ge(setup, 3)
            for h2 in range(2):
                pool.memset(vB[SEQ * h2:SEQ * h2 + SEQ, :, :, h2, HD:VW], 1.0).then_inc(setup, 1)
            pool.wait_ge(setup, 5)
            pool.wait_ge(consts, LOADED)
            with pool.Fori(0, N) as i:
                wait_apart(pool, cx_in, i * 32 + 32, pool_mark)
                wait_apart(pool, out_ready, i * TG, pool_mark)
                for h2 in range(2):
                    if h2:
                        wait_apart(pool, vB_done, i * 2 + h2, pool_mark)
                    r = slice(SEQ * h2, SEQ * h2 + SEQ)
                    pool.tensor_copy(vB[r, :, :, h2, 0:HD],
                                     cx[r, :, :].rearrange("p b (hp two e) -> p b hp two e", two=2, e=HD)[:, :, :, h2, :]
                                     ).then_inc(vB_done, 1)
                for t in T:
                    pool.wait_ge(hn_done, i * TG + t + 1)
                    pool.tensor_tensor(hn[:, t, :], hn[:, t, :], lns[:, :], ALU.mult).then_inc(hs_done, 1)

        @blk.scalar
        def _(act):
            act.preload_act_table_set("natural_log_exp_and_others")
            act.wait_ge(moments_step, 6)
            act.activation(xr[:, 0, :], xvar[:, 1, :], ACT.Ln, bias=g.ln_eps[:, :], scale=1.0 / D).then_inc(xr_done, 1)
            act.wait_ge(xr_done, 1)
            act.activation(xr[:, 1, :], xr[:, 0, :], ACT.Exp, scale=-0.5).then_inc(xr_done, 1)
            act.wait_ge(consts, LOADED)
            with act.Fori(0, N) as i:
                act.wait_ge(qT_in_ps, i + 1)
                act.activation(qT[:, :], qT_ps[:, :], ACT.Copy).then_inc(qT_done, 1)
                act.wait_ge(kT_in_ps, i + 1)
                kv = kT_ps[:, :].rearrange("p (b t) -> p b t", b=NB)
                for h2 in range(2):
                    act.activation(kE[:, :, h2, :], kv, ACT.Copy, scale=m_h2[:, h2:h2 + 1]).then_inc(kE_done, 1)
                act.wait_ge(gates_ready, i + 1)
                act.activation(f_abs[:, :], gate_ps[32:40, :], ACT.Abs, bias=gate_b[32:40, 1:2]).then_inc(f_step, 1)
                act.wait_ge(f_step, i * 3 + 1)
                act.activation(f_abs[:, :], f_abs[:, :], ACT.Exp, scale=-1.0).then_inc(f_step, 1)
                act.wait_ge(f_step, i * 3 + 2)
                act.activation(f_abs[:, :], f_abs[:, :], ACT.Ln, bias=1.0).then_inc(f_step, 1)
                for b in B:
                    act.wait_ge(scores_ready, i * NB + b + 1)
                    act.activation(dE[:, b % 3, :, :], e_ps[b % 3], ACT.Exp).then_inc(exps_done, 1)
                    if b == 0:
                        act.wait_ge(fl_ready, i * TG + TG)
                        act.activation(fl[:, :, :], fl_ps, ACT.Exp, scale=-1.0).then_inc(fl_done, 1)
                act.wait_ge(hmom_step, i * 6 + 6)
                act.activation(hr[:, 0, :], mom[:, 1, :], ACT.Ln, bias=g.ln_eps[:, :], scale=1.0 / D).then_inc(hr_done, 1)
                act.wait_ge(hr_done, i * 2 + 1)
                act.activation(hr[:, 1, :], hr[:, 0, :], ACT.Exp, scale=-0.5).then_inc(hr_done, 1)

        @blk.tensor
        def _(pe):
            pe.wait_ge(setup, 5)
            pe.wait_ge(casts_done, 3)
            pe.wait_ge(consts, LOADED)
            with pe.Fori(0, N) as i:
                pe.wait_ge(cx_in, i * 32 + 32)
                for t in T:
                    pe.wait_ge(q_done, i * TG + t + 1)
                    mm = pe.transpose(qT_ps[:, P * t:P * t + P], q_tok[:, t, :], g.ident[:, :])
                mm.then_inc(qT_in_ps, 1)
                for b in B:
                    mm = pe.transpose(kT_ps[:, SEQ * b:SEQ * b + SEQ], cx[0:SEQ, b, :], g.ident[0:SEQ, 0:SEQ])
                mm.then_inc(kT_in_ps, 1)
                pe.wait_ge(qT_done, i + 1)
                pe.matmul(gate_ps[0:40, :], wg[:, 0, :], qT[:, :], start=True, stop=False)
                pe.wait_ge(kE_done, 2 * i + 2)
                for h2 in range(2):
                    mm = pe.matmul(gate_ps[0:40, :], wgc[:, :], kE[:, :, h2, :], start=False, stop=(h2 == 1))
                mm.then_inc(gates_ready, 1)
                pe.wait_ge(qG_done, HP * i + HP)

                def scores(b):
                    if b >= 3:
                        pe.wait_ge(c_done, i * NB + b - 2)
                    pe.matmul(s_ps[b % 3], kE[:, b, :, :], qG[:, :, SEQ * b:SEQ * b + SEQ], start=True, stop=True)
                    if b == 0:
                        pe.wait_ge(arg_done, 6 * i + 6)
                    pe.matmul(e_ps[b % 3], argL[:, b, :, :], argR[:, b, :, :], start=True, stop=False)
                    pe.matmul(e_ps[b % 3], ident16[:, :], causal[:, :].unsqueeze(1).to_broadcast([P, HP, SEQ]),
                              start=False, stop=True).then_inc(scores_ready, 1)

                def values(b):
                    t, r = b // 2, slice(SEQ * (b % 2), SEQ * (b % 2) + SEQ)
                    if b == 0:
                        pe.wait_ge(vB_done, 2 * i + 2)
                    pe.wait_ge(c_done, i * NB + b + 1)
                    for hp in range(HP):
                        mm = pe.matmul(out_ps[t][r, 2 * VW * hp:2 * VW * hp + 2 * VW], cT[:, b % 3, hp, :],
                                       vB[:, b, hp, :, :], start=True, stop=True)
                    if b % 2:
                        mm.then_inc(out_ready, 1)

                scores(0)
                pe.wait_ge(gate_step, i * 6 + 6)
                scores(1)
                for t in T:
                    mm = pe.transpose(fl_ps[:, t, :], floor[:, P * t:P * t + P], g.ident[0:NH, 0:NH])
                    mm.then_inc(fl_ready, 1)
                for b in B:
                    if b + 2 < NB:
                        scores(b + 2)
                    values(b)

        @blk.vector
        def _(dve):
            ln_moments(dve, g.st, xvar, moments_step, 0)
            dve.wait_ge(consts, LOADED)
            dve.tensor_copy(causal[:, :], causal32[:, :]).then_inc(casts_done, 1)
            dve.tensor_copy(ident16[:, :], g.ident[:, :]).then_inc(casts_done, 1)
            dve.tensor_tensor(wgc[:, :], wg[:, 1, :], wg[:, 2, :], ALU.add).then_inc(casts_done, 1)
            dve.wait_ge(xr_done, 2)
            with dve.Fori(0, N) as i:
                for t in T:
                    n = i * TG + t
                    dve.tensor_scalar(q_tok[:, t, :], g.x[:, n, :], xvar[:, 0, bass.ds(n, 1)], xr[:, 1, bass.ds(n, 1)],
                                      ALU.subtract, ALU.mult).then_inc(q_done, 1)
                dve.wait_ge(qT_done, i + 1)
                for hp in range(HP):
                    dve.tensor_scalar(qG[:, hp, :], qT[:, :], m_pair[:, hp:hp + 1], 1.0 / HD ** 0.5,
                                      ALU.mult, ALU.mult).then_inc(qG_done, 1)
                dve.wait_ge(f_step, i * 3 + 1)
                dve.tensor_scalar(f_min[:, :], gate_ps[32:40, :], gate_b[32:40, 1:2], 0.0,
                                  ALU.add, ALU.min).then_inc(gate_step, 1)
                dve.wait_ge(f_step, i * 3 + 3)
                dve.wait_ge(gate_step, i * 6 + 1)
                dve.tensor_tensor(f_min[:, :], f_min[:, :], f_abs[:, :], ALU.subtract).then_inc(gate_step, 1)
                dve.wait_ge(gate_step, i * 6 + 2)
                dve.tensor_tensor_scan(cs[:, :], keep[:, :], f_min[:, :], 0.0, ALU.mult, ALU.add).then_inc(gate_step, 1)
                dve.wait_ge(gate_step, i * 6 + 3)
                dve.scalar_tensor_tensor(out=gg[:, :], in0=gate_ps[0:8, :], scalar=gate_b[0:8, 0:1], in1=cs[:, :],
                                         op0=ALU.add, op1=ALU.subtract).then_inc(gate_step, 1)
                dve.wait_ge(gate_step, i * 6 + 4)
                dve.tensor_tensor_scan(cm[:, :], restart[:, :], gg[:, :], -1e30, ALU.add, ALU.max).then_inc(gate_step, 1)
                for h2 in range(2):
                    dve.tensor_scalar(argL[0:8, :, h2, :], gg[:, :].rearrange("p (b t) -> p b t", b=NB),
                                      m_par[:, h2:h2 + 1], None, ALU.mult).then_inc(arg_done, 1)
                dve.wait_ge(gate_step, i * 6 + 5)
                for hp in range(HP):
                    dve.tensor_scalar(argR[32:40, :, hp, :], cm[:, :].rearrange("p (b t) -> p b t", b=NB),
                                      m_hp[:, hp:hp + 1], -1.0, ALU.mult, ALU.mult).then_inc(arg_done, 1)
                dve.tensor_tensor(floor[:, :], cs[:, :], cm[:, :], ALU.add).then_inc(gate_step, 1)

                def normalise(t):
                    k = (i * TG + t) * 3
                    o = out_ps[t].rearrange("p (h v) -> p h v", v=VW)
                    dve.wait_ge(out_ready, i * TG + t + 1)
                    dve.wait_ge(fl_done, i + 1)
                    dve.scalar_tensor_tensor(out=den[:, t, :], in0=o[:, :, HD], scalar=-1.0, in1=fl[:, t, :],
                                             op0=ALU.mult, op1=ALU.max).then_inc(den_step, 1)
                    dve.wait_ge(den_step, k + 1)
                    dve.tensor_tensor(den[:, t, :], o[:, :, HD], den[:, t, :], ALU.max).then_inc(den_step, 1)
                    dve.wait_ge(den_step, k + 2)
                    dve.tensor_scalar(den[:, t, :], den[:, t, :], 1e-6, None, ALU.add).then_inc(den_step, 1)
                    dve.wait_ge(den_step, k + 3)
                    dve.reciprocal(den[:, t, :], den[:, t, :]).then_inc(h_done, 1)
                    dve.wait_ge(h_done, (i * TG + t) * 2 + 1)
                    dve.tensor_tensor(h[:, t, :].rearrange("p (h e) -> p h e", h=NH), o[:, :, 0:HD],
                                      den[:, t, :].unsqueeze(2).to_broadcast([P, NH, HD]), ALU.mult).then_inc(h_done, 1)
                    dve.wait_ge(h_done, (i * TG + t) * 2 + 2)
                    dve.wait_ge(consts, 16)
                    dve.bn_stats(st[:, t, :], h[:, t, :]).then_inc(bn_done, 1)

                for b in B:
                    dve.wait_ge(exps_done, i * NB + b + 1)
                    dve.tensor_tensor(cT[:, b % 3, :, :], s_ps[b % 3], dE[:, b % 3, :, :], ALU.mult).then_inc(c_done, 1)
                    if b % 2 and b > 1:
                        normalise(b // 2 - 1)
                normalise(TG - 1)
                dve.wait_ge(bn_done, i * TG + TG)
                ln_moments(dve, st, mom, hmom_step, i * 6)
                dve.wait_ge(hr_done, i * 2 + 2)
                for t in T:
                    dve.tensor_scalar(hn[:, t, :], h[:, t, :], mom[:, 0, t:t + 1], hr[:, 1, t:t + 1],
                                      ALU.subtract, ALU.mult).then_inc(hn_done, 1)
                for t in T:
                    n = i * TG + t
                    dve.wait_ge(hs_done, n + 1)
                    dve.tensor_tensor(g.x[:, n, :], g.x[:, n, :], hn[:, t, :], ALU.add).then_inc(x_new, 1)
                for t in T:
                    n = i * TG + t
                    dve.wait_ge(x_new, n + 1)
                    dve.wait_ge(consts, 16)
                    dve.bn_stats(g.st[:, n, :], g.x[:, n, :]).then_inc(st_done, 1)
            dve.wait_ge(st_done, g.tiles)


def normed_transposed(nc, g, w, name, hidden):
    TG, N, TOK = STREAMS, g.tiles // STREAMS, STREAMS * P
    E = 20 if hidden else 8
    F = 32
    T = range(TG)
    with Arena(nc, name) as a:
        wgate = a.sb("wgate", [F if hidden else D, E])
        wg1 = a.sb("wg1", [D, F])
        bg1 = a.sb("bg1", [F, 1])
        bg2 = a.sb("bg2", [P, E])
        first = a.sb("first", [P, g.tiles, E])
        xvar = a.sb("xvar", [P, 3, g.tiles])
        xr = a.sb("xr", [P, 2, g.tiles])
        xn = a.sb("xn", [P, TG, D])
        xT = a.sb("xT", [D, 2, TOK])
        hT = a.sb("hT", [F, 2, TOK])
        lg = a.sb("lg", [P, g.tiles, E])
        top = a.sb("top", [P, 2, g.tiles])
        eq = a.sb("eq", [P, g.tiles, E])
        pre = a.sb("pre", [P, g.tiles, E])
        pick = a.sb("pick", [P, 2, g.tiles, E])
        ex = a.sb("ex", [P, g.tiles, E])
        tr_ps = [a.ps(f"tr{u}", [P, 512]) for u in range(2)]
        h_ps = [a.ps(f"h{u}", [F, 512]) for u in range(2)]
        lg_ps = [a.ps(f"lg{u}", [P, 512])[:, 0:TG * E].rearrange("p (t e) -> p t e", t=TG) for u in range(2)]
        consts = a.sem("consts")
        moments_step = a.sem("moments_step")
        xr_done = a.sem("xr_done")
        xn_done = a.sem("xn_done")
        tr_ready = a.sem("tr_ready")
        xT_done = a.sem("xT_done")
        kept = a.sem("kept")
        h_ready = a.sem("h_ready")
        h_done = a.sem("h_done")
        lg_ready = a.sem("lg_ready")
        lg_done = a.sem("lg_done")
        top_step = a.sem("top_step")
        ex_done = a.sem("ex_done")
        pool_mark = a.sem("pool_mark")
        blk = a.ctx.enter_context(nc.Block())
        loads = [(wgate[:, :], w[name + "_gate"]), (first[:, :, :], w[name + "_first"][:, 0:g.tiles, :])]
        if hidden:
            loads += [(wg1[:, :], w[name + "_wg1"]), (bg1[:, :], w[name + "_bg1"]), (bg2[:, :], w[name + "_bg2"])]
        LOADED = 16 * len(loads)
        last = g.tiles

        @blk.sync
        def _(sp):
            for dst, src in loads:
                sp.dma_start(dst, src).then_inc(consts, 16)

        @blk.scalar
        def _(act):
            act.preload_act_table_set("natural_log_exp_and_others")
            act.wait_ge(moments_step, 6)
            act.activation(xr[:, 0, :], xvar[:, 1, :], ACT.Ln, bias=g.ln_eps[:, :], scale=1.0 / D).then_inc(xr_done, 1)
            act.wait_ge(xr_done, 1)
            act.activation(xr[:, 1, :], xr[:, 0, :], ACT.Exp, scale=-0.5).then_inc(xr_done, 1)
            act.wait_ge(consts, LOADED)
            if hidden:
                act.preload_act_table(ACT.Gelu)
            with act.Fori(0, N // 2) as i2:
                for u in range(2):
                    i = i2 * 2 + u
                    act.wait_ge(tr_ready, i + 1)
                    act.wait_ge(kept, i2 * 2)
                    act.activation(xT[:, u, :], tr_ps[u][:, :], ACT.Copy).then_inc(xT_done, 1)
                    if hidden:
                        act.wait_ge(h_ready, i + 1)
                        act.activation(hT[:, u, :], h_ps[u][:, :], ACT.Gelu, bias=bg1[:, :]).then_inc(h_done, 1)
            act.preload_act_table_set("natural_log_exp_and_others")
            act.wait_ge(ex_done, 1)
            act.activation(ex[:, :, :], ex[:, :, :], ACT.Exp).then_inc(ex_done, 1)

        @blk.gpsimd
        def _(pool):
            with pool.Fori(0, N // 2) as i2:
                for u in range(2):
                    i = i2 * 2 + u
                    wait_apart(pool, xT_done, i + 1, pool_mark)
                    pool.tensor_copy(g.xT[:, bass.ds(i * TOK, TOK)], xT[:, u, :]).then_inc(kept, 1)

        @blk.tensor
        def _(pe):
            pe.wait_ge(consts, LOADED)
            with pe.Fori(0, N // 2) as i2:
                for u in range(2):
                    i = i2 * 2 + u
                    for t in T:
                        pe.wait_ge(xn_done, i * TG + t + 1)
                        mm = pe.transpose(tr_ps[u][:, P * t:P * t + P], xn[:, t, :], g.ident[:, :])
                    mm.then_inc(tr_ready, 1)
                    pe.wait_ge(xT_done, i + 1)
                    src = xT
                    if hidden:
                        pe.matmul(h_ps[u][:, :], wg1[:, :], xT[:, u, :], start=True, stop=True).then_inc(h_ready, 1)
                        pe.wait_ge(h_done, i + 1)
                        src = hT
                    for t in T:
                        mm = pe.matmul(lg_ps[u][:, t, :], src[:, u, P * t:P * t + P], wgate[:, :], start=True, stop=True)
                    mm.then_inc(lg_ready, 1)

        @blk.vector
        def _(dve):
            ln_moments(dve, g.st, xvar, moments_step, 0)
            dve.wait_ge(xr_done, 2)
            dve.wait_ge(consts, LOADED)
            with dve.Fori(0, N // 2) as i2:
                for u in range(2):
                    i = i2 * 2 + u
                    dve.wait_ge(tr_ready, i)
                    for t in T:
                        n = i * TG + t
                        dve.tensor_scalar(xn[:, t, :], g.x[:, n, :], xvar[:, 0, bass.ds(n, 1)], xr[:, 1, bass.ds(n, 1)],
                                          ALU.subtract, ALU.mult).then_inc(xn_done, 1)
                    dve.wait_ge(lg_ready, i + 1)
                    if hidden:
                        dve.tensor_tensor(lg[:, bass.ds(i * TG, TG), :], lg_ps[u],
                                          bg2[:, :].unsqueeze(1).to_broadcast([P, TG, E]), ALU.add).then_inc(lg_done, 1)
                    else:
                        dve.tensor_copy(lg[:, bass.ds(i * TG, TG), :], lg_ps[u]).then_inc(lg_done, 1)
            dve.wait_ge(lg_done, N)

            def over_experts(m):
                return m.unsqueeze(2).to_broadcast([P, last, E])

            flat = lambda m: m.rearrange("p t e -> p (t e)")
            step = 0
            src = lg
            for k in range(2):
                dve.tensor_reduce(top[:, k, :], src[:, :, :], AX.X, ALU.max).then_inc(top_step, 1)
                dve.wait_ge(top_step, step + 1)
                dve.tensor_tensor(eq[:, :, :], src[:, :, :], over_experts(top[:, k, :]), ALU.is_equal).then_inc(top_step, 1)
                dve.wait_ge(top_step, step + 2)
                dve.tensor_tensor_scan(flat(pre[:, :, :]), flat(first[:, :, :]), flat(eq[:, :, :]), 0.0,
                                       ALU.mult, ALU.add).then_inc(top_step, 1)
                dve.wait_ge(top_step, step + 3)
                dve.scalar_tensor_tensor(out=pick[:, k, :, :], in0=pre[:, :, :], scalar=1.0, in1=eq[:, :, :],
                                         op0=ALU.is_equal, op1=ALU.mult).then_inc(top_step, 1)
                dve.wait_ge(top_step, step + 4)
                step += 4
                if k == 0:
                    dve.scalar_tensor_tensor(out=ex[:, :, :], in0=pick[:, 0, :, :], scalar=-3e38, in1=lg[:, :, :],
                                             op0=ALU.mult, op1=ALU.add).then_inc(top_step, 1)
                    dve.wait_ge(top_step, step + 1)
                    step += 1
                    src = ex
            dve.tensor_tensor(pick[:, 0, :, :], pick[:, 0, :, :], pick[:, 1, :, :], ALU.add).then_inc(top_step, 1)
            dve.tensor_tensor(ex[:, :, :], lg[:, :, :], over_experts(top[:, 0, :]), ALU.subtract).then_inc(ex_done, 1)
            dve.wait_ge(ex_done, 2)
            dve.tensor_reduce(top[:, 1, :], ex[:, :, :], AX.X, ALU.add).then_inc(top_step, 1)
            dve.wait_ge(top_step, step + 2)
            dve.reciprocal(top[:, 1, :], top[:, 1, :]).then_inc(top_step, 1)
            dve.tensor_tensor(pick[:, 0, :, :], pick[:, 0, :, :], ex[:, :, :], ALU.mult).then_inc(top_step, 1)
            dve.wait_ge(top_step, step + 4)
            dve.tensor_tensor(g.rw[:, 0:last, 0:E], pick[:, 0, :, :], over_experts(top[:, 1, :]), ALU.mult).then_inc(top_step, 1)
            dve.wait_ge(top_step, step + 5)


def silu_experts(nc, g, w):
    TG, N, TOK = STREAMS, g.tiles // STREAMS, STREAMS * P
    E, UNITS = 8, 8
    T = range(TG)
    with Arena(nc, "se") as a:
        w1 = a.sb("w1", [D, 2, UNITS, P])
        w2 = a.sb("w2", [P, UNITS, D])
        sel32 = a.sb("sel32", [E + 1, UNITS, P])
        sel = a.sb("sel", [E + 1, UNITS, P], bf16)
        rwx = a.sb("rwx", [P, TG, E + 1])
        rw_hi = a.sb("rw_hi", [E + 1, TOK], bf16)
        rw_lo = a.sb("rw_lo", [E + 1, TOK], bf16)
        act_g = a.sb("act_g", [P, 2, TOK])
        hid = a.sb("hid", [P, 2, TOK])
        hw = a.sb("hw", [P, 2, TOK])
        yT = a.sb("yT", [D, TOK])
        y_ps = [a.ps(f"y{u}", [P, 512]) for u in range(2)]
        g_ps = [a.ps(f"g{u}", [P, 512]) for u in range(2)]
        b_ps = [a.ps(f"b{u}", [P, 512]) for u in range(2)]
        out_ps = a.ps("out", [P, 512])
        tr_ps = a.ps("tr", [P, 512])
        consts = a.sem("consts")
        rwx_done = a.sem("rwx_done")
        casts_done = a.sem("casts_done")
        rwT_ready = a.sem("rwT_ready")
        rwT_done = a.sem("rwT_done")
        up_ready = a.sem("up_ready")
        b_ready = a.sem("b_ready")
        silu_done = a.sem("silu_done")
        hid_done = a.sem("hid_done")
        hw_done = a.sem("hw_done")
        down_ready = a.sem("down_ready")
        yT_done = a.sem("yT_done")
        y_ready = a.sem("y_ready")
        x_new = a.sem("x_new")
        st_done = a.sem("st_done")
        blk = a.ctx.enter_context(nc.Block())
        loads = [(w1[:, :, :, :], w["se_w1"]), (w2[:, :, :], w["se_w2"]), (sel32[:, :, :], w["se_sel"])]
        LOADED = 16 * len(loads)

        @blk.sync
        def _(sp):
            for dst, src in loads:
                sp.dma_start(dst, src).then_inc(consts, 16)

        @blk.gpsimd
        def _(pool):
            pool.memset(rwx[:, :, :], 1.0).then_inc(casts_done, 1)

        @blk.scalar
        def _(act):
            act.preload_act_table(ACT.Silu)
            with act.Fori(0, N) as i:
                act.wait_ge(rwT_ready, i + 1)
                act.activation(rw_hi[:, :], tr_ps[0:E + 1, :], ACT.Copy).then_inc(rwT_done, 1)
                for n in range(UNITS):
                    act.wait_ge(up_ready, i * UNITS + n + 1)
                    if n >= 2:
                        act.wait_ge(hid_done, i * UNITS + n - 1)
                    act.activation(act_g[:, n % 2, :], g_ps[n % 2][:, :], ACT.Silu).then_inc(silu_done, 1)
                act.wait_ge(down_ready, i + 1)
                act.activation(yT[:, :], out_ps[:, :], ACT.Copy).then_inc(yT_done, 1)

        @blk.tensor
        def _(pe):
            pe.wait_ge(consts, LOADED)
            pe.wait_ge(casts_done, 2)
            with pe.Fori(0, N) as i:
                pe.wait_ge(rwx_done, i + 1)
                for t in T:
                    mm = pe.transpose(tr_ps[0:E + 1, P * t:P * t + P], rwx[:, t, :], g.ident[:, :])
                mm.then_inc(rwT_ready, 1)

                def up(n):
                    pe.matmul(y_ps[n % 2][:, :], w1[:, 0, n, :], g.xT[:, bass.ds(i * TOK, TOK)], start=True, stop=True)
                    pe.matmul(g_ps[n % 2][:, :], w1[:, 1, n, :], g.xT[:, bass.ds(i * TOK, TOK)],
                              start=True, stop=True).then_inc(up_ready, 1)
                    if n == 0:
                        pe.wait_ge(rwT_done, 2 * i + 2)
                    if n >= 2:
                        pe.wait_ge(hw_done, i * UNITS + n - 1)
                    pe.matmul(b_ps[n % 2][:, :], sel[:, n, :], rw_hi[:, :], start=True, stop=False)
                    pe.matmul(b_ps[n % 2][:, :], sel[:, n, :], rw_lo[:, :], start=False, stop=True).then_inc(b_ready, 1)

                def down(n):
                    pe.wait_ge(hw_done, i * UNITS + n + 1)
                    return pe.matmul(out_ps[:, :], w2[:, n, :], hw[:, n % 2, :], start=(n == 0), stop=(n == UNITS - 1))

                up(0)
                for n in range(UNITS):
                    if n + 1 < UNITS:
                        if n >= 1:
                            pe.wait_ge(hid_done, i * UNITS + n)
                        up(n + 1)
                    mm = down(n)
                mm.then_inc(down_ready, 1)
                pe.wait_ge(yT_done, i + 1)
                for t in T:
                    mm = pe.transpose(tr_ps[:, P * t:P * t + P], yT[:, P * t:P * t + P], g.ident[:, :])
                mm.then_inc(y_ready, 1)

        @blk.vector
        def _(dve):
            dve.wait_ge(consts, LOADED)
            dve.tensor_copy(sel[:, :, :], sel32[:, :, :]).then_inc(casts_done, 1)
            dve.wait_ge(casts_done, 2)
            with dve.Fori(0, N) as i:
                dve.tensor_copy(rwx[:, :, 0:E], g.rw[:, bass.ds(i * TG, TG), 0:E]).then_inc(rwx_done, 1)
                dve.wait_ge(rwT_done, 2 * i + 1)
                dve.tensor_tensor(rw_lo[:, :], tr_ps[0:E + 1, :], rw_hi[:, :], ALU.subtract).then_inc(rwT_done, 1)
                for n in range(UNITS):
                    dve.wait_ge(silu_done, i * UNITS + n + 1)
                    dve.tensor_tensor(hid[:, n % 2, :], y_ps[n % 2][:, :], act_g[:, n % 2, :], ALU.mult).then_inc(hid_done, 1)
                    dve.wait_ge(hid_done, i * UNITS + n + 1)
                    dve.wait_ge(b_ready, i * UNITS + n + 1)
                    dve.tensor_tensor(hw[:, n % 2, :], b_ps[n % 2][:, :], hid[:, n % 2, :], ALU.mult).then_inc(hw_done, 1)
                dve.wait_ge(y_ready, i + 1)
                xs = g.x[:, bass.ds(i * TG, TG), :]
                dve.tensor_tensor(xs, tr_ps[:, :].rearrange("p (t d) -> p t d", t=TG), xs, ALU.add).then_inc(x_new, 1)
                dve.wait_ge(x_new, i + 1)
                for t in T:
                    n = i * TG + t
                    dve.bn_stats(g.st[:, n, :], g.x[:, n, :]).then_inc(st_done, 1)
            dve.wait_ge(st_done, g.tiles)


def linear_experts(nc, g, w, out_dram):
    TG, N, TOK = STREAMS, g.tiles // STREAMS, STREAMS * P
    E, C = 20, 4
    CH = E // C
    T = range(TG)
    with Arena(nc, "le") as a:
        we = a.sb("we", [D, CH, C * D])
        be = a.sb("be", [E, D])
        rws = a.sb("rws", [P, TG, E])
        rwT = a.sb("rwT", [E, TOK])
        xTs = a.sb("xTs", [D, TOK])
        prod = a.sb("prod", [P, 4, C * D])
        acc = a.sb("acc", [P, 2, C * D])
        part = a.sb("part", [P, 2, D])
        e_ps = [a.ps(f"e{k}", [P, 512]) for k in range(5)]
        tr_ps = a.ps("tr", [E, 512])
        b_ps = [a.ps(f"b{k}", [P, 512]) for k in range(2)]
        consts = a.sem("consts")
        xTs_done = a.sem("xTs_done")
        rws_done = a.sem("rws_done")
        rwT_ready = a.sem("rwT_ready")
        rwT_done = a.sem("rwT_done")
        e_ready = a.sem("e_ready")
        b_ready = a.sem("b_ready")
        prod_done = a.sem("prod_done")
        acc_done = a.sem("acc_done")
        fold_done = a.sem("fold_done")
        part_done = a.sem("part_done")
        x_new = a.sem("x_new")
        stored = a.sem("stored")
        pool_mark = a.sem("pool_mark")
        sp_mark = a.sem("sp_mark")
        blk = a.ctx.enter_context(nc.Block())
        loads = [(we[:, :, :], w["le_we"]), (be[:, :], w["le_be"])]
        LOADED = 16 * len(loads)

        @blk.sync
        def _(sp):
            for dst, src in loads:
                sp.dma_start(dst, src).then_inc(consts, 16)
            with sp.Fori(0, N) as i:
                wait_apart(sp, x_new, i * TG + TG, sp_mark)
                sp.dma_start(out_dram[:, bass.ds(i * TG, TG), :], g.x[:, bass.ds(i * TG, TG), :]).then_inc(stored, 16)
            sp.wait_ge(stored, 16 * N)

        @blk.scalar
        def _(act):
            act.preload_act_table_set("natural_log_exp_and_others")
            with act.Fori(0, N) as i:
                act.wait_ge(e_ready, i * TG * CH)
                act.activation(xTs[:, :], g.xT[:, bass.ds(i * TOK, TOK)], ACT.Copy).then_inc(xTs_done, 1)
                act.wait_ge(rwT_ready, i + 1)
                act.activation(rwT[:, :], tr_ps[:, :], ACT.Copy).then_inc(rwT_done, 1)

        @blk.tensor
        def _(pe):
            pe.wait_ge(consts, LOADED)
            with pe.Fori(0, N) as i:
                pe.wait_ge(rws_done, i + 1)
                for t in T:
                    mm = pe.transpose(tr_ps[:, P * t:P * t + P], rws[:, t, :], g.ident[:, :])
                mm.then_inc(rwT_ready, 1)
                pe.wait_ge(xTs_done, i + 1)
                for t in T:
                    for c in range(CH):
                        pe.wait_ge(prod_done, i * TG * CH + t * CH + c - CH + 1 if t else i * TG * CH)
                        pe.matmul(e_ps[c][:, :], xTs[:, P * t:P * t + P], we[:, c, :], start=True, stop=True).then_inc(e_ready, 1)
                    if t == 0:
                        pe.wait_ge(rwT_done, i + 1)
                    if t >= 2:
                        pe.wait_ge(part_done, i * TG + t - 1)
                    pe.matmul(b_ps[t % 2][:, 0:D], rwT[:, P * t:P * t + P], be[:, :], start=True, stop=True).then_inc(b_ready, 1)

        @blk.gpsimd
        def _(pool):
            with pool.Fori(0, N) as i:
                for t in T:
                    m = (i * TG + t) * CH
                    k = (i * TG + t) * (CH + 1)
                    for c in range(1, CH):
                        pool.wait_ge(prod_done, m + c + 1)
                        if c > 1:
                            pool.wait_ge(acc_done, k + c - 1)
                        pool.tensor_tensor(acc[:, t % 2, :], prod[:, (c - 1) % 4, :] if c == 1 else acc[:, t % 2, :],
                                           prod[:, c % 4, :], ALU.add).then_inc(acc_done, 1)
                    pool.wait_ge(acc_done, k + CH - 1)
                    pool.tensor_tensor(acc[:, t % 2, 0:2 * D], acc[:, t % 2, 0:2 * D], acc[:, t % 2, 2 * D:4 * D], ALU.add).then_inc(acc_done, 1)
                    pool.wait_ge(acc_done, k + CH)
                    pool.tensor_tensor(acc[:, t % 2, 0:D], acc[:, t % 2, 0:D], acc[:, t % 2, D:2 * D], ALU.add).then_inc(acc_done, 1)

        @blk.vector
        def _(dve):
            with dve.Fori(0, N) as i:
                dve.tensor_copy(rws[:, :, :], g.rw[:, bass.ds(i * TG, TG), 0:E]).then_inc(rws_done, 1)

                def finish(t):
                    dve.wait_ge(acc_done, (i * TG + t + 1) * (CH + 1))
                    dve.tensor_tensor(part[:, t % 2, :], b_ps[t % 2][:, 0:D], acc[:, t % 2, 0:D], ALU.add).then_inc(part_done, 1)
                    dve.wait_ge(part_done, i * TG + t + 1)
                    n = i * TG + t
                    dve.tensor_tensor(g.x[:, n, :], g.x[:, n, :], part[:, t % 2, :], ALU.add).then_inc(x_new, 1)

                for t in T:
                    m = (i * TG + t) * CH
                    for c in range(CH):
                        dve.wait_ge(e_ready, m + c + 1)
                        if c == 4:
                            dve.wait_ge(acc_done, (i * TG + t) * (CH + 1) + 1)
                        elif t:
                            dve.wait_ge(acc_done, (i * TG + t) * (CH + 1) - 2)
                        dve.tensor_tensor(prod[:, c % 4, :].rearrange("p (e d) -> p e d", e=C),
                                          e_ps[c][:, :].rearrange("p (e d) -> p e d", e=C),
                                          g.rw[:, i * TG + t, C * c:C * c + C].unsqueeze(2).to_broadcast([P, C, D]),
                                          ALU.mult).then_inc(prod_done, 1)
                    if t:
                        dve.wait_ge(b_ready, i * TG + t)
                        finish(t - 1)
                dve.wait_ge(b_ready, i * TG + TG)
                finish(TG - 1)


def softmax_attention(nc, g, w, name, ctx_dram):
    causal = ctx_dram is None
    TG, N, TOK = STREAMS, g.tiles // STREAMS, STREAMS * P
    NB = TG * BPT
    G, M, HD = 4, 4, 8
    SCALE = 1.0 / HD ** 0.5
    T, B = range(TG), range(NB)
    with Arena(nc, name) as a:
        NQ = 4 if causal else 2
        wqk = a.sb("wqk", [D, NQ, D])
        wv = a.sb("wv", [D, D])
        wo = a.sb("wo", [D, D])
        cols = a.sb("cols", [D, 16])
        m_group, m_member = cols[:, 8:12], cols[:, 12:16]
        bo = a.sb("bo", [P, D])
        rope = a.sb("rope", [D, 2, SEQ])
        cm32 = a.sb("cm32", [P, 2, SEQ])
        cm = a.sb("cm", [P, 2, SEQ], bf16)
        v_mask = a.sb("v_mask", [P, 2, D])
        ident16 = a.sb("ident16", [P, P], bf16)
        bvb = a.sb("bvb", [D, P])
        ybias = a.sb("ybias", [P, D])
        xvar = a.sb("xvar", [P, 3, g.tiles])
        xr = a.sb("xr", [P, 5, g.tiles])
        z = a.sb("z", [P, TG, D])
        an = a.sb("an", [P, TG, D])
        aT = a.sb("aT", [D, NB, 2 if causal else 1, SEQ])
        kv_in = a.sb("kv_in", [P, TG, D])
        cT = a.sb("cT", [D, NB, 2, SEQ]) if not causal else aT
        ra = a.sb("ra", [D, 2, TOK])
        rb = a.sb("rb", [D, 2, TOK])
        qg = a.sb("qg", [D, NB, G, SEQ])
        km = a.sb("km", [D, NB, M, SEQ])
        vB = a.sb("vB", [P, NB, 2, D])
        nm = a.sb("nm", [P, 2, 2 * M])
        nmT = a.sb("nmT", [40, 2, P], bf16)
        nm_sel32 = a.sb("nm_sel32", [40, 2, 2, P])
        nm_sel = a.sb("nm_sel", [40, 2, 2, P], bf16)
        pT = a.sb("pT", [P, 2, 2, G, SEQ])
        rden = a.sb("rden", [D, TOK])
        atT = a.sb("atT", [D, TOK])
        zb = a.sb("zb", [P, TG, D])
        banks = [a.ps(f"bank{n}", [P, 512]) for n in range(8)]
        s_ps = banks[0:2]
        st_ps = banks[2:4]
        num_ps, den_ps = banks[4], banks[5]
        v_ps = banks[6:8]
        y_ps = banks[6]
        nmT_ps = [banks[7][0:2 * M, 0:P], banks[6][0:2 * M, 0:P]]
        aT_ps, cT_ps = banks[0], banks[1]
        qk_ps = banks[2:6]

        consts = a.sem("consts")
        casts_done = a.sem("casts_done")
        moments_step = a.sem("moments_step")
        ln_step = a.sem("ln_step")
        rr_done = a.sem("rr_done")
        bias_ready = a.sem("bias_ready")
        ybias_done = a.sem("ybias_done")
        kv_loaded = a.sem("kv_loaded")
        an_done = a.sem("an_done")
        z_done = a.sem("z_done")
        aT_ready = a.sem("aT_ready")
        cT_ready = a.sem("cT_ready")
        aT_done = a.sem("aT_done")
        cT_done = a.sem("cT_done")
        qk_ready = a.sem("qk_ready")
        v_ready = a.sem("v_ready")
        ab_done = a.sem("ab_done")
        rope_done = a.sem("rope_done")
        qg_done = a.sem("qg_done")
        km_done = a.sem("km_done")
        vB_done = a.sem("vB_done")
        s_ready = a.sem("s_ready")
        nm_done = a.sem("nm_done")
        nmT_ready = a.sem("nmT_ready")
        nm_hi_done = a.sem("nm_hi_done")
        nm_lo_done = a.sem("nm_lo_done")
        rows_cleared = a.sem("rows_cleared")
        st_ready = a.sem("st_ready")
        p_done = a.sem("p_done")
        pv_done = a.sem("pv_done")
        rden_done = a.sem("rden_done")
        atT_done = a.sem("atT_done")
        zb_step = a.sem("zb_step")
        y_ready = a.sem("y_ready")
        x_new = a.sem("x_new")
        st_done = a.sem("st_done")
        mark = a.sem("mark")
        blk = a.ctx.enter_context(nc.Block())
        loads = [(wqk[:, :, :], w[name + "_wqk"]), (wv[:, :], w[name + "_wv"]), (wo[:, :], w[name + "_wo"]),
                 (cols[:, :], w[name + "_cols"]), (bo[:, :], w[name + "_bo"]), (v_mask[:, :, :], w["at_v_mask"]), (nm_sel32[:, :, :, :], w["at_nm_sel"])]
        if causal:
            loads += [(rope[:, :, :], w["at_rope"]), (cm32[:, :, :], w["at_causal"])]
        LOADED = 16 * len(loads)

        @blk.sync
        def _(sp):
            for dst, src in loads:
                sp.dma_start(dst, src).then_inc(consts, 16)
            if not causal:
                with sp.Fori(0, N) as i:
                    wait_apart(sp, kv_loaded, i * 16, mark)
                    wait_apart(sp, cT_ready, i, mark)
                    sp.dma_start(kv_in[:, :, :], ctx_dram[:, bass.ds(i * TG, TG), :]).then_inc(kv_loaded, 16)
                sp.wait_ge(kv_loaded, 16 * N)

        @blk.gpsimd
        def _(pool):
            pool.memset(nmT[:, :, :], 0.0).then_inc(rows_cleared, 1)
            pool.wait_ge(ybias_done, 1)
            with pool.Fori(0, N) as i:
                for t in T:
                    n = i * TG + t
                    if causal:
                        pool.wait_ge(z_done, n + 1)
                        pool.tensor_tensor(zb[:, t, :], z[:, t, :], ybias[:, :], ALU.add).then_inc(zb_step, 1)
                        pool.wait_ge(zb_step, 2 * n + 1)
                        pool.tensor_tensor(zb[:, t, :], zb[:, t, :], g.x[:, n, :], ALU.add).then_inc(zb_step, 1)
                    else:
                        pool.wait_ge(x_new, i)
                        pool.tensor_tensor(zb[:, t, :], ybias[:, :], g.x[:, n, :], ALU.add).then_inc(zb_step, 2)

        @blk.scalar
        def _(act):
            act.preload_act_table_set("natural_log_exp_and_others")
            act.wait_ge(moments_step, 6)
            act.activation(xr[:, 0, :], xvar[:, 1, :], ACT.Ln, bias=g.ln_eps[:, :], scale=1.0 / D).then_inc(ln_step, 1)
            act.wait_ge(ln_step, 1)
            act.activation(xr[:, 1, :], xr[:, 0, :], ACT.Exp, scale=-0.5).then_inc(ln_step, 1)
            if causal:
                act.wait_ge(rr_done, 2)
                act.activation(xr[:, 2, :], xr[:, 4, :], ACT.Ln, bias=g.ln_eps[:, :], scale=1.0 / D).then_inc(ln_step, 1)
                act.wait_ge(ln_step, 3)
                act.activation(xr[:, 2, :], xr[:, 2, :], ACT.Exp, scale=-0.5).then_inc(ln_step, 1)
            act.wait_ge(consts, LOADED)
            with act.Fori(0, N) as i:
                act.wait_ge(aT_ready, i + 1)
                rows = lambda ps: ps[:, :].rearrange("p (b s) -> p b s", b=NB)
                twice = lambda ps: rows(ps).unsqueeze(2).to_broadcast([D, NB, 2, SEQ])
                if causal:
                    act.activation(aT[:, :, :, :], twice(aT_ps), ACT.Identity, bias=cols[:, 6:7],
                                   scale=cols[:, 5:6]).then_inc(aT_done, 1)
                else:
                    act.activation(aT[:, :, 0, :], rows(aT_ps), ACT.Copy).then_inc(aT_done, 1)
                    act.wait_ge(cT_ready, i + 1)
                    act.activation(cT[:, :, :, :], twice(cT_ps), ACT.Copy).then_inc(cT_done, 1)
                    act.wait_ge(qk_ready, i * 2 + 1)
                    act.activation(ra[:, 0, :], qk_ps[0][:, :], ACT.Identity, bias=cols[:, 0:1]).then_inc(rope_done, 1)
                    act.wait_ge(qk_ready, i * 2 + 2)
                    act.activation(ra[:, 1, :], qk_ps[1][:, :], ACT.Identity, bias=cols[:, 1:2]).then_inc(rope_done, 1)
                act.wait_ge(rope_done, i * 2 + 2)
                for m in range(M):
                    act.activation(km[:, :, m, :], ra[:, 1, :].rearrange("p (b s) -> p b s", b=NB), ACT.Copy,
                                   scale=m_member[:, m:m + 1]).then_inc(km_done, 1)

                def max_hi(b):
                    act.wait_ge(nmT_ready, i * NB + b + 1)
                    act.activation(nmT[0:2 * M, b % 2, :], nmT_ps[b % 2], ACT.Copy).then_inc(nm_hi_done, 1)

                max_hi(0)
                for b in B:
                    n = i * NB + b
                    if b + 1 < NB:
                        max_hi(b + 1)
                    act.wait_ge(st_ready, n + 1)
                    if b >= 2:
                        act.wait_ge(pv_done, n - 1)
                    act.activation(pT[:, b % 2, :, :, :], st_ps[b % 2][:, :].rearrange("p (h g s) -> p h g s", h=2, g=G),
                                   ACT.Exp, scale=SCALE).then_inc(p_done, 1)

        @blk.tensor
        def _(pe):
            pe.wait_ge(consts, LOADED)
            pe.wait_ge(casts_done, 4 if causal else 3)
            pe.wait_ge(rows_cleared, 1)
            pe.matmul(y_ps[:, 0:D], bvb[:, :], wo[:, :], start=True, stop=True).then_inc(bias_ready, 1)
            pe.wait_ge(ybias_done, 1)
            with pe.Fori(0, N) as i:
                for t in T:
                    pe.wait_ge(an_done, i * TG + t + 1)
                    mm = pe.transpose(aT_ps[:, P * t:P * t + P], an[:, t, :], g.ident[:, :])
                mm.then_inc(aT_ready, 1)
                if not causal:
                    pe.wait_ge(kv_loaded, i * 16 + 16)
                    for t in T:
                        mm = pe.transpose(cT_ps[:, P * t:P * t + P], kv_in[:, t, :], g.ident[:, :])
                    mm.then_inc(cT_ready, 1)
                pe.wait_ge(aT_done, i + 1)
                for k in range(NQ):
                    if k == 1 and not causal:
                        pe.wait_ge(cT_done, i + 1)
                    pe.matmul(qk_ps[k][:, :], wqk[:, k, :], (cT if k % 2 else aT)[:, :, 0, :], start=True, stop=True).then_inc(qk_ready, 1)
                for b in B:
                    mm = pe.matmul(v_ps[b // 4][:, D * (b % 4):D * (b % 4) + D],
                                   cT[:, b, :, :], wv[:, :],
                                   start=True, stop=True)
                    if b % 4 == 3:
                        mm.then_inc(v_ready, 1)

                def mask(bank, k):
                    if causal:
                        pe.matmul(bank[:, :], ident16[:, :], cm[:, k, :].unsqueeze(1).to_broadcast([P, 8, SEQ]),
                                  start=True, stop=False, skip_group_check=True)

                def scores(b):
                    s = slice(SEQ * b, SEQ * b + SEQ)
                    if b >= 2:
                        pe.wait_ge(nm_done, i * NB + b - 1)
                    mask(s_ps[b % 2], 0)
                    for half in range(2):
                        mm = pe.matmul(s_ps[b % 2][:, 256 * half:256 * half + 256], qg[:, b, 2 * half:2 * half + 2, :],
                                       km[:, b, :, :], start=not causal, stop=True, skip_group_check=True)
                    mm.then_inc(s_ready, 1)

                def max_rows(b):
                    pe.wait_ge(nm_done, i * NB + b + 1)
                    if b >= 2:
                        pe.wait_ge(nm_lo_done, i * NB + b - 1)
                    pe.transpose(nmT_ps[b % 2], nm[:, b % 2, :], g.ident[:, :]).then_inc(nmT_ready, 1)

                def scores_t(b):
                    n, s, bank = i * NB + b, slice(SEQ * b, SEQ * b + SEQ), st_ps[b % 2]
                    if b >= 2:
                        pe.wait_ge(p_done, n - 1)
                    mask(bank, 1)
                    for half in range(2):
                        pe.matmul(bank[:, 256 * half:256 * half + 256], km[:, b, 2 * half:2 * half + 2, :], qg[:, b, :, :],
                                  start=not causal, stop=False, skip_group_check=True)
                        if half == 0:
                            pe.wait_ge(nm_hi_done, n + 1)
                            pe.wait_ge(nm_lo_done, n + 1)
                        for k in range(2):
                            mm = pe.matmul(bank[:, 256 * half + P * k:256 * half + P * k + P], nm_sel[:, half, k, :],
                                           nmT[:, b % 2, :], start=False, stop=(k == 1), skip_group_check=True)
                    mm.then_inc(st_ready, 1)

                def values(b):
                    n, s = i * NB + b, slice(SEQ * b, SEQ * b + SEQ)
                    pe.wait_ge(p_done, n + 1)
                    for gr in range(G):
                        r = slice(32 * gr, 32 * gr + 32)
                        for out, den in ((num_ps, False), (den_ps, True)):
                            for half in range(2):
                                lhs = v_mask[:, half, 0:32] if den else vB[:, b, half, r]
                                mm = pe.matmul(out[r, s], lhs, pT[:, b % 2, half, gr, :], start=(half == 0),
                                               stop=(half == 1), tile_position=(0, 32 * gr), skip_group_check=True)
                    mm.then_inc(pv_done, 1)

                pe.wait_ge(qg_done, i * G + G)
                pe.wait_ge(km_done, i * M + M)
                scores(0)
                scores(1)
                pe.wait_ge(vB_done, i * 2 + 2)
                max_rows(0)
                for b in B:
                    if b + 1 < NB:
                        max_rows(b + 1)
                    scores_t(b)
                    if b + 2 < NB:
                        scores(b + 2)
                    if b >= 1:
                        values(b - 1)
                values(NB - 1)
                pe.wait_ge(atT_done, i + 1)
                for t in T:
                    mm = pe.matmul(y_ps[:, D * t:D * t + D], atT[:, P * t:P * t + P], wo[:, :], start=True, stop=True)
                mm.then_inc(y_ready, 1)

        @blk.vector
        def _(dve):
            ln_moments(dve, g.st, xvar, moments_step, 0)
            dve.wait_ge(consts, LOADED)
            dve.tensor_copy(ident16[:, :], g.ident[:, :]).then_inc(casts_done, 1)
            dve.tensor_copy(bvb[:, :], cols[:, 4:5].to_broadcast([D, P])).then_inc(casts_done, 1)
            dve.tensor_copy(nm_sel[:, :, :, :], nm_sel32[:, :, :, :]).then_inc(casts_done, 1)
            if causal:
                dve.tensor_copy(cm[:, :, :], cm32[:, :, :]).then_inc(casts_done, 1)
            dve.wait_ge(bias_ready, 1)
            dve.tensor_tensor(ybias[:, :], y_ps[:, 0:D], bo[:, :], ALU.add).then_inc(ybias_done, 1)
            dve.wait_ge(ln_step, 2)
            if causal:
                dve.tensor_tensor(xr[:, 4, :], xvar[:, 1, :], xr[:, 1, :], ALU.mult).then_inc(rr_done, 1)
                dve.wait_ge(rr_done, 1)
                dve.tensor_tensor(xr[:, 4, :], xr[:, 4, :], xr[:, 1, :], ALU.mult).then_inc(rr_done, 1)
                dve.wait_ge(ln_step, 4)
                dve.tensor_tensor(xr[:, 3, :], xr[:, 1, :], xr[:, 2, :], ALU.mult).then_inc(rr_done, 1)
                dve.wait_ge(rr_done, 3)
            with dve.Fori(0, N) as i:
                for t in T:
                    n = i * TG + t
                    if causal:
                        dve.tensor_scalar(z[:, t, :], g.x[:, n, :], xvar[:, 0, bass.ds(n, 1)], xr[:, 1, bass.ds(n, 1)],
                                          ALU.subtract, ALU.mult).then_inc(z_done, 1)
                    dve.tensor_scalar(an[:, t, :], g.x[:, n, :], xvar[:, 0, bass.ds(n, 1)],
                                      xr[:, 3 if causal else 1, bass.ds(n, 1)], ALU.subtract, ALU.mult).then_inc(an_done, 1)
                if causal:
                    for k in range(NQ):
                        dst = (rb if k >= 2 else ra)[:, k % 2, :].rearrange("p (b s) -> p b s", b=NB)
                        dve.wait_ge(qk_ready, i * NQ + k + 1)
                        dve.scalar_tensor_tensor(out=dst, in0=qk_ps[k][:, :].rearrange("p (b s) -> p b s", b=NB),
                                                 scalar=cols[:, k:k + 1],
                                                 in1=rope[:, k // 2, :].unsqueeze(1).to_broadcast([D, NB, SEQ]),
                                                 op0=ALU.add, op1=ALU.mult).then_inc(ab_done, 1)
                    for k in (1, 0):
                        dve.wait_ge(ab_done, i * NQ + 3 + k)
                        dve.tensor_tensor(ra[:, k, :], ra[:, k, :], rb[:, k, :], ALU.add).then_inc(rope_done, 1)
                dve.wait_ge(rope_done, i * 2 + 2)
                for k in range(G):
                    dve.tensor_scalar(qg[:, :, k, :], ra[:, 0, :].rearrange("p (b s) -> p b s", b=NB), m_group[:, k:k + 1], None, ALU.mult).then_inc(qg_done, 1)
                for c in range(2):
                    dve.wait_ge(v_ready, i * 2 + c + 1)
                    dve.tensor_tensor(vB[:, 4 * c:4 * c + 4, :, :],
                                      v_ps[c][:, :].rearrange("p (b d) -> p b d", b=4).unsqueeze(2).to_broadcast([P, 4, 2, D]),
                                      v_mask[:, :, :].unsqueeze(1).to_broadcast([P, 4, 2, D]), ALU.mult).then_inc(vB_done, 1)

                def max_lo(b):
                    dve.wait_ge(nm_hi_done, i * NB + b + 1)
                    dve.tensor_tensor(nmT[32:32 + 2 * M, b % 2, :], nmT_ps[b % 2], nmT[0:2 * M, b % 2, :],
                                      ALU.subtract).then_inc(nm_lo_done, 1)

                for b in B:
                    dve.wait_ge(s_ready, i * NB + b + 1)
                    dve.tensor_reduce(nm[:, b % 2, :], s_ps[b % 2][:, :].rearrange("p (h t) -> p h t", t=SEQ), AX.X,
                                      ALU.max, negate=True).then_inc(nm_done, 1)
                    if b:
                        max_lo(b - 1)
                max_lo(NB - 1)
                dve.wait_ge(pv_done, i * NB + NB)
                dve.reciprocal(rden[:, :], den_ps[:, :]).then_inc(rden_done, 1)
                dve.wait_ge(rden_done, i + 1)
                dve.tensor_tensor(atT[:, :], num_ps[:, :], rden[:, :], ALU.mult).then_inc(atT_done, 1)
                dve.wait_ge(y_ready, i + 1)
                dve.wait_ge(zb_step, (i + 1) * TG * 2)
                dve.tensor_tensor(g.x[:, bass.ds(i * TG, TG), :], y_ps[:, :].rearrange("p (t d) -> p t d", t=TG),
                                  zb[:, :, :], ALU.add).then_inc(x_new, 1)
                dve.wait_ge(x_new, i + 1)
                for t in T:
                    n = i * TG + t
                    dve.bn_stats(g.st[:, n, :], g.x[:, n, :]).then_inc(st_done, 1)
            dve.wait_ge(st_done, g.tiles)


class Shared:
    pass


def decoder_kernel(nc, w, x_dram, ctx_dram, out_dram, tiles=64, stages=6):
    g = Shared()
    g.tiles = tiles
    with Arena(nc, "all") as a:
        g.x = a.sb("x", [P, tiles, D])
        g.st = a.sb("st", [P, tiles, 6])
        g.xT = a.sb("xT", [D, tiles * P])
        g.rw = a.sb("rw", [P, tiles, 20])
        g.ident = a.sb("ident", [P, P])
        g.ln_eps = a.sb("ln_eps", [P, 1])
        xv = x_dram.rearrange("b s d -> (b s) d").rearrange("(t p) d -> p t d", p=P)
        cv = ctx_dram.rearrange("b s d -> (b s) d").rearrange("(t p) d -> p t d", p=P)
        ctx_rows = ctx_dram.rearrange("b s d -> s b d")
        ov = out_dram.rearrange("b s d -> (b s) d").rearrange("(t p) d -> p t d", p=P)
        linear_attention(nc, g, w, xv)
        if stages >= 2:
            mlstm(nc, g, w, ctx_rows)
        if stages >= 3:
            normed_transposed(nc, g, w, "r0", hidden=False)
            silu_experts(nc, g, w)
        if stages >= 4:
            softmax_attention(nc, g, w, "sa", None)
        if stages >= 5:
            softmax_attention(nc, g, w, "xa", cv)
        if stages >= 6:
            normed_transposed(nc, g, w, "r1", hidden=True)
            linear_experts(nc, g, w, ov)
        if stages < 6:
            with Arena(nc, "end") as e:
                stored = e.sem("stored")
                blk = e.ctx.enter_context(nc.Block())

                @blk.sync
                def _(sp):
                    sp.dma_start(ov, g.x[:, :, :]).then_inc(stored, 16)
                    sp.wait_ge(stored, 16)


def shape_constants():
    import numpy as np
    hd = 8
    pos = np.arange(64, dtype=np.float32)[:, None]
    freq = (1.0 / 10000.0 ** (np.arange(0, hd, 2, dtype=np.float32) / hd)).astype(np.float32)
    ang = pos * freq[None]
    cos, sin = np.cos(ang).astype(np.float32), np.sin(ang).astype(np.float32)
    c = {}
    c["ident"] = np.eye(128, dtype=np.float32)
    c["rope_c"] = np.tile(np.repeat(cos, 2, axis=1), (2, 32))
    s = np.stack([sin, -sin], axis=-1).reshape(64, 8)
    c["rope_s"] = np.tile(s, (2, 32))
    head = np.arange(128) // 8
    same = (head[:, None] == head[None, :]).astype(np.float32)
    c["kv_mask"] = np.concatenate([same, (head[:, None] == np.arange(16)[None]).astype(np.float32)], axis=1)
    p, h8 = np.arange(128), np.arange(8)
    c["ml_m_h2"] = (p[:, None] // 16 % 2 == np.arange(2)[None])
    c["ml_m_pair"] = (p[:, None] // 32 == np.arange(4)[None])
    first = np.arange(512) % 64 == 0
    c["ml_keep"] = np.tile(1.0 - first, (8, 1))
    c["ml_restart"] = np.tile(-1e30 * first, (8, 1))
    c["ml_m_par"] = (h8[:, None] % 2 == np.arange(2)[None])
    c["ml_m_hp"] = (h8[:, None] // 2 == np.arange(4)[None])
    t, s = np.arange(64)[:, None], np.arange(64)[None]
    c["ml_causal"] = np.tile(np.where(t <= s, 0.0, -1e30), (2, 1))
    c["ml_argL"] = np.broadcast_to((h8[:, None] % 2 == np.arange(2)[None])[:, None, :, None], (8, 8, 2, 64))
    c["ml_argR"] = np.broadcast_to((h8[:, None] // 2 == np.arange(4)[None])[:, None, :, None], (8, 8, 4, 64))
    for name, experts in (("r0_first", 8), ("r1_first", 20)):
        c[name] = np.broadcast_to(np.arange(experts) > 0, (128, 64, experts))
    unit = np.arange(1024)
    owner = np.where(unit < 768, unit // 96, 8)
    c["se_sel"] = (owner[None, :] == np.arange(9)[:, None]).reshape(9, 8, 128)
    c["at_rope"] = np.stack([np.tile(np.repeat(cos.T, 2, axis=0), (16, 1)),
                             np.tile(np.stack([-sin.T, sin.T], axis=1).reshape(8, 64), (16, 1))], axis=1)
    hidden = np.where(s <= t, 0.0, -1e30)
    c["at_causal"] = np.stack([np.tile(hidden, (2, 1)), np.tile(hidden.T, (2, 1))], axis=1)
    half = np.arange(128)[:, None, None] // 64
    sel = np.zeros((40, 2, 2, 128))
    for hf in range(2):
        for k in range(2):
            for m in range(2):
                sel[[k * 4 + 2 * hf + m, 32 + k * 4 + 2 * hf + m], hf, k, 64 * m:64 * m + 64] = 1.0
    c["at_nm_sel"] = sel
    c["at_v_mask"] = (p[None, None, :] // 8 % 4) == 2 * np.arange(2)[None, :, None] + half
    return {k: np.ascontiguousarray(v, dtype=np.float32) for k, v in c.items()}


def laid_out(inputs):
    import numpy as np
    i = inputs
    c = {}
    c["la_wqkv"] = np.concatenate([i["L0_attn_Wq"], i["L0_attn_Wk"], i["L0_attn_Wv"]], axis=1)
    c["la_wo"] = i["L0_attn_Wo"]
    f32 = np.float32
    wg = np.zeros((128, 3, 40), f32)
    wg[:, :, 0:8] = i["L0_xattn_igate_w"].reshape(8, 3, 128).transpose(2, 1, 0)
    wg[:, :, 32:40] = i["L0_xattn_fgate_w"].reshape(8, 3, 128).transpose(2, 1, 0)
    c["ml_wg"] = wg
    gb = np.zeros((40, 2), f32)
    gb[0:8, 0] = i["L0_xattn_igate_b"]
    gb[32:40, 1] = i["L0_xattn_fgate_b"]
    c["ml_gate_b"] = gb
    c["ml_scale"] = np.tile(i["L0_xattn_ln_scale"], (128, 1))
    w1, ws1 = i["L0_ffn_W1"], i["L0_ffn_Ws1"]
    up = np.zeros((2, 1024, 128), f32)
    for k in range(2):
        up[k, 0:768] = w1[:, 96 * k:96 * k + 96].reshape(768, 128)
        up[k, 768:960] = ws1[192 * k:192 * k + 192]
    c["se_w1"] = up.transpose(2, 0, 1).reshape(128, 2, 8, 128)
    down = np.zeros((1024, 128), f32)
    down[0:768] = i["L0_ffn_W2"].transpose(0, 2, 1).reshape(768, 128)
    down[768:960] = i["L0_ffn_Ws2"].T
    c["se_w2"] = down.reshape(8, 128, 128).transpose(1, 0, 2)
    partner = np.arange(128) ^ 1
    feature = np.arange(128)[:, None]
    masks = [feature // 32 == np.arange(4)[None], feature // 8 % 4 == np.arange(4)[None]]
    for name, src, extra in (("sa", "L1_attn", True), ("xa", "L1_xattn", False)):
        wq, wk = i[src + "_Wq"], i[src + "_Wk"]
        bq, bk = i[src + "_bq"], i[src + "_bk"]
        qk = [wq, wk] + ([wq[:, partner], wk[:, partner]] if extra else [])
        c[name + "_wqk"] = np.stack(qk, axis=1)
        c[name + "_wv"], c[name + "_wo"] = i[src + "_Wv"], i[src + "_Wo"]
        c[name + "_bo"] = np.tile(i[src + "_bo"], (128, 1))
        col = [bq, bk, bq[partner], bk[partner], i[src + "_bv"]]
        col += [i["L1_attn_ln_gamma"], i["L1_attn_ln_beta"], np.zeros(128, f32)]
        c[name + "_cols"] = np.concatenate([np.stack(col, axis=1)] + [m.astype(f32) for m in masks], axis=1)
    c["le_we"] = i["L1_ffn_We"].transpose(1, 0, 2).reshape(128, 5, 512)
    c["le_be"] = i["L1_ffn_be"]
    c["r0_gate"] = i["L0_ffn_gate_w"].T
    c["r1_gate"] = i["L1_ffn_wg2"][:, 0:20]
    c["r1_wg1"] = i["L1_ffn_wg1"]
    c["r1_bg1"] = i["L1_ffn_bg1"].reshape(32, 1)
    c["r1_bg2"] = np.tile(i["L1_ffn_bg2"][0:20], (128, 1))
    return {k: np.ascontiguousarray(v) for k, v in c.items()}


def kernel(**inputs):
    import numpy as _np
    import concourse.bacc as _bacc
    from concourse import mybir as _mybir
    from concourse.bass_utils import run_bass_kernel_spmd as _run

    inputs = {k: _np.asarray(v) for k, v in inputs.items()}
    nc = _bacc.Bacc("TRN2", target_bir_lowering=False, num_devices=1)
    arrays = {"x": inputs["x"], "ctx": inputs["ctx_1024"], **shape_constants(), **laid_out(inputs)}
    aps = {k: nc.dram_tensor(f"in_{k}", v.shape, _mybir.dt.from_np(v.dtype), kind="ExternalInput").ap()
           for k, v in arrays.items()}
    out = nc.dram_tensor("out", inputs["x"].shape, _mybir.dt.float32, kind="ExternalOutput").ap()
    decoder_kernel(nc, aps, aps["x"], aps["ctx"], out)
    r = _run(nc, [{f"in_{k}": _np.ascontiguousarray(v) for k, v in arrays.items()}], core_ids=[0])
    return r.results[0]["out"]
```

```python
import concourse.bass as bass
from concourse import mybir
from contextlib import ExitStack

fp32 = mybir.dt.float32
bf16 = mybir.dt.bfloat16
ALU = mybir.AluOpType
ACT = mybir.ActivationFunctionType
AX = mybir.AxisListType

P = 128
SEQ = 64
BPT = P // SEQ
D = 128
LN_EPS = 1e-5
STREAMS = 4


class Arena:

    def __init__(self, nc, stage):
        self.nc, self.stage, self.ctx, self.held = nc, stage, ExitStack(), []

    def __enter__(self):
        return self

    def __exit__(self, *a):
        self.ctx.__exit__(*a)
        if self.held:
            self.nc.clear_and_free_semaphores(self.held)
            self.nc.all_engine_barrier()

    def sb(self, name, shape, dt=fp32):
        return self.ctx.enter_context(self.nc.sbuf_tensor(f"{self.stage}_{name}", shape, dt))

    def ps(self, name, shape, dt=fp32):
        return self.ctx.enter_context(self.nc.psum_tensor(f"{self.stage}_{name}", shape, dt))

    def sem(self, name):
        self.held.append(self.nc.alloc_semaphore(f"{self.stage}_{name}"))
        return self.held[-1]

    def sems(self, name, n):
        return [self.sem(f"{name}{i}") for i in range(n)]


def wait_apart(eng, sem, value, mark):
    eng.wait_ge(sem, value)
    eng.sem_inc(mark, 1)


def ln_moments(dve, st, work, moments_step, done):
    even, odd = st[:, :, 1], st[:, :, 4]
    mean, var, diff = work[:, 0, :], work[:, 1, :], work[:, 2, :]
    dve.tensor_tensor(mean, even, odd, ALU.add).then_inc(moments_step, 1)
    dve.tensor_tensor(diff, even, odd, ALU.subtract).then_inc(moments_step, 1)
    dve.tensor_tensor(var, st[:, :, 2], st[:, :, 5], ALU.add).then_inc(moments_step, 1)
    dve.wait_ge(moments_step, done + 3)
    dve.tensor_scalar(mean, mean, 0.5, None, ALU.mult).then_inc(moments_step, 1)
    dve.scalar_tensor_tensor(out=diff, in0=diff, scalar=D / 4.0, in1=diff, op0=ALU.mult,
                             op1=ALU.mult).then_inc(moments_step, 1)
    dve.wait_ge(moments_step, done + 5)
    dve.tensor_tensor(var, var, diff, ALU.add).then_inc(moments_step, 1)


def linear_attention(nc, g, w, x_dram):
    N = g.tiles // STREAMS
    HD = 8
    NH = D // HD
    KVW = D + NH
    with Arena(nc, "la") as a:
        wqkv = a.sb("wqkv", [D, 3 * D])
        wo = a.sb("wo", [D, D])
        rope_c = a.sb("rope_c", [P, 2 * D])
        rope_s = a.sb("rope_s", [P, 2 * D])
        kv_mask = a.sb("kv_mask", [D, KVW])
        U = range(STREAMS)
        st0 = a.sb("st0", [P, STREAMS, 6])
        mom = a.sb("mom", [P, 3, STREAMS])
        lnv = a.sb("lnv", [P, 2, STREAMS])
        xn = a.sb("xn", [P, STREAMS, D])
        xnT = a.sb("xnT", [D, STREAMS, P])
        ra = a.sb("ra", [P, STREAMS, 2 * D])
        rb = a.sb("rb", [P, STREAMS, 2 * D])
        qk = a.sb("qk", [P, STREAMS, 2 * D])
        vo = a.sb("vo", [P, STREAMS, BPT, KVW])
        qT = a.sb("qT", [D, STREAMS, P])
        kvm = a.sb("kvm", [D, STREAMS, BPT, KVW])
        den = a.sb("den", [P, STREAMS, NH])
        at = a.sb("at", [P, STREAMS, D])
        atT = a.sb("atT", [D, STREAMS, P])
        bank_a = [a.ps(f"bank_a{u}", [P, 512]) for u in U]
        bank_b = [a.ps(f"bank_b{u}", [P, 512]) for u in U]
        qkv_ps = [b[:, 0:3 * D] for b in bank_a]
        tr_ps = [b[:, 3 * D:4 * D] for b in bank_a]
        kv_ps = [b[:, 0:BPT * KVW].rearrange("p (b n) -> p b n", b=BPT) for b in bank_b]
        y_ps = [b[:, 0:D] for b in bank_b]
        o_ps = [b[:, 2 * KVW:3 * KVW] for b in bank_b]

        consts = a.sem("consts")
        x_in = a.sems("x_in", STREAMS)
        bn_done = a.sem("bn_done")
        moments_step = a.sem("moments_step")
        ln_done = a.sem("ln_done")
        rstd_done = a.sem("rstd_done")
        ones_set = a.sem("ones_set")
        xn_done = a.sems("xn_done", STREAMS)
        xnT_ps = a.sems("xnT_ps", STREAMS)
        xnT_done = a.sems("xnT_done", STREAMS)
        qkv_done = a.sems("qkv_done", STREAMS)
        rope_ab = a.sems("rope_ab", STREAMS)
        rope_sum = a.sems("rope_sum", STREAMS)
        v_done = a.sems("v_done", STREAMS)
        qk_done = a.sems("qk_done", STREAMS)
        kv_sum = a.sems("kv_sum", STREAMS)
        kvm_done = a.sems("kvm_done", STREAMS)
        qT_ps = a.sems("qT_ps", STREAMS)
        qT_done = a.sems("qT_done", STREAMS)
        o_done = a.sems("o_done", STREAMS)
        den_done = a.sems("den_done", STREAMS)
        at_done = a.sems("at_done", STREAMS)
        atT_ps = a.sems("atT_ps", STREAMS)
        atT_done = a.sems("atT_done", STREAMS)
        y_done = a.sems("y_done", STREAMS)
        x_new = a.sems("x_new", STREAMS)
        bn2_done = a.sem("bn2_done")
        blk = a.ctx.enter_context(nc.Block())

        @blk.sync
        def _(sp):
            with sp.Fori(0, N) as i:
                for u in U:
                    sp.wait_ge(x_in[u], i * 16)
                    n = i * STREAMS + u
                    sp.dma_start(g.x[:, n, :], x_dram[:, n, :]).then_inc(x_in[u], 16)
            for u in U:
                sp.wait_ge(x_in[u], 16 * N)

        @blk.scalar
        def _(act):
            loads = [(wqkv[:, :], w["la_wqkv"]), (wo[:, :], w["la_wo"]), (g.ident[:, :], w["ident"]),
                     (rope_c[:, :], w["rope_c"]), (rope_s[:, :], w["rope_s"]), (kv_mask[:, :], w["kv_mask"])]
            for dst, src in loads:
                act.dma_start(dst, src).then_inc(consts, 16)
            act.wait_ge(consts, 16 * len(loads))
            act.wait_ge(ones_set, 2 + BPT)
            act.preload_act_table_set("natural_log_exp_and_others")
            with act.Fori(0, N) as i:
                act.wait_ge(moments_step, i * 6 + 6)
                act.activation(lnv[:, 0, :], mom[:, 1, :], ACT.Ln, bias=g.ln_eps[:, :], scale=1.0 / D).then_inc(ln_done, 1)
                act.wait_ge(ln_done, i + 1)
                act.activation(lnv[:, 1, :], lnv[:, 0, :], ACT.Exp, scale=-0.5).then_inc(rstd_done, 1)
                for u in U:
                    act.wait_ge(xnT_ps[u], i + 1)
                    act.activation(xnT[:, u, :], tr_ps[u], ACT.Copy).then_inc(xnT_done[u], 1)
                for u in U:
                    act.wait_ge(rope_ab[u], 2 * i + 2)
                    for b in range(BPT):
                        r = slice(SEQ * b, SEQ * b + SEQ)
                        act.activation(vo[r, u, b, 0:D], qkv_ps[u][r, 2 * D:3 * D], ACT.Copy).then_inc(v_done[u], 1)
                    act.wait_ge(rope_sum[u], i + 1)
                    act.activation(qk[:, u, :], ra[:, u, :], ACT.Relu).then_inc(qk_done[u], 1)
                for u in U:
                    act.wait_ge(qT_ps[u], i + 1)
                    act.activation(qT[:, u, :], tr_ps[u], ACT.Copy).then_inc(qT_done[u], 1)
                for u in U:
                    act.wait_ge(atT_ps[u], i + 1)
                    act.activation(atT[:, u, :], tr_ps[u], ACT.Copy).then_inc(atT_done[u], 1)

        @blk.tensor
        def _(pe):
            pe.wait_ge(ones_set, 2 + BPT)
            pe.wait_ge(consts, 16 * 6)
            with pe.Fori(0, N) as i:
                for u in U:
                    pe.wait_ge(xn_done[u], i + 1)
                    pe.transpose(tr_ps[u], xn[:, u, :], g.ident[:, :]).then_inc(xnT_ps[u], 1)
                for u in U:
                    pe.wait_ge(xnT_done[u], i + 1)
                    pe.matmul(qkv_ps[u], xnT[:, u, :], wqkv[:, :], start=True, stop=True).then_inc(qkv_done[u], 1)
                for u in U:
                    pe.wait_ge(qk_done[u], i + 1)
                    pe.transpose(tr_ps[u], qk[:, u, 0:D], g.ident[:, :]).then_inc(qT_ps[u], 1)
                    pe.wait_ge(v_done[u], BPT * (i + 1))
                    pe.matmul(kv_ps[u], qk[:, u, D:2 * D], vo[:, u, :, :], start=True, stop=True).then_inc(kv_sum[u], 1)
                for u in U:
                    pe.wait_ge(qT_done[u], i + 1)
                    pe.wait_ge(kvm_done[u], i + 1)
                    for b in range(BPT):
                        r = slice(SEQ * b, SEQ * b + SEQ)
                        mm = pe.matmul(o_ps[u][r, :], qT[:, u, r], kvm[:, u, b, :], start=True, stop=True)
                    mm.then_inc(o_done[u], 1)
                for u in U:
                    pe.wait_ge(at_done[u], i + 1)
                    pe.transpose(tr_ps[u], at[:, u, :], g.ident[:, :]).then_inc(atT_ps[u], 1)
                for u in U:
                    pe.wait_ge(atT_done[u], i + 1)
                    pe.matmul(y_ps[u], atT[:, u, :], wo[:, :], start=True, stop=True).then_inc(y_done[u], 1)

        @blk.gpsimd
        def _(pool):
            pool.memset(g.ln_eps[:, :], LN_EPS).then_inc(ones_set, 1)
            pool.memset(vo[:, :, :, :], 0.0).then_inc(ones_set, 1)
            pool.wait_ge(ones_set, 2)
            for b in range(BPT):
                pool.memset(vo[SEQ * b:SEQ * b + SEQ, :, b, D:KVW], 1.0).then_inc(ones_set, 1)

        @blk.vector
        def _(dve):
            dve.wait_ge(consts, 16 * 6)
            dve.wait_ge(ones_set, 2 + BPT)
            with dve.Fori(0, N) as i:
                for u in U:
                    dve.wait_ge(x_in[u], i * 16 + 16)
                    dve.wait_ge(consts, 16)
                    dve.bn_stats(st0[:, u, :], g.x[:, i * STREAMS + u, :]).then_inc(bn_done, 1)
                dve.wait_ge(bn_done, i * STREAMS + STREAMS)
                ln_moments(dve, st0, mom, moments_step, i * 6)
                dve.wait_ge(rstd_done, i + 1)
                for u in U:
                    dve.tensor_scalar(xn[:, u, :], g.x[:, i * STREAMS + u, :], mom[:, 0, u:u + 1], lnv[:, 1, u:u + 1],
                                      ALU.subtract, ALU.mult).then_inc(xn_done[u], 1)
                for u in U:
                    dve.wait_ge(qkv_done[u], i + 1)
                    dve.tensor_tensor(ra[:, u, :], qkv_ps[u][:, 0:2 * D], rope_c[:, :], ALU.mult).then_inc(rope_ab[u], 1)
                    dve.tensor_tensor(rb[:, u, :], qkv_ps[u][:, 0:2 * D], rope_s[:, :], ALU.mult).then_inc(rope_ab[u], 1)
                for u in U:
                    dve.wait_ge(rope_ab[u], 2 * i + 2)
                    av = ra[:, u, :].rearrange("p (n two) -> p n two", two=2)
                    bv = rb[:, u, :].rearrange("p (n two) -> p n two", two=2)
                    dve.tensor_tensor(av, av, bv[:, :, ::-1], ALU.add).then_inc(rope_sum[u], 1)
                for u in U:
                    dve.wait_ge(kv_sum[u], i + 1)
                    dve.tensor_tensor(kvm[:, u, :, :], kv_ps[u], kv_mask[:, :].unsqueeze(1).to_broadcast([D, BPT, KVW]),
                                      ALU.mult).then_inc(kvm_done[u], 1)
                for u in U:
                    dve.wait_ge(o_done[u], i + 1)
                    dve.tensor_scalar(den[:, u, :], o_ps[u][:, D:KVW], 1e-6, None, ALU.add).then_inc(den_done[u], 1)
                for u in U:
                    dve.wait_ge(den_done[u], 2 * i + 1)
                    dve.reciprocal(den[:, u, :], den[:, u, :]).then_inc(den_done[u], 1)
                for u in U:
                    dve.wait_ge(den_done[u], 2 * i + 2)
                    dve.tensor_tensor(at[:, u, :].rearrange("p (h e) -> p h e", h=NH),
                                      o_ps[u][:, 0:D].rearrange("p (h e) -> p h e", h=NH),
                                      den[:, u, :].unsqueeze(2).to_broadcast([P, NH, HD]), ALU.mult).then_inc(at_done[u], 1)
                for u in U:
                    n = i * STREAMS + u
                    dve.wait_ge(y_done[u], i + 1)
                    dve.tensor_tensor(g.x[:, n, :], g.x[:, n, :], y_ps[u], ALU.add).then_inc(x_new[u], 1)
                for u in U:
                    dve.wait_ge(x_new[u], i + 1)
                    dve.wait_ge(consts, 16)
                    dve.bn_stats(g.st[:, i * STREAMS + u, :], g.x[:, i * STREAMS + u, :]).then_inc(bn2_done, 1)
            dve.wait_ge(bn2_done, g.tiles)


def pipelined(eng, steps, step):
    step(0, 0, True, True)
    if steps > 2:
        with eng.Fori(0, (steps - 2) // 2) as k:
            for s in range(2):
                step(2 * k + 1 + s, (1 + s) % 2, True, True)
    step(steps - 1, 1, True, False)
    step(steps, 0, False, False)


def pipelined(eng, steps, step):
    step(0, 0, True, True)
    if steps > 2:
        with eng.Fori(0, (steps - 2) // 2) as k:
            for s in range(2):
                step(2 * k + 1 + s, (1 + s) % 2, True, True)
    step(steps - 1, 1, True, False)
    step(steps, 0, False, False)


def pipelined(eng, steps, step):
    step(0, 0, True, True)
    if steps > 2:
        with eng.Fori(0, (steps - 2) // 2) as k:
            for s in range(2):
                step(2 * k + 1 + s, (1 + s) % 2, True, True)
    step(steps - 1, 1, True, False)
    step(steps, 0, False, False)


def pipelined(eng, steps, step):
    step(0, 0, True, True)
    if steps > 2:
        with eng.Fori(0, (steps - 2) // 2) as k:
            for s in range(2):
                step(2 * k + 1 + s, (1 + s) % 2, True, True)
    step(steps - 1, 1, True, False)
    step(steps, 0, False, False)


def pipelined(eng, steps, step):
    step(0, 0, True, True)
    if steps > 2:
        with eng.Fori(0, (steps - 2) // 2) as k:
            for s in range(2):
                step(2 * k + 1 + s, (1 + s) % 2, True, True)
    step(steps - 1, 1, True, False)
    step(steps, 0, False, False)


def pipelined(eng, steps, step):
    step(0, 0, True, True)
    if steps > 2:
        with eng.Fori(0, (steps - 2) // 2) as k:
            for s in range(2):
                step(2 * k + 1 + s, (1 + s) % 2, True, True)
    step(steps - 1, 1, True, False)
    step(steps, 0, False, False)


def mlstm(nc, g, w, ctx_rows):
    TG = STREAMS
    TOK = TG * P
    NB = TG * BPT
    N = g.tiles // TG
    NH, HD = 8, 16
    HP = NH // 2
    VW = HD + 1
    T, B = range(TG), range(NB)
    VALUES = 3
    CB = VALUES + 1
    with Arena(nc, "ml") as a:
        wg = a.sb("wg", [D, 3, 40])
        wgc = a.sb("wgc", [D, 40])
        gate_b = a.sb("gate_b", [40, 2])
        lns = a.sb("lns", [P, D])
        m_h2 = a.sb("m_h2", [D, 2])
        m_pair = a.sb("m_pair", [D, HP])
        keep = a.sb("keep", [NH, TOK])
        restart = a.sb("restart", [NH, TOK])
        m_par = a.sb("m_par", [NH, 2])
        m_hp = a.sb("m_hp", [NH, HP])
        causal = a.sb("causal", [P, SEQ], bf16)
        causal32 = a.sb("causal32", [P, SEQ])
        ident16 = a.sb("ident16", [P, P], bf16)
        xvar = a.sb("xvar", [P, 3, g.tiles])
        xr = a.sb("xr", [P, 2, g.tiles])
        q_tok = a.sb("q_tok", [P, TG, D])
        qT = a.sb("qT", [D, TOK])
        kT = a.sb("kT", [D, TOK])
        cx = a.sb("cx", [P, NB, D])
        qG = a.sb("qG", [D, 2, HP, TOK])
        kE = a.sb("kE", [D, 2, NB, 2, SEQ])
        vB = a.sb("vB", [P, 2, NB, HP, 2, VW])
        argL = a.sb("argL", [40, 2, NB, 2, SEQ])
        argR = a.sb("argR", [40, 2, NB, HP, SEQ])
        fl = a.sb("fl", [P, 2, TG, NH])
        h = a.sb("h", [P, 2, TG, D])
        st = a.sb("st", [P, 2, TG, 6])
        f_abs = a.sb("f_abs", [NH, TOK])
        f_min = a.sb("f_min", [NH, TOK])
        cs = a.sb("cs", [NH, TOK])
        gg = a.sb("gg", [NH, TOK])
        cm = a.sb("cm", [NH, TOK])
        floor = a.sb("floor", [NH, TOK])
        dE = a.sb("dE", [P, CB, HP, SEQ])
        cT = a.sb("cT", [P, CB, HP, SEQ])
        den = a.sb("den", [P, TG, NH])
        mom = a.sb("mom", [P, 3, TG])
        hr = a.sb("hr", [P, 2, TG])
        hn = a.sb("hn", [P, TG, D])
        row_ps = [a.ps(f"row{n}", [P, 512]) for n in range(CB)]
        f_ps = [a.ps(f"f{n}", [P, 512]) for n in range(2)]
        qT_ps, kT_ps = f_ps
        gate_ps = qT_ps
        fl_ps = kT_ps[:, 0:TG * NH].rearrange("p (t h) -> p t h", t=TG)
        out_ps = [a.ps(f"out{n}", [P, 512])[:, 0:NH * VW] for n in range(2)]
        s_ps = [b[:, 0:HP * SEQ].rearrange("p (h s) -> p h s", h=HP) for b in row_ps]
        e_ps = [b[:, HP * SEQ:2 * HP * SEQ].rearrange("p (h s) -> p h s", h=HP) for b in row_ps]

        consts = a.sem("consts")
        cx_in = a.sem("cx_in")
        setup = a.sem("setup")
        casts_done = a.sem("casts_done")
        pool_mark = a.sem("pool_mark")
        sp_mark = a.sem("sp_mark")
        pe_mark = a.sem("pe_mark")
        moments_step = a.sem("moments_step")
        xr_done = a.sem("xr_done")
        q_done = a.sem("q_done")
        qT_in_ps = a.sem("qT_in_ps")
        kT_in_ps = a.sem("kT_in_ps")
        qT_done = a.sem("qT_done")
        qG_done = a.sem("qG_done")
        kT_done = a.sem("kT_done")
        kE_done = a.sem("kE_done")
        vB_done = a.sem("vB_done")
        gates_ready = a.sem("gates_ready")
        f_step = a.sem("f_step")
        gate_step = a.sem("gate_step")
        arg_done = a.sem("arg_done")
        scores_ready = a.sem("scores_ready")
        exps_done = a.sem("exps_done")
        c_done = a.sem("c_done")
        fl_ready = a.sem("fl_ready")
        pv_done = a.sem("pv_done")
        fl_done = a.sem("fl_done")
        den_step = a.sem("den_step")
        h_done = a.sem("h_done")
        bn_done = a.sem("bn_done")
        hmom_step = a.sem("hmom_step")
        hr_done = a.sem("hr_done")
        hn_done = a.sem("hn_done")
        hs_done = a.sem("hs_done")
        x_new = a.sem("x_new")
        st_done = a.sem("st_done")
        blk = a.ctx.enter_context(nc.Block())
        loads = [(wg[:, :, :], w["ml_wg"]), (gate_b[:, :], w["ml_gate_b"]), (lns[:, :], w["ml_scale"]),
                 (m_h2[:, :], w["ml_m_h2"]), (m_pair[:, :], w["ml_m_pair"]), (keep[:, :], w["ml_keep"]),
                 (restart[:, :], w["ml_restart"]), (m_par[:, :], w["ml_m_par"]), (m_hp[:, :], w["ml_m_hp"]),
                 (causal32[:, :], w["ml_causal"])]
        for u in range(2):
            loads += [(argL[32:40, u, :, :, :], w["ml_argL"]), (argR[0:8, u, :, :, :], w["ml_argR"])]
        LOADED = 16 * len(loads)

        by_row = lambda m: m.rearrange("p (b t) -> p b t", b=NB)
        first = lambda j: isinstance(j, int) and j == 0

        def has(i, b, lag, new):
            return new if b >= lag else not first(i)

        @blk.sync
        def _(sp):
            sp.wait_ge(setup, 3)
            for dst, src in loads:
                sp.dma_start(dst, src).then_inc(consts, 16)
            for h2 in range(2):
                sp.dma_start(cx[SEQ * h2:SEQ * h2 + SEQ, :, :], ctx_rows[:, 0:NB, :]).then_inc(cx_in, 16)
            with sp.Fori(0, N - 1) as k:
                wait_apart(sp, cx_in, k * 32 + 32, sp_mark)
                wait_apart(sp, kT_in_ps, k + 1, sp_mark)
                wait_apart(sp, vB_done, k * 2 + 2, sp_mark)
                for h2 in range(2):
                    sp.dma_start(cx[SEQ * h2:SEQ * h2 + SEQ, :, :],
                                 ctx_rows[:, bass.ds(k * NB + NB, NB), :]).then_inc(cx_in, 16)
            sp.wait_ge(cx_in, 32 * N)

        @blk.gpsimd
        def _(pool):
            pool.memset(vB[:, :, :, :, :, :], 0.0).then_inc(setup, 1)
            pool.memset(argL[:, :, :, :, :], 0.0).then_inc(setup, 1)
            pool.memset(argR[:, :, :, :, :], 0.0).then_inc(setup, 1)
            pool.wait_ge(setup, 3)
            for u in range(2):
                for h2 in range(2):
                    pool.memset(vB[SEQ * h2:SEQ * h2 + SEQ, u, :, :, h2, HD:VW], 1.0).then_inc(setup, 1)
            pool.wait_ge(setup, 7)
            pool.wait_ge(consts, LOADED)

            def prepare(j, u, b):
                if b in (0, 1):
                    r = slice(SEQ * b, SEQ * b + SEQ)
                    if b == 0:
                        wait_apart(pool, cx_in, j * 32 + 32, pool_mark)
                    else:
                        wait_apart(pool, vB_done, j * 2 + 1, pool_mark)
                    pool.tensor_copy(vB[r, u, :, :, b, 0:HD],
                                     cx[r, :, :].rearrange("p b (hp two e) -> p b hp two e", two=2, e=HD)[:, :, :, b, :]
                                     ).then_inc(vB_done, 1)
                if 3 <= b < 7:
                    pool.wait_ge(vB_done, j * 2 + 2)
                    pool.wait_ge(qT_done, j + 1)
                    pool.tensor_tensor(qG[:, u, b - 3, :], qT[:, :], m_pair[:, b - 3:b - 2].to_broadcast([D, TOK]),
                                       ALU.mult).then_inc(qG_done, 1)

            def step(i, u, new, ahead):
                for b in B:
                    if ahead:
                        if b == 0 and not first(i):
                            wait_apart(pool, pv_done, i * NB, pool_mark)
                        prepare(i + 1, 1 - u, b)
                    if b == 7 and not first(i):
                        pool.wait_ge(hn_done, i * TG)
                        pool.tensor_tensor(hn[:, :, :], hn[:, :, :], lns[:, :].unsqueeze(1).to_broadcast([P, TG, D]),
                                           ALU.mult).then_inc(hs_done, 1)

            for b in B:
                prepare(0, 0, b)
            pipelined(pool, N, step)

        @blk.scalar
        def _(act):
            act.preload_act_table_set("natural_log_exp_and_others")
            act.wait_ge(moments_step, 6)
            act.activation(xr[:, 0, :], xvar[:, 1, :], ACT.Ln, bias=g.ln_eps[:, :], scale=1.0 / D).then_inc(xr_done, 1)
            act.wait_ge(xr_done, 1)
            act.activation(xr[:, 1, :], xr[:, 0, :], ACT.Exp, scale=-0.5).then_inc(xr_done, 1)
            act.wait_ge(consts, LOADED)

            def prepare(j, u, b):
                if b == 0:
                    if not first(j):
                        act.wait_ge(gates_ready, j)
                    act.wait_ge(kT_in_ps, j + 1)
                    act.activation(kT[:, :], kT_ps[:, :], ACT.Copy).then_inc(kT_done, 1)
                    for h2 in range(2):
                        act.activation(kE[:, u, :, h2, :], by_row(kT_ps[:, :]), ACT.Copy, scale=m_h2[:, h2:h2 + 1]).then_inc(kE_done, 1)
                if b == 2:
                    if not first(j):
                        act.wait_ge(qG_done, j * HP)
                    act.wait_ge(qT_in_ps, j + 1)
                    act.activation(qT[:, :], qT_ps[:, :], ACT.Copy).then_inc(qT_done, 1)
                if b == 3:
                    act.wait_ge(gates_ready, j + 1)
                    act.activation(f_abs[:, :], gate_ps[32:40, :], ACT.Abs, bias=gate_b[32:40, 1:2]).then_inc(f_step, 1)
                    act.wait_ge(f_step, j * 3 + 1)
                    act.activation(f_abs[:, :], f_abs[:, :], ACT.Exp, scale=-1.0).then_inc(f_step, 1)
                    act.wait_ge(f_step, j * 3 + 2)
                    act.activation(f_abs[:, :], f_abs[:, :], ACT.Ln, bias=1.0).then_inc(f_step, 1)
                if b == 5:
                    act.wait_ge(gate_step, j * 6 + 4)
                    for h2 in range(2):
                        act.activation(argL[0:8, u, :, h2, :], by_row(gg[:, :]), ACT.Copy,
                                       scale=m_par[:, h2:h2 + 1]).then_inc(arg_done, 1)
                if b in (5, 6):
                    act.wait_ge(gate_step, j * 6 + 5)
                    for hp in (0, 1) if b == 5 else (2, 3):
                        act.activation(argR[32:40, u, :, hp, :], by_row(cm[:, :]), ACT.Copy,
                                       scale=m_hp[:, hp:hp + 1]).then_inc(arg_done, 1)

            def step(i, u, new, ahead):
                for b in B:
                    r = i * NB + b
                    if new:
                        act.wait_ge(scores_ready, r + 1)
                        act.activation(dE[:, b % CB, :, :], e_ps[b % CB], ACT.Exp).then_inc(exps_done, 1)
                    if b == 4 and not first(i):
                        act.wait_ge(hmom_step, i * 6)
                        act.activation(hr[:, 0, :], mom[:, 1, :], ACT.Ln, bias=g.ln_eps[:, :], scale=1.0 / D).then_inc(hr_done, 1)
                        act.wait_ge(hr_done, i * 2 - 1)
                        act.activation(hr[:, 1, :], hr[:, 0, :], ACT.Exp, scale=-0.5).then_inc(hr_done, 1)
                    if b == 2 and new:
                        act.wait_ge(fl_ready, i * TG + TG)
                        act.activation(fl[:, u, :, :], fl_ps, ACT.Exp, scale=-1.0).then_inc(fl_done, 1)
                    if ahead:
                        prepare(i + 1, 1 - u, b)

            for b in B:
                prepare(0, 0, b)
            pipelined(act, N, step)

        @blk.tensor
        def _(pe):
            pe.wait_ge(setup, 7)
            pe.wait_ge(casts_done, 3)
            pe.wait_ge(consts, LOADED)

            def prepare(j, u, b):
                if b == 0:
                    if not (isinstance(j, int) and j <= 1):
                        wait_apart(pe, fl_done, j - 1, pe_mark)
                    wait_apart(pe, cx_in, j * 32 + 32, pe_mark)
                    for k in B:
                        mm = pe.transpose(kT_ps[:, SEQ * k:SEQ * k + SEQ], cx[0:SEQ, k, :], g.ident[0:SEQ, 0:SEQ])
                    mm.then_inc(kT_in_ps, 1)
                if b == 1:
                    if not first(j):
                        pe.wait_ge(gate_step, j * 6)
                    for t in T:
                        pe.wait_ge(q_done, j * TG + t + 1)
                        mm = pe.transpose(qT_ps[:, P * t:P * t + P], q_tok[:, t, :], g.ident[:, :])
                    mm.then_inc(qT_in_ps, 1)
                if b == 3:
                    pe.wait_ge(qT_done, j + 1)
                    pe.matmul(gate_ps[0:40, :], wg[:, 0, :], qT[:, :], start=True, stop=False)
                    pe.wait_ge(kT_done, j + 1)
                    pe.matmul(gate_ps[0:40, :], wgc[:, :], kT[:, :], start=False, stop=True).then_inc(gates_ready, 1)

            def step(i, u, new, ahead):
                for b in B:
                    r = i * NB + b
                    if new:
                        if b == 0:
                            pe.wait_ge(qG_done, HP * i + HP)
                            pe.wait_ge(kE_done, 2 * i + 2)
                        if has(i, b, CB, new):
                            pe.wait_ge(c_done, r - CB + 1)
                        pe.matmul(s_ps[b % CB], kE[:, u, b, :, :], qG[:, u, :, SEQ * b:SEQ * b + SEQ], start=True, stop=True)
                        if b == 0:
                            pe.wait_ge(arg_done, 6 * i + 6)
                        pe.matmul(e_ps[b % CB], argL[:, u, b, :, :], argR[:, u, b, :, :], start=True, stop=False)
                        pe.matmul(e_ps[b % CB], ident16[:, :], causal[:, :].unsqueeze(1).to_broadcast([P, HP, SEQ]),
                                  start=False, stop=True).then_inc(scores_ready, 1)
                    if has(i, b, VALUES, new):
                        row, v = (b - VALUES) % NB, u if b >= VALUES else 1 - u
                        t, q = row // 2, slice(SEQ * (row % 2), SEQ * (row % 2) + SEQ)
                        pe.wait_ge(c_done, r - VALUES + 1)
                        if row % 2 == 0 and has(i, b, VALUES + 4, new or b < VALUES + 4):
                            pe.wait_ge(h_done, (r - VALUES) - 2)
                        for hp in range(HP):
                            mm = pe.matmul(out_ps[t % 2][q, 2 * VW * hp:2 * VW * hp + 2 * VW], cT[:, (b - VALUES) % CB, hp, :],
                                           vB[:, v, row, hp, :, :], start=True, stop=True)
                        mm.then_inc(pv_done, 1)
                    if b == 2 and new:
                        wait_apart(pe, gate_step, i * 6 + 6, pe_mark)
                        wait_apart(pe, kE_done, 2 * i + (4 if ahead else 2), pe_mark)
                        for t in T:
                            pe.transpose(fl_ps[:, t, :], floor[:, P * t:P * t + P], g.ident[0:NH, 0:NH]).then_inc(fl_ready, 1)
                    if ahead:
                        prepare(i + 1, 1 - u, b)

            for b in B:
                prepare(0, 0, b)
            pipelined(pe, N, step)

        @blk.vector
        def _(dve):
            ln_moments(dve, g.st, xvar, moments_step, 0)
            dve.wait_ge(consts, LOADED)
            dve.tensor_copy(causal[:, :], causal32[:, :]).then_inc(casts_done, 1)
            dve.tensor_copy(ident16[:, :], g.ident[:, :]).then_inc(casts_done, 1)
            dve.tensor_tensor(wgc[:, :], wg[:, 1, :], wg[:, 2, :], ALU.add).then_inc(casts_done, 1)
            dve.wait_ge(xr_done, 2)

            def prepare(j, u, b):
                if b == 0:
                    if not first(j):
                        dve.wait_ge(qT_in_ps, j)
                    for t in T:
                        n = j * TG + t
                        dve.tensor_scalar(q_tok[:, t, :], g.x[:, n, :], xvar[:, 0, bass.ds(n, 1)], xr[:, 1, bass.ds(n, 1)],
                                          ALU.subtract, ALU.mult).then_inc(q_done, 1)
                if b == 4:
                    dve.wait_ge(f_step, j * 3 + 1)
                    dve.tensor_scalar(f_min[:, :], gate_ps[32:40, :], gate_b[32:40, 1:2], 0.0,
                                      ALU.add, ALU.min).then_inc(gate_step, 1)
                    dve.wait_ge(f_step, j * 3 + 3)
                    dve.wait_ge(gate_step, j * 6 + 1)
                    dve.tensor_tensor(f_min[:, :], f_min[:, :], f_abs[:, :], ALU.subtract).then_inc(gate_step, 1)
                    dve.wait_ge(gate_step, j * 6 + 2)
                    dve.tensor_tensor_scan(cs[:, :], keep[:, :], f_min[:, :], 0.0, ALU.mult, ALU.add).then_inc(gate_step, 1)
                    if not first(j):
                        dve.wait_ge(arg_done, j * 6)
                    dve.wait_ge(gate_step, j * 6 + 3)
                    dve.scalar_tensor_tensor(out=gg[:, :], in0=gate_ps[0:8, :], scalar=gate_b[0:8, 0:1], in1=cs[:, :],
                                             op0=ALU.add, op1=ALU.subtract).then_inc(gate_step, 1)
                if b == 5:
                    dve.wait_ge(gate_step, j * 6 + 4)
                    dve.tensor_tensor_scan(cm[:, :], restart[:, :], gg[:, :], -1e30, ALU.add, ALU.max).then_inc(gate_step, 1)
                if b == 6:
                    if not first(j):
                        dve.wait_ge(fl_ready, j * TG)
                    dve.wait_ge(gate_step, j * 6 + 5)
                    dve.tensor_tensor(floor[:, :], cs[:, :], cm[:, :], ALU.add).then_inc(gate_step, 1)

            def normalise(i, u, t):
                n = i * TG + t
                k = n * 3
                o = out_ps[t % 2].rearrange("p (h v) -> p h v", v=VW)
                dve.wait_ge(pv_done, n * 2 + 2)
                dve.wait_ge(fl_done, i + 1)
                dve.scalar_tensor_tensor(out=den[:, t, :], in0=o[:, :, HD], scalar=-1.0, in1=fl[:, u, t, :],
                                         op0=ALU.mult, op1=ALU.max).then_inc(den_step, 1)
                dve.wait_ge(den_step, k + 1)
                dve.tensor_tensor(den[:, t, :], o[:, :, HD], den[:, t, :], ALU.max).then_inc(den_step, 1)
                dve.wait_ge(den_step, k + 2)
                dve.tensor_scalar(den[:, t, :], den[:, t, :], 1e-6, None, ALU.add).then_inc(den_step, 1)
                dve.wait_ge(den_step, k + 3)
                dve.reciprocal(den[:, t, :], den[:, t, :]).then_inc(h_done, 1)
                dve.wait_ge(h_done, n * 2 + 1)
                dve.tensor_tensor(h[:, u, t, :].rearrange("p (h e) -> p h e", h=NH), o[:, :, 0:HD],
                                  den[:, t, :].unsqueeze(2).to_broadcast([P, NH, HD]), ALU.mult).then_inc(h_done, 1)
                dve.wait_ge(h_done, n * 2 + 2)
                dve.wait_ge(consts, 16)
                dve.bn_stats(st[:, u, t, :], h[:, u, t, :]).then_inc(bn_done, 1)

            def step(i, u, new, ahead):
                for b in B:
                    r = i * NB + b
                    if new:
                        dve.wait_ge(exps_done, r + 1)
                        if has(i, b, CB, new):
                            dve.wait_ge(pv_done, r - CB + 1)
                        dve.tensor_tensor(cT[:, b % CB, :, :], s_ps[b % CB], dE[:, b % CB, :, :], ALU.mult).then_inc(c_done, 1)
                    if b % 2 and has(i, b, VALUES + 2, new):
                        t = (b - VALUES - 2) // 2
                        normalise(i if t >= 0 else i - 1, u if t >= 0 else 1 - u, t % TG)
                    if not first(i):
                        if b == 4:
                            dve.wait_ge(bn_done, i * TG)
                            ln_moments(dve, st[:, 1 - u, :, :], mom, hmom_step, (i - 1) * 6)
                        if b == 5:
                            dve.wait_ge(hr_done, i * 2)
                            for t in T:
                                dve.tensor_scalar(hn[:, t, :], h[:, 1 - u, t, :], mom[:, 0, t:t + 1], hr[:, 1, t:t + 1],
                                                  ALU.subtract, ALU.mult).then_inc(hn_done, 1)
                        if b == 7:
                            rows = g.x[:, bass.ds(i * TG - TG, TG), :]
                            dve.wait_ge(hs_done, i)
                            dve.tensor_tensor(rows, rows, hn[:, :, :], ALU.add).then_inc(x_new, 1)
                        if b == 7:
                            dve.wait_ge(x_new, i)
                            for t in T:
                                n = i * TG - TG + t
                                dve.wait_ge(consts, 16)
                                dve.bn_stats(g.st[:, n, :], g.x[:, n, :]).then_inc(st_done, 1)
                    if ahead:
                        prepare(i + 1, 1 - u, b)

            for b in B:
                prepare(0, 0, b)
            pipelined(dve, N, step)
            dve.wait_ge(st_done, g.tiles)


def normed_transposed(nc, g, w, name, hidden):
    TG, N, TOK = STREAMS, g.tiles // STREAMS, STREAMS * P
    E = 20 if hidden else 8
    F = 32
    T = range(TG)
    with Arena(nc, name) as a:
        wgate = a.sb("wgate", [F if hidden else D, E])
        wg1 = a.sb("wg1", [D, F])
        bg1 = a.sb("bg1", [F, 1])
        bg2 = a.sb("bg2", [P, E])
        first = a.sb("first", [P, g.tiles, E])
        xvar = a.sb("xvar", [P, 3, g.tiles])
        xr = a.sb("xr", [P, 2, g.tiles])
        xn = a.sb("xn", [P, 2, TG, D])
        xT = a.sb("xT", [D, 2, TOK])
        hT = a.sb("hT", [F, 2, TOK])
        lg = a.sb("lg", [P, g.tiles, E])
        top = a.sb("top", [P, 2, g.tiles])
        eq = a.sb("eq", [P, g.tiles, E])
        pre = a.sb("pre", [P, g.tiles, E])
        pick = a.sb("pick", [P, 2, g.tiles, E])
        ex = a.sb("ex", [P, g.tiles, E])
        tr_ps = [a.ps(f"tr{u}", [P, 512]) for u in range(2)]
        h_ps = [a.ps(f"h{u}", [F, 512]) for u in range(2)]
        lg_ps = [a.ps(f"lg{u}", [P, 512])[:, 0:TG * E].rearrange("p (t e) -> p t e", t=TG) for u in range(2)]
        consts = a.sem("consts")
        moments_step = a.sem("moments_step")
        xr_done = a.sem("xr_done")
        xn_done = a.sem("xn_done")
        tr_ready = a.sem("tr_ready")
        xT_done = a.sem("xT_done")
        kept = a.sem("kept")
        h_ready = a.sem("h_ready")
        h_done = a.sem("h_done")
        lg_ready = a.sem("lg_ready")
        lg_done = a.sem("lg_done")
        top_step = a.sem("top_step")
        ex_done = a.sem("ex_done")
        pool_mark = a.sem("pool_mark")
        blk = a.ctx.enter_context(nc.Block())
        loads = [(wgate[:, :], w[name + "_gate"]), (first[:, :, :], w[name + "_first"][:, 0:g.tiles, :])]
        if hidden:
            loads += [(wg1[:, :], w[name + "_wg1"]), (bg1[:, :], w[name + "_bg1"]), (bg2[:, :], w[name + "_bg2"])]
        LOADED = 16 * len(loads)
        last = g.tiles
        first_step = lambda i: isinstance(i, int) and i == 0

        @blk.sync
        def _(sp):
            for dst, src in loads:
                sp.dma_start(dst, src).then_inc(consts, 16)

        @blk.scalar
        def _(act):
            act.preload_act_table_set("natural_log_exp_and_others")
            act.wait_ge(moments_step, 6)
            act.activation(xr[:, 0, :], xvar[:, 1, :], ACT.Ln, bias=g.ln_eps[:, :], scale=1.0 / D).then_inc(xr_done, 1)
            act.wait_ge(xr_done, 1)
            act.activation(xr[:, 1, :], xr[:, 0, :], ACT.Exp, scale=-0.5).then_inc(xr_done, 1)
            act.wait_ge(consts, LOADED)
            if hidden:
                act.preload_act_table(ACT.Gelu)

            def step(i, u, new, ahead):
                if hidden and not first_step(i):
                    act.wait_ge(h_ready, i)
                    act.activation(hT[:, 1 - u, :], h_ps[1 - u][:, :], ACT.Gelu, bias=bg1[:, :]).then_inc(h_done, 1)
                if new:
                    act.wait_ge(tr_ready, i + 1)
                    if not first_step(i):
                        act.wait_ge(kept, i)
                    act.activation(xT[:, u, :], tr_ps[u][:, :], ACT.Copy).then_inc(xT_done, 1)

            pipelined(act, N, step)
            act.preload_act_table_set("natural_log_exp_and_others")
            act.wait_ge(ex_done, 1)
            act.activation(ex[:, :, :], ex[:, :, :], ACT.Exp).then_inc(ex_done, 1)

        @blk.gpsimd
        def _(pool):
            pool.sem_inc(kept, 1)

            def step(i, u, new, ahead):
                if new:
                    wait_apart(pool, xT_done, i + 1, pool_mark)
                    pool.tensor_copy(g.xT[:, bass.ds(i * TOK, TOK)], xT[:, u, :]).then_inc(kept, 1)

            pipelined(pool, N, step)

        @blk.tensor
        def _(pe):
            pe.wait_ge(consts, LOADED)

            def step(i, u, new, ahead):
                before = not first_step(i)
                if before:
                    pe.wait_ge(xT_done, i)
                    if hidden:
                        pe.matmul(h_ps[1 - u][:, :], wg1[:, :], xT[:, 1 - u, :], start=True, stop=True).then_inc(h_ready, 1)
                if new:
                    for t in T:
                        pe.wait_ge(xn_done, i * TG + t + 1)
                        mm = pe.transpose(tr_ps[u][:, P * t:P * t + P], xn[:, u, t, :], g.ident[:, :])
                    mm.then_inc(tr_ready, 1)
                if before:
                    if hidden:
                        pe.wait_ge(h_done, i)
                    for t in T:
                        mm = pe.matmul(lg_ps[1 - u][:, t, :], (hT if hidden else xT)[:, 1 - u, P * t:P * t + P],
                                       wgate[:, :], start=True, stop=True)
                    mm.then_inc(lg_ready, 1)

            pipelined(pe, N, step)

        @blk.vector
        def _(dve):
            ln_moments(dve, g.st, xvar, moments_step, 0)
            dve.wait_ge(xr_done, 2)
            dve.wait_ge(consts, LOADED)

            def step(i, u, new, ahead):
                for t in T if new else ():
                    n = i * TG + t
                    dve.tensor_scalar(xn[:, u, t, :], g.x[:, n, :], xvar[:, 0, bass.ds(n, 1)], xr[:, 1, bass.ds(n, 1)],
                                      ALU.subtract, ALU.mult).then_inc(xn_done, 1)
                if not first_step(i):
                    dst = lg[:, bass.ds(i * TG - TG, TG), :]
                    dve.wait_ge(lg_ready, i)
                    if hidden:
                        dve.tensor_tensor(dst, lg_ps[1 - u], bg2[:, :].unsqueeze(1).to_broadcast([P, TG, E]), ALU.add).then_inc(lg_done, 1)
                    else:
                        dve.tensor_copy(dst, lg_ps[1 - u]).then_inc(lg_done, 1)

            pipelined(dve, N, step)
            dve.wait_ge(lg_done, N)

            def over_experts(m):
                return m.unsqueeze(2).to_broadcast([P, last, E])

            flat = lambda m: m.rearrange("p t e -> p (t e)")
            step = 0
            src = lg
            for k in range(2):
                dve.tensor_reduce(top[:, k, :], src[:, :, :], AX.X, ALU.max).then_inc(top_step, 1)
                dve.wait_ge(top_step, step + 1)
                dve.tensor_tensor(eq[:, :, :], src[:, :, :], over_experts(top[:, k, :]), ALU.is_equal).then_inc(top_step, 1)
                dve.wait_ge(top_step, step + 2)
                dve.tensor_tensor_scan(flat(pre[:, :, :]), flat(first[:, :, :]), flat(eq[:, :, :]), 0.0,
                                       ALU.mult, ALU.add).then_inc(top_step, 1)
                dve.wait_ge(top_step, step + 3)
                dve.scalar_tensor_tensor(out=pick[:, k, :, :], in0=pre[:, :, :], scalar=1.0, in1=eq[:, :, :],
                                         op0=ALU.is_equal, op1=ALU.mult).then_inc(top_step, 1)
                dve.wait_ge(top_step, step + 4)
                step += 4
                if k == 0:
                    dve.scalar_tensor_tensor(out=ex[:, :, :], in0=pick[:, 0, :, :], scalar=-3e38, in1=lg[:, :, :],
                                             op0=ALU.mult, op1=ALU.add).then_inc(top_step, 1)
                    dve.wait_ge(top_step, step + 1)
                    step += 1
                    src = ex
            dve.tensor_tensor(pick[:, 0, :, :], pick[:, 0, :, :], pick[:, 1, :, :], ALU.add).then_inc(top_step, 1)
            dve.tensor_tensor(ex[:, :, :], lg[:, :, :], over_experts(top[:, 0, :]), ALU.subtract).then_inc(ex_done, 1)
            dve.wait_ge(ex_done, 2)
            dve.tensor_reduce(top[:, 1, :], ex[:, :, :], AX.X, ALU.add).then_inc(top_step, 1)
            dve.wait_ge(top_step, step + 2)
            dve.reciprocal(top[:, 1, :], top[:, 1, :]).then_inc(top_step, 1)
            dve.tensor_tensor(pick[:, 0, :, :], pick[:, 0, :, :], ex[:, :, :], ALU.mult).then_inc(top_step, 1)
            dve.wait_ge(top_step, step + 4)
            dve.tensor_tensor(g.rw[:, 0:last, 0:E], pick[:, 0, :, :], over_experts(top[:, 1, :]), ALU.mult).then_inc(top_step, 1)
            dve.wait_ge(top_step, step + 5)


def silu_experts(nc, g, w):
    TG, N, TOK = STREAMS, g.tiles // STREAMS, STREAMS * P
    E, UNITS = 8, 8
    T = range(TG)
    with Arena(nc, "se") as a:
        w1 = a.sb("w1", [D, 2, UNITS, P])
        w2 = a.sb("w2", [P, UNITS, D])
        sel32 = a.sb("sel32", [E + 1, UNITS, P])
        sel = a.sb("sel", [E + 1, UNITS, P], bf16)
        rwx = a.sb("rwx", [P, TG, E + 1])
        rw_hi = a.sb("rw_hi", [E + 1, 2, TOK], bf16)
        rw_lo = a.sb("rw_lo", [E + 1, 2, TOK], bf16)
        act_g = a.sb("act_g", [P, 2, TOK])
        hid = a.sb("hid", [P, 2, TOK])
        hw = a.sb("hw", [P, 2, TOK])
        yT = a.sb("yT", [D, TOK])
        y_ps = [a.ps(f"y{u}", [P, 512]) for u in range(2)]
        g_ps = [a.ps(f"g{u}", [P, 512]) for u in range(2)]
        b_ps = [a.ps(f"b{u}", [P, 512]) for u in range(2)]
        out_ps = a.ps("out", [P, 512])
        tr_ps = a.ps("tr", [P, 512])
        consts = a.sem("consts")
        rwx_done = a.sem("rwx_done")
        casts_done = a.sem("casts_done")
        rwT_ready = a.sem("rwT_ready")
        rw_hi_done = a.sem("rw_hi_done")
        rw_lo_done = a.sem("rw_lo_done")
        up_ready = a.sem("up_ready")
        b_ready = a.sem("b_ready")
        silu_done = a.sem("silu_done")
        hid_done = a.sem("hid_done")
        hw_done = a.sem("hw_done")
        down_ready = a.sem("down_ready")
        yT_done = a.sem("yT_done")
        y_ready = a.sem("y_ready")
        x_new = a.sem("x_new")
        st_done = a.sem("st_done")
        blk = a.ctx.enter_context(nc.Block())
        loads = [(w1[:, :, :, :], w["se_w1"]), (w2[:, :, :], w["se_w2"]), (sel32[:, :, :], w["se_sel"])]
        LOADED = 16 * len(loads)
        first = lambda j: isinstance(j, int) and j == 0

        def has(i, s, lag, new):
            return new if s >= lag else not first(i)

        @blk.sync
        def _(sp):
            for dst, src in loads:
                sp.dma_start(dst, src).then_inc(consts, 16)

        @blk.gpsimd
        def _(pool):
            pool.memset(rwx[:, :, :], 1.0).then_inc(casts_done, 1)

        @blk.scalar
        def _(act):
            act.preload_act_table(ACT.Silu)

            def prepare(j, u, s):
                if s == 5:
                    act.wait_ge(rwT_ready, j + 1)
                    act.activation(rw_hi[:, u, :], tr_ps[0:E + 1, :], ACT.Copy).then_inc(rw_hi_done, 1)

            def step(i, u, new, ahead):
                for s in range(UNITS):
                    n = i * UNITS + s
                    if new:
                        act.wait_ge(up_ready, n + 1)
                        if has(i, s, 2, new):
                            act.wait_ge(hid_done, n - 1)
                        act.activation(act_g[:, s % 2, :], g_ps[s % 2][:, :], ACT.Silu).then_inc(silu_done, 1)
                    if s == 0 and not first(i):
                        act.wait_ge(down_ready, i)
                        act.activation(yT[:, :], out_ps[:, :], ACT.Copy).then_inc(yT_done, 1)
                    if ahead:
                        prepare(i + 1, 1 - u, s)

            for s in range(UNITS):
                prepare(0, 0, s)
            pipelined(act, N, step)

        @blk.tensor
        def _(pe):
            pe.wait_ge(consts, LOADED)
            pe.wait_ge(casts_done, 2)

            def prepare(j, u, s):
                if s == 5:
                    pe.wait_ge(rwx_done, j + 1)
                    if not (isinstance(j, int) and j <= 1):
                        pe.wait_ge(x_new, j - 1)
                    for t in T:
                        mm = pe.transpose(tr_ps[0:E + 1, P * t:P * t + P], rwx[:, t, :], g.ident[:, :])
                    mm.then_inc(rwT_ready, 1)

            def step(i, u, new, ahead):
                for s in range(UNITS):
                    n = i * UNITS + s
                    if new:
                        if has(i, s, 2, new):
                            pe.wait_ge(hid_done, n - 1)
                        for k, bank in ((0, y_ps), (1, g_ps)):
                            mm = pe.matmul(bank[s % 2][:, :], w1[:, k, s, :], g.xT[:, bass.ds(i * TOK, TOK)], start=True, stop=True)
                        mm.then_inc(up_ready, 1)
                        if s == 0:
                            pe.wait_ge(rw_hi_done, i + 1)
                            pe.wait_ge(rw_lo_done, i + 1)
                        if has(i, s, 2, new):
                            pe.wait_ge(hw_done, n - 1)
                        pe.matmul(b_ps[s % 2][:, :], sel[:, s, :], rw_hi[:, u, :], start=True, stop=False)
                        pe.matmul(b_ps[s % 2][:, :], sel[:, s, :], rw_lo[:, u, :], start=False, stop=True).then_inc(b_ready, 1)
                    if has(i, s, 1, new):
                        part = (s - 1) % UNITS
                        pe.wait_ge(hw_done, n)
                        if part == 0 and not first(i):
                            pe.wait_ge(yT_done, i)
                        mm = pe.matmul(out_ps[:, :], w2[:, part, :], hw[:, (s - 1) % 2, :], start=(part == 0),
                                       stop=(part == UNITS - 1))
                        if part == UNITS - 1:
                            mm.then_inc(down_ready, 1)
                    if s == 2 and not first(i):
                        pe.wait_ge(yT_done, i)
                        if ahead or new:
                            pe.wait_ge(rw_lo_done, i + 1)
                        for t in T:
                            mm = pe.transpose(tr_ps[:, P * t:P * t + P], yT[:, P * t:P * t + P], g.ident[:, :])
                        mm.then_inc(y_ready, 1)
                    if ahead:
                        prepare(i + 1, 1 - u, s)

            for s in range(UNITS):
                prepare(0, 0, s)
            pipelined(pe, N, step)

        @blk.vector
        def _(dve):
            dve.wait_ge(consts, LOADED)
            dve.tensor_copy(sel[:, :, :], sel32[:, :, :]).then_inc(casts_done, 1)
            dve.wait_ge(casts_done, 2)

            def prepare(j, u, s):
                if s == 4:
                    if not first(j):
                        dve.wait_ge(rwT_ready, j)
                    dve.tensor_copy(rwx[:, :, 0:E], g.rw[:, bass.ds(j * TG, TG), 0:E]).then_inc(rwx_done, 1)
                if s == 6:
                    dve.wait_ge(rw_hi_done, j + 1)
                    dve.tensor_tensor(rw_lo[:, u, :], tr_ps[0:E + 1, :], rw_hi[:, u, :], ALU.subtract).then_inc(rw_lo_done, 1)

            def step(i, u, new, ahead):
                for s in range(UNITS):
                    n = i * UNITS + s
                    if new:
                        dve.wait_ge(silu_done, n + 1)
                        dve.tensor_tensor(hid[:, s % 2, :], y_ps[s % 2][:, :], act_g[:, s % 2, :], ALU.mult).then_inc(hid_done, 1)
                        dve.wait_ge(hid_done, n + 1)
                        dve.wait_ge(b_ready, n + 1)
                        dve.tensor_tensor(hw[:, s % 2, :], b_ps[s % 2][:, :], hid[:, s % 2, :], ALU.mult).then_inc(hw_done, 1)
                    if s == 3 and not first(i):
                        xs = g.x[:, bass.ds(i * TG - TG, TG), :]
                        dve.wait_ge(y_ready, i)
                        dve.tensor_tensor(xs, tr_ps[:, :].rearrange("p (t d) -> p t d", t=TG), xs, ALU.add).then_inc(x_new, 1)
                        dve.wait_ge(x_new, i)
                        for t in T:
                            m = i * TG - TG + t
                            dve.bn_stats(g.st[:, m, :], g.x[:, m, :]).then_inc(st_done, 1)
                    if ahead:
                        prepare(i + 1, 1 - u, s)

            for s in range(UNITS):
                prepare(0, 0, s)
            pipelined(dve, N, step)
            dve.wait_ge(st_done, g.tiles)


def linear_experts(nc, g, w, out_dram):
    TG, N, TOK = STREAMS, g.tiles // STREAMS, STREAMS * P
    E, C = 20, 4
    CH = E // C
    T = range(TG)
    BY_ACT, BY_DVE = (1, 3), (0, 2, 4)
    with Arena(nc, "le") as a:
        we = a.sb("we", [D, CH, C * D])
        be = a.sb("be", [E, D])
        rws = a.sb("rws", [P, 2, TG, E])
        rwT = a.sb("rwT", [E, 2, TOK])
        xTs = a.sb("xTs", [D, 2, TOK])
        prod = a.sb("prod", [P, 2, CH, C * D])
        acc = a.sb("acc", [P, 2, C * D])
        part = a.sb("part", [P, 2, 2 * D])
        e_ps = [a.ps(f"e{k}", [P, 512]) for k in range(CH)]
        tr_ps = a.ps("tr", [E, 512])
        b_ps = [a.ps(f"b{k}", [P, 512]) for k in range(2)]
        consts = a.sem("consts")
        xTs_done = a.sem("xTs_done")
        rws_done = a.sem("rws_done")
        rwT_ready = a.sem("rwT_ready")
        rwT_done = a.sem("rwT_done")
        e_ready = a.sem("e_ready")
        b_ready = a.sem("b_ready")
        act_prod = a.sem("act_prod")
        dve_prod = a.sem("dve_prod")
        pair_done = a.sem("pair_done")
        acc_done = a.sem("acc_done")
        fold_done = a.sem("fold_done")
        part_done = a.sem("part_done")
        x_new = a.sem("x_new")
        stored = a.sem("stored")
        sp_mark = a.sem("sp_mark")
        blk = a.ctx.enter_context(nc.Block())
        loads = [(we[:, :, :], w["le_we"]), (be[:, :], w["le_be"])]
        LOADED = 16 * len(loads)

        def at_least(n, lag):
            return not isinstance(n, int) or n >= lag

        @blk.sync
        def _(sp):
            for dst, src in loads:
                sp.dma_start(dst, src).then_inc(consts, 16)
            with sp.Fori(0, N) as i:
                wait_apart(sp, x_new, i * TG + TG, sp_mark)
                sp.dma_start(out_dram[:, bass.ds(i * TG, TG), :], g.x[:, bass.ds(i * TG, TG), :]).then_inc(stored, 16)
            sp.wait_ge(stored, 16 * N)

        @blk.scalar
        def _(act):
            act.preload_act_table_set("natural_log_exp_and_others")

            def prepare(j, u, t):
                if t == 0:
                    act.activation(xTs[:, u, :], g.xT[:, bass.ds(j * TOK, TOK)], ACT.Copy).then_inc(xTs_done, 1)
                if t == 2:
                    act.wait_ge(rwT_ready, j + 1)
                    act.activation(rwT[:, u, :], tr_ps[:, :], ACT.Copy).then_inc(rwT_done, 1)

            def step(i, u, new, ahead):
                for t in T:
                    n = i * TG + t
                    if new:
                        for c in BY_ACT:
                            act.wait_ge(e_ready, n * CH + c + 1)
                            if c == BY_ACT[0] and at_least(n, 2):
                                act.wait_ge(acc_done, (n - 1) * 3)
                            for e in range(C):
                                s = slice(D * e, D * e + D)
                                op = act.activation(prod[:, t % 2, c, s], e_ps[c][:, s], ACT.Copy,
                                                    scale=rws[:, u, t, C * c + e:C * c + e + 1])
                            op.then_inc(act_prod, 1)
                    if ahead:
                        prepare(i + 1, 1 - u, t)

            for t in T:
                prepare(0, 0, t)
            act.wait_ge(rws_done, 1)
            pipelined(act, N, step)

        @blk.tensor
        def _(pe):
            pe.wait_ge(consts, LOADED)

            def prepare(j, u, t):
                if t == 1:
                    pe.wait_ge(rws_done, j + 1)
                    for k in T:
                        mm = pe.transpose(tr_ps[:, P * k:P * k + P], rws[:, u, k, :], g.ident[:, :])
                    mm.then_inc(rwT_ready, 1)

            def step(i, u, new, ahead):
                for t in T if new else ():
                    n = i * TG + t
                    s = slice(P * t, P * t + P)
                    for c in range(CH):
                        if c == 0 and t == 0:
                            pe.wait_ge(xTs_done, i + 1)
                        if at_least(n, 1):
                            if c in BY_ACT:
                                pe.wait_ge(act_prod, (n - 1) * 2 + BY_ACT.index(c) + 1)
                            else:
                                pe.wait_ge(dve_prod, (n - 1) * 3 + BY_DVE.index(c) + 1)
                        pe.matmul(e_ps[c][:, :], xTs[:, u, s], we[:, c, :], start=True, stop=True).then_inc(e_ready, 1)
                    if t == 0:
                        pe.wait_ge(rwT_done, i + 1)
                    if at_least(n, 2):
                        pe.wait_ge(part_done, n - 1)
                    pe.matmul(b_ps[t % 2][:, 0:D], rwT[:, u, s], be[:, :], start=True, stop=True).then_inc(b_ready, 1)
                    if ahead:
                        prepare(i + 1, 1 - u, t)

            for t in T:
                prepare(0, 0, t)
            pipelined(pe, N, step)

        @blk.gpsimd
        def _(pool):
            def step(i, u, new, ahead):
                for t in T if new else ():
                    n = i * TG + t
                    p, sum_ = prod[:, t % 2, :, :], acc[:, t % 2, :]
                    if at_least(n, 2):
                        pool.wait_ge(fold_done, (n - 1) * 2)
                    pool.wait_ge(dve_prod, n * 3 + 1)
                    pool.wait_ge(act_prod, n * 2 + 1)
                    pool.tensor_tensor(sum_, p[:, 0, :], p[:, 1, :], ALU.add).then_inc(acc_done, 1)
                    pool.wait_ge(acc_done, n * 3 + 1)
                    pool.wait_ge(dve_prod, n * 3 + 2)
                    pool.tensor_tensor(sum_, sum_, p[:, 2, :], ALU.add).then_inc(acc_done, 1)
                    pool.wait_ge(acc_done, n * 3 + 2)
                    pool.wait_ge(pair_done, n + 1)
                    pool.tensor_tensor(sum_, sum_, p[:, 4, :], ALU.add).then_inc(acc_done, 1)

            pipelined(pool, N, step)

        @blk.vector
        def _(dve):
            def prepare(j, u, t):
                if t == 0:
                    dve.tensor_copy(rws[:, u, :, :], g.rw[:, bass.ds(j * TG, TG), 0:E]).then_inc(rws_done, 1)

            def step(i, u, new, ahead):
                for t in T:
                    n = i * TG + t
                    last = (new or t == 0) and at_least(n, 1)
                    q, sum_ = part[:, (t - 1) % 2, :], acc[:, (t - 1) % 2, :]

                    def weighted(k):
                        c = BY_DVE[k]
                        dve.wait_ge(e_ready, n * CH + c + 1)
                        dve.tensor_tensor(prod[:, t % 2, c, :].rearrange("p (e d) -> p e d", e=C),
                                          e_ps[c][:, :].rearrange("p (e d) -> p e d", e=C),
                                          rws[:, u, t, C * c:C * c + C].unsqueeze(2).to_broadcast([P, C, D]),
                                          ALU.mult).then_inc(dve_prod, 1)

                    if new:
                        if at_least(n, 2):
                            dve.wait_ge(acc_done, (n - 1) * 3)
                        weighted(0)
                        weighted(1)
                    if last:
                        dve.wait_ge(acc_done, n * 3)
                        dve.tensor_tensor(q, sum_[:, 0:2 * D], sum_[:, 2 * D:4 * D], ALU.add).then_inc(fold_done, 1)
                    if new:
                        weighted(2)
                    if last:
                        dve.wait_ge(fold_done, n * 2 - 1)
                        dve.tensor_tensor(q[:, 0:D], q[:, 0:D], q[:, D:2 * D], ALU.add).then_inc(fold_done, 1)
                    if new:
                        dve.wait_ge(act_prod, n * 2 + 2)
                        dve.wait_ge(dve_prod, n * 3 + 3)
                        dve.tensor_tensor(prod[:, t % 2, 4, :], prod[:, t % 2, 3, :], prod[:, t % 2, 4, :], ALU.add).then_inc(pair_done, 1)
                    if last:
                        dve.wait_ge(fold_done, n * 2)
                        dve.wait_ge(b_ready, n)
                        dve.tensor_tensor(q[:, 0:D], b_ps[(t - 1) % 2][:, 0:D], q[:, 0:D], ALU.add).then_inc(part_done, 1)
                        if ahead:
                            prepare(i + 1, 1 - u, t)
                        dve.wait_ge(part_done, n)
                        dve.tensor_tensor(g.x[:, n - 1, :], g.x[:, n - 1, :], q[:, 0:D], ALU.add).then_inc(x_new, 1)
                    elif ahead:
                        prepare(i + 1, 1 - u, t)

            for t in T:
                prepare(0, 0, t)
            pipelined(dve, N, step)


def softmax_attention(nc, g, w, name, ctx_dram):
    causal = ctx_dram is None
    TG, N, TOK = STREAMS, g.tiles // STREAMS, STREAMS * P
    NB = TG * BPT
    G, M, HD = 4, 4, 8
    H = 2 * M
    SCALE = 1.0 / HD ** 0.5
    T, B = range(TG), range(NB)
    TRANSPOSE, VALUES = 3, 4
    PB = 4
    with Arena(nc, name) as a:
        NQ = 4 if causal else 2
        wqk = a.sb("wqk", [D, NQ, D])
        wv = a.sb("wv", [D, D])
        wo = a.sb("wo", [D, D])
        cols = a.sb("cols", [D, 16])
        m_group, m_member = cols[:, 8:12], cols[:, 12:16]
        bo = a.sb("bo", [P, D])
        rope = a.sb("rope", [D, 2, SEQ])
        cm32 = a.sb("cm32", [P, SEQ])
        cm = a.sb("cm", [P, SEQ], bf16)
        v_mask = a.sb("v_mask", [P, 2, D])
        ident16 = a.sb("ident16", [P, P], bf16)
        bvb = a.sb("bvb", [D, P])
        ybias = a.sb("ybias", [P, D])
        xvar = a.sb("xvar", [P, 3, g.tiles])
        xr = a.sb("xr", [P, 5, g.tiles])
        z = a.sb("z", [P, TG, D])
        an = a.sb("an", [P, TG, D])
        aT = a.sb("aT", [D, NB, 2, SEQ])
        kv_in = a.sb("kv_in", [P, TG, D])
        cT = aT if causal else a.sb("cT", [D, NB, 2, SEQ])
        ra = a.sb("ra", [D, 2, TOK])
        rb = a.sb("rb", [D, 2, TOK])
        qg = a.sb("qg", [D, 2, NB, G, SEQ])
        km = a.sb("km", [D, 2, NB, M, SEQ])
        vB = a.sb("vB", [P, 2, NB, 2, D])
        nm = a.sb("nm", [P, PB, H])
        rden = a.sb("rden", [P, PB, H])
        prob = a.sb("prob", [P, PB, H, SEQ])
        pT = a.sb("pT", [P, 2, TOK])
        atT = a.sb("atT", [D, TOK])
        s_ps = [a.ps(f"s{n}", [P, 512]) for n in range(2)]
        pT_ps = [a.ps(f"pT{n}", [P, 512]) for n in range(2)]
        at_ps = a.ps("at", [P, 512])
        f_ps = [a.ps(f"f{n}", [P, 512]) for n in range(3)]
        aT_ps, cT_ps, y_ps = f_ps[0], f_ps[1], f_ps[2]
        qk_ps = [f_ps[2], f_ps[0], f_ps[1], f_ps[2]]
        v_ps = [f_ps[0], f_ps[1]]

        consts = a.sem("consts")
        casts_done = a.sem("casts_done")
        moments_step = a.sem("moments_step")
        ln_step = a.sem("ln_step")
        rr_done = a.sem("rr_done")
        bias_ready = a.sem("bias_ready")
        ybias_done = a.sem("ybias_done")
        kv_loaded = a.sem("kv_loaded")
        an_done = a.sem("an_done")
        z_done = a.sem("z_done")
        aT_ready = a.sem("aT_ready")
        cT_ready = a.sem("cT_ready")
        aT_done = a.sem("aT_done")
        cT_done = a.sem("cT_done")
        qk_ready = a.sem("qk_ready")
        qk_left = a.sem("qk_left")
        rope_done = a.sem("rope_done")
        v_ready = a.sem("v_ready")
        qg_done = a.sem("qg_done")
        km_done = a.sem("km_done")
        vB_done = a.sem("vB_done")
        base_done = a.sem("base_done")
        s_ready = a.sem("s_ready")
        nm_done = a.sem("nm_done")
        sub_done = a.sem("sub_done")
        exp_done = a.sem("exp_done")
        sum_done = a.sem("sum_done")
        rden_done = a.sem("rden_done")
        prob_done = a.sem("prob_done")
        pT_ready = a.sem("pT_ready")
        pT_done = a.sem("pT_done")
        pv_done = a.sem("pv_done")
        atT_done = a.sem("atT_done")
        y_ready = a.sem("y_ready")
        x_new = a.sem("x_new")
        st_done = a.sem("st_done")
        mark = a.sem("mark")
        blk = a.ctx.enter_context(nc.Block())
        loads = [(wqk[:, :, :], w[name + "_wqk"]), (wv[:, :], w[name + "_wv"]), (wo[:, :], w[name + "_wo"]),
                 (cols[:, :], w[name + "_cols"]), (bo[:, :], w[name + "_bo"]), (v_mask[:, :, :], w["at_v_mask"])]
        if causal:
            loads += [(rope[:, :, :], w["at_rope"]), (cm32[:, :], w["at_causal"])]
        LOADED = 16 * len(loads)

        by_row = lambda m: m.rearrange("p (b s) -> p b s", b=NB)
        step_rows = lambda i: g.x[:, bass.ds(i * TG, TG), :]

        def has(i, b, lag, new):
            return new if b >= lag else not (isinstance(i, int) and i == 0)

        @blk.sync
        def _(sp):
            for dst, src in loads:
                sp.dma_start(dst, src).then_inc(consts, 16)
            if not causal:
                sp.dma_start(kv_in[:, :, :], ctx_dram[:, 0:TG, :]).then_inc(kv_loaded, 16)
                with sp.Fori(0, N - 1) as k:
                    wait_apart(sp, kv_loaded, k * 16 + 16, mark)
                    wait_apart(sp, cT_ready, k + 1, mark)
                    sp.dma_start(kv_in[:, :, :], ctx_dram[:, bass.ds(k * TG + TG, TG), :]).then_inc(kv_loaded, 16)
                sp.wait_ge(kv_loaded, 16 * N)

        @blk.gpsimd
        def _(pool):
            pool.wait_ge(ybias_done, 1)

            def prepare(j, u, b):
                bias = ybias[:, :].unsqueeze(1).to_broadcast([P, TG, D])
                if causal:
                    if b == 1:
                        pool.wait_ge(z_done, j * TG + TG)
                        pool.tensor_tensor(z[:, :, :], z[:, :, :], bias, ALU.add).then_inc(base_done, 1)
                    if b == 2:
                        pool.wait_ge(base_done, 2 * j + 1)
                        pool.wait_ge(an_done, j * TG + TG)
                        pool.tensor_tensor(step_rows(j), z[:, :, :], step_rows(j), ALU.add).then_inc(base_done, 1)
                    if b in (3, 4):
                        k = b - 3
                        pool.wait_ge(qk_left, j * NQ + 3 + k)
                        pool.tensor_tensor(ra[:, k, :], ra[:, k, :], rb[:, k, :], ALU.add).then_inc(rope_done, 1)
                elif b == 2:
                    pool.wait_ge(an_done, j * TG + TG)
                    pool.tensor_tensor(step_rows(j), bias, step_rows(j), ALU.add).then_inc(base_done, 2)
                if b >= 4:
                    pool.wait_ge(rope_done, j * 2 + (1 if causal else 2))
                    for k in ((0,), (1,), (2,), (3,))[b - 4]:
                        pool.tensor_tensor(qg[:, u, :, k, :], by_row(ra[:, 0, :]),
                                           m_group[:, k:k + 1].unsqueeze(2).to_broadcast([D, NB, SEQ]),
                                           ALU.mult).then_inc(qg_done, 1)

            def step(i, u, new, ahead):
                for b in B:
                    r = i * NB + b
                    if has(i, b, 1, new):
                        pool.wait_ge(rden_done, r)
                        k = (b - 1) % PB
                        pool.tensor_tensor(prob[:, k, :, :], prob[:, k, :, :],
                                           rden[:, k, :].unsqueeze(2).to_broadcast([P, H, SEQ]), ALU.mult).then_inc(prob_done, 1)
                    if ahead:
                        prepare(i + 1, 1 - u, b)

            for b in B:
                prepare(0, 0, b)
            pipelined(pool, N, step)

        @blk.scalar
        def _(act):
            act.preload_act_table_set("natural_log_exp_and_others")
            act.wait_ge(moments_step, 6)
            act.activation(xr[:, 0, :], xvar[:, 1, :], ACT.Ln, bias=g.ln_eps[:, :], scale=1.0 / D).then_inc(ln_step, 1)
            act.wait_ge(ln_step, 1)
            act.activation(xr[:, 1, :], xr[:, 0, :], ACT.Exp, scale=-0.5).then_inc(ln_step, 1)
            if causal:
                act.wait_ge(rr_done, 2)
                act.activation(xr[:, 2, :], xr[:, 4, :], ACT.Ln, bias=g.ln_eps[:, :], scale=1.0 / D).then_inc(ln_step, 1)
                act.wait_ge(ln_step, 3)
                act.activation(xr[:, 2, :], xr[:, 2, :], ACT.Exp, scale=-0.5).then_inc(ln_step, 1)
            act.wait_ge(consts, LOADED)

            def prepare(j, u, b):
                twice = lambda ps: by_row(ps[:, :]).unsqueeze(2).to_broadcast([D, NB, 2, SEQ])
                if b == 1:
                    act.wait_ge(aT_ready, j + 1)
                    if causal:
                        act.activation(aT[:, :, :, :], twice(aT_ps), ACT.Identity, bias=cols[:, 6:7],
                                       scale=cols[:, 5:6]).then_inc(aT_done, 1)
                    else:
                        act.activation(aT[:, :, 0, :], by_row(aT_ps[:, :]), ACT.Copy).then_inc(aT_done, 1)
                        act.wait_ge(cT_ready, j + 1)
                        act.activation(cT[:, :, :, :], twice(cT_ps), ACT.Copy).then_inc(cT_done, 1)
                if b == 2 and not causal:
                    for k in range(2):
                        act.wait_ge(qk_ready, j * 2 + k + 1)
                        act.activation(ra[:, k, :], qk_ps[k][:, :], ACT.Identity, bias=cols[:, k:k + 1]).then_inc(rope_done, 1)
                if b in (5, 6):
                    c = b - 5
                    for k in range(2):
                        if b == 5 and k == 0:
                            act.wait_ge(rope_done, j * 2 + 2)
                        m = 2 * c + k
                        act.activation(km[:, u, :, m, :], by_row(ra[:, 1, :]), ACT.Copy,
                                       scale=m_member[:, m:m + 1]).then_inc(km_done, 1)

            def step(i, u, new, ahead):
                for b in B:
                    r = i * NB + b
                    if has(i, b, TRANSPOSE, new):
                        act.wait_ge(pT_ready, r - TRANSPOSE + 1)
                        if has(i, b, TRANSPOSE + 2, new or b < TRANSPOSE + 2):
                            act.wait_ge(pv_done, r - TRANSPOSE - 1)
                        act.activation(pT[:, (b - TRANSPOSE) % 2, :], pT_ps[(b - TRANSPOSE) % 2][:, :], ACT.Copy).then_inc(pT_done, 1)
                    if b == VALUES and has(i, 0, 1, new):
                        act.wait_ge(pv_done, r - VALUES)
                        act.activation(atT[:, :], at_ps[:, :], ACT.Copy).then_inc(atT_done, 1)
                    if new:
                        act.wait_ge(sub_done, r + 1)
                        act.activation(prob[:, b % PB, :, :], prob[:, b % PB, :, :], ACT.Exp, scale=SCALE).then_inc(exp_done, 1)
                    if ahead:
                        prepare(i + 1, 1 - u, b)

            for b in B:
                prepare(0, 0, b)
            pipelined(act, N, step)

        @blk.tensor
        def _(pe):
            pe.wait_ge(consts, LOADED)
            pe.wait_ge(casts_done, 3 if causal else 2)
            pe.matmul(y_ps[:, 0:D], bvb[:, :], wo[:, :], start=True, stop=True).then_inc(bias_ready, 1)
            pe.wait_ge(ybias_done, 1)

            def project(j, k, left):
                if left is not None:
                    pe.wait_ge(qk_left, left)
                pe.matmul(qk_ps[k][:, :], wqk[:, k, :], (cT if k % 2 else aT)[:, :, 0, :], start=True, stop=True).then_inc(qk_ready, 1)

            def prepare(j, u, b):
                if b == 1:
                    if not (isinstance(j, int) and j == 0):
                        pe.wait_ge(vB_done, 2 * j)
                    for t in T:
                        pe.wait_ge(an_done, j * TG + t + 1)
                        mm = pe.transpose(aT_ps[:, P * t:P * t + P], an[:, t, :], g.ident[:, :])
                    mm.then_inc(aT_ready, 1)
                    if not causal:
                        pe.wait_ge(kv_loaded, j * 16 + 16)
                        for t in T:
                            mm = pe.transpose(cT_ps[:, P * t:P * t + P], kv_in[:, t, :], g.ident[:, :])
                        mm.then_inc(cT_ready, 1)
                if b == 2:
                    pe.wait_ge(aT_done, j + 1)
                    project(j, 0, None)
                    if not causal:
                        pe.wait_ge(cT_done, j + 1)
                    project(j, 1, None)
                if causal and b == 3:
                    project(j, 2, None)
                if causal and b == 4:
                    project(j, 3, j * NQ + 1)
                if b in (4, 5):
                    c = b - 4
                    if causal:
                        pe.wait_ge(qk_left, j * NQ + 2 + c)
                    else:
                        pe.wait_ge(rope_done, 2 * j + 2)
                    for k in range(4):
                        mm = pe.matmul(v_ps[c][:, D * k:D * k + D], cT[:, 4 * c + k, :, :], wv[:, :], start=True, stop=True)
                    mm.then_inc(v_ready, 1)

            def step(i, u, new, ahead):
                for b in B:
                    r = i * NB + b
                    if new:
                        bank = s_ps[b % 2]
                        if b == 0:
                            pe.wait_ge(qg_done, i * G + G)
                            pe.wait_ge(km_done, i * M + M)
                        if has(i, b, 2, new):
                            pe.wait_ge(sub_done, r - 1)
                        if causal:
                            pe.matmul(bank[:, :], ident16[:, :], cm[:, :].unsqueeze(1).to_broadcast([P, H, SEQ]),
                                      start=True, stop=False, skip_group_check=True)
                        for half in range(2):
                            mm = pe.matmul(bank[:, 256 * half:256 * half + 256], qg[:, u, b, 2 * half:2 * half + 2, :],
                                           km[:, u, b, :, :], start=not causal, stop=True, skip_group_check=True)
                        mm.then_inc(s_ready, 1)
                    if has(i, b, TRANSPOSE, new):
                        k = (b - TRANSPOSE) % PB
                        pe.wait_ge(prob_done, r - TRANSPOSE + 1)
                        if has(i, b, TRANSPOSE + 2, new or b < TRANSPOSE + 2):
                            pe.wait_ge(pT_done, r - TRANSPOSE - 1)
                        for c in range(4):
                            mm = pe.transpose(pT_ps[(b - TRANSPOSE) % 2][:, P * c:P * c + P], prob[:, k, 2 * c:2 * c + 2, :], g.ident[:, :])
                        mm.then_inc(pT_ready, 1)
                    if ahead:
                        prepare(i + 1, 1 - u, b)
                    if has(i, b, VALUES, new):
                        pe.wait_ge(pT_done, r - VALUES + 1)
                        row, v = (b - VALUES) % NB, u if b >= VALUES else 1 - u
                        if row == 0:
                            pe.wait_ge(vB_done, 2 * i + 2)
                            if has(i, 0, 1, new):
                                pe.wait_ge(atT_done, i)
                        probs = pT[:, (b - VALUES) % 2, :].rearrange("p (h j g s) -> p h j g s", h=2, j=2, g=2)
                        for gr in range(G):
                            q = slice(32 * gr, 32 * gr + 32)
                            for j in range(2):
                                mm = pe.matmul(at_ps[q, SEQ * row:SEQ * row + SEQ], vB[:, v, row, j, q],
                                               probs[:, gr // 2, j, gr % 2, :], start=(j == 0), stop=(j == 1),
                                               tile_position=(0, 32 * gr), skip_group_check=True)
                        mm.then_inc(pv_done, 1)
                    if b == 5 and has(i, 0, 1, new):
                        pe.wait_ge(atT_done, i)
                        if ahead and causal:
                            pe.wait_ge(qk_left, i * NQ + 2 * NQ)
                        for t in T:
                            mm = pe.matmul(y_ps[:, D * t:D * t + D], atT[:, P * t:P * t + P], wo[:, :], start=True, stop=True)
                        mm.then_inc(y_ready, 1)

            for b in B:
                prepare(0, 0, b)
            pipelined(pe, N, step)

        @blk.vector
        def _(dve):
            ln_moments(dve, g.st, xvar, moments_step, 0)
            dve.wait_ge(consts, LOADED)
            dve.tensor_copy(ident16[:, :], g.ident[:, :]).then_inc(casts_done, 1)
            dve.tensor_copy(bvb[:, :], cols[:, 4:5].to_broadcast([D, P])).then_inc(casts_done, 1)
            if causal:
                dve.tensor_copy(cm[:, :], cm32[:, :]).then_inc(casts_done, 1)
            dve.wait_ge(bias_ready, 1)
            dve.tensor_tensor(ybias[:, :], y_ps[:, 0:D], bo[:, :], ALU.add).then_inc(ybias_done, 1)
            dve.wait_ge(ln_step, 2)
            if causal:
                dve.tensor_tensor(xr[:, 4, :], xvar[:, 1, :], xr[:, 1, :], ALU.mult).then_inc(rr_done, 1)
                dve.wait_ge(rr_done, 1)
                dve.tensor_tensor(xr[:, 4, :], xr[:, 4, :], xr[:, 1, :], ALU.mult).then_inc(rr_done, 1)
                dve.wait_ge(ln_step, 4)
                dve.tensor_tensor(xr[:, 3, :], xr[:, 1, :], xr[:, 2, :], ALU.mult).then_inc(rr_done, 1)
                dve.wait_ge(rr_done, 3)

            def prepare(j, u, b):
                if b == 0:
                    if not (isinstance(j, int) and j == 0):
                        dve.wait_ge(base_done, 2 * j)
                        dve.wait_ge(aT_ready, j)
                    for t in T:
                        n = j * TG + t
                        mean, rstd = xvar[:, 0, bass.ds(n, 1)], xr[:, 1, bass.ds(n, 1)]
                        if causal:
                            dve.tensor_scalar(z[:, t, :], g.x[:, n, :], mean, rstd, ALU.subtract, ALU.mult).then_inc(z_done, 1)
                            rstd = xr[:, 3, bass.ds(n, 1)]
                        dve.tensor_scalar(an[:, t, :], g.x[:, n, :], mean, rstd, ALU.subtract, ALU.mult).then_inc(an_done, 1)
                if causal and b in (2, 3, 4):
                    if b == 2 and not (isinstance(j, int) and j == 0):
                        dve.wait_ge(km_done, j * M)
                        dve.wait_ge(qg_done, j * G)
                    for k in ((0, 1), (2,), (3,))[b - 2]:
                        dve.wait_ge(qk_ready, j * NQ + k + 1)
                        dve.scalar_tensor_tensor(out=by_row((rb if k >= 2 else ra)[:, k % 2, :]), in0=by_row(qk_ps[k][:, :]),
                                                 scalar=cols[:, k:k + 1],
                                                 in1=rope[:, k // 2, :].unsqueeze(1).to_broadcast([D, NB, SEQ]),
                                                 op0=ALU.add, op1=ALU.mult).then_inc(qk_left, 1)
                if b in (5, 6):
                    c = b - 5
                    dve.wait_ge(v_ready, j * 2 + c + 1)
                    dve.tensor_tensor(vB[:, u, 4 * c:4 * c + 4, :, :],
                                      v_ps[c][:, :].rearrange("p (b d) -> p b d", b=4).unsqueeze(2).to_broadcast([P, 4, 2, D]),
                                      v_mask[:, :, :].unsqueeze(1).to_broadcast([P, 4, 2, D]), ALU.mult).then_inc(vB_done, 1)

            def step(i, u, new, ahead):
                for b in B:
                    r = i * NB + b
                    k = (b - 1) % PB
                    if new:
                        scores = s_ps[b % 2][:, :].rearrange("p (h t) -> p h t", t=SEQ)
                        dve.wait_ge(s_ready, r + 1)
                        dve.tensor_reduce(nm[:, b % PB, :], scores, AX.X, ALU.max).then_inc(nm_done, 1)
                    if has(i, b, 1, new):
                        dve.wait_ge(exp_done, r)
                        dve.tensor_reduce(rden[:, k, :], prob[:, k, :, :], AX.X, ALU.add).then_inc(sum_done, 1)
                    if new:
                        dve.wait_ge(nm_done, r + 1)
                        if has(i, b, PB, new):
                            dve.wait_ge(pT_ready, r - PB + 1)
                        dve.tensor_tensor(prob[:, b % PB, :, :], scores,
                                          nm[:, b % PB, :].unsqueeze(2).to_broadcast([P, H, SEQ]), ALU.subtract).then_inc(sub_done, 1)
                    if has(i, b, 1, new):
                        dve.wait_ge(sum_done, r)
                        dve.reciprocal(rden[:, k, :], rden[:, k, :]).then_inc(rden_done, 1)
                    if b in (6, 7) and has(i, 0, 1, new):
                        if b == 6:
                            dve.wait_ge(y_ready, i)
                            dve.wait_ge(base_done, 2 * i)
                            dve.tensor_tensor(step_rows(i - 1), y_ps[:, :].rearrange("p (t d) -> p t d", t=TG),
                                              step_rows(i - 1), ALU.add).then_inc(x_new, 1)
                        else:
                            dve.wait_ge(x_new, i)
                            for t in T:
                                n = i * TG - TG + t
                                dve.bn_stats(g.st[:, n, :], g.x[:, n, :]).then_inc(st_done, 1)
                    if ahead:
                        prepare(i + 1, 1 - u, b)

            for b in B:
                prepare(0, 0, b)
            pipelined(dve, N, step)
            dve.wait_ge(st_done, g.tiles)


class Shared:
    pass


def decoder_kernel(nc, w, x_dram, ctx_dram, out_dram, tiles=64, stages=6):
    g = Shared()
    g.tiles = tiles
    with Arena(nc, "all") as a:
        g.x = a.sb("x", [P, tiles, D])
        g.st = a.sb("st", [P, tiles, 6])
        g.xT = a.sb("xT", [D, tiles * P])
        g.rw = a.sb("rw", [P, tiles, 20])
        g.ident = a.sb("ident", [P, P])
        g.ln_eps = a.sb("ln_eps", [P, 1])
        xv = x_dram.rearrange("b s d -> (b s) d").rearrange("(t p) d -> p t d", p=P)
        cv = ctx_dram.rearrange("b s d -> (b s) d").rearrange("(t p) d -> p t d", p=P)
        ctx_rows = ctx_dram.rearrange("b s d -> s b d")
        ov = out_dram.rearrange("b s d -> (b s) d").rearrange("(t p) d -> p t d", p=P)
        linear_attention(nc, g, w, xv)
        if stages >= 2:
            mlstm(nc, g, w, ctx_rows)
        if stages >= 3:
            normed_transposed(nc, g, w, "r0", hidden=False)
            silu_experts(nc, g, w)
        if stages >= 4:
            softmax_attention(nc, g, w, "sa", None)
        if stages >= 5:
            softmax_attention(nc, g, w, "xa", cv)
        if stages >= 6:
            normed_transposed(nc, g, w, "r1", hidden=True)
            linear_experts(nc, g, w, ov)
        if stages < 6:
            with Arena(nc, "end") as e:
                stored = e.sem("stored")
                blk = e.ctx.enter_context(nc.Block())

                @blk.sync
                def _(sp):
                    sp.dma_start(ov, g.x[:, :, :]).then_inc(stored, 16)
                    sp.wait_ge(stored, 16)


def shape_constants():
    import numpy as np
    hd = 8
    pos = np.arange(64, dtype=np.float32)[:, None]
    freq = (1.0 / 10000.0 ** (np.arange(0, hd, 2, dtype=np.float32) / hd)).astype(np.float32)
    ang = pos * freq[None]
    cos, sin = np.cos(ang).astype(np.float32), np.sin(ang).astype(np.float32)
    c = {}
    c["ident"] = np.eye(128, dtype=np.float32)
    c["rope_c"] = np.tile(np.repeat(cos, 2, axis=1), (2, 32))
    s = np.stack([sin, -sin], axis=-1).reshape(64, 8)
    c["rope_s"] = np.tile(s, (2, 32))
    head = np.arange(128) // 8
    same = (head[:, None] == head[None, :]).astype(np.float32)
    c["kv_mask"] = np.concatenate([same, (head[:, None] == np.arange(16)[None]).astype(np.float32)], axis=1)
    p, h8 = np.arange(128), np.arange(8)
    c["ml_m_h2"] = (p[:, None] // 16 % 2 == np.arange(2)[None])
    c["ml_m_pair"] = (p[:, None] // 32 == np.arange(4)[None]) / 16 ** 0.5
    first = np.arange(512) % 64 == 0
    c["ml_keep"] = np.tile(1.0 - first, (8, 1))
    c["ml_restart"] = np.tile(-1e30 * first, (8, 1))
    c["ml_m_par"] = (h8[:, None] % 2 == np.arange(2)[None])
    c["ml_m_hp"] = -1.0 * (h8[:, None] // 2 == np.arange(4)[None])
    t, s = np.arange(64)[:, None], np.arange(64)[None]
    c["ml_causal"] = np.tile(np.where(t <= s, 0.0, -1e30), (2, 1))
    c["ml_argL"] = np.broadcast_to((h8[:, None] % 2 == np.arange(2)[None])[:, None, :, None], (8, 8, 2, 64))
    c["ml_argR"] = np.broadcast_to((h8[:, None] // 2 == np.arange(4)[None])[:, None, :, None], (8, 8, 4, 64))
    for name, experts in (("r0_first", 8), ("r1_first", 20)):
        c[name] = np.broadcast_to(np.arange(experts) > 0, (128, 64, experts))
    unit = np.arange(1024)
    owner = np.where(unit < 768, unit // 96, 8)
    c["se_sel"] = (owner[None, :] == np.arange(9)[:, None]).reshape(9, 8, 128)
    c["at_rope"] = np.stack([np.tile(np.repeat(cos.T, 2, axis=0), (16, 1)),
                             np.tile(np.stack([-sin.T, sin.T], axis=1).reshape(8, 64), (16, 1))], axis=1)
    c["at_causal"] = np.tile(np.where(s <= t, 0.0, -1e30), (2, 1))
    half = np.arange(128)[:, None, None] // 64
    c["at_v_mask"] = (p[None, None, :] // 8 % 4) == 2 * np.arange(2)[None, :, None] + half
    return {k: np.ascontiguousarray(v, dtype=np.float32) for k, v in c.items()}


def laid_out(inputs):
    import numpy as np
    i = inputs
    c = {}
    c["la_wqkv"] = np.concatenate([i["L0_attn_Wq"], i["L0_attn_Wk"], i["L0_attn_Wv"]], axis=1)
    c["la_wo"] = i["L0_attn_Wo"]
    f32 = np.float32
    wg = np.zeros((128, 3, 40), f32)
    wg[:, :, 0:8] = i["L0_xattn_igate_w"].reshape(8, 3, 128).transpose(2, 1, 0)
    wg[:, :, 32:40] = i["L0_xattn_fgate_w"].reshape(8, 3, 128).transpose(2, 1, 0)
    c["ml_wg"] = wg
    gb = np.zeros((40, 2), f32)
    gb[0:8, 0] = i["L0_xattn_igate_b"]
    gb[32:40, 1] = i["L0_xattn_fgate_b"]
    c["ml_gate_b"] = gb
    c["ml_scale"] = np.tile(i["L0_xattn_ln_scale"], (128, 1))
    w1, ws1 = i["L0_ffn_W1"], i["L0_ffn_Ws1"]
    up = np.zeros((2, 1024, 128), f32)
    for k in range(2):
        up[k, 0:768] = w1[:, 96 * k:96 * k + 96].reshape(768, 128)
        up[k, 768:960] = ws1[192 * k:192 * k + 192]
    c["se_w1"] = up.transpose(2, 0, 1).reshape(128, 2, 8, 128)
    down = np.zeros((1024, 128), f32)
    down[0:768] = i["L0_ffn_W2"].transpose(0, 2, 1).reshape(768, 128)
    down[768:960] = i["L0_ffn_Ws2"].T
    c["se_w2"] = down.reshape(8, 128, 128).transpose(1, 0, 2)
    partner = np.arange(128) ^ 1
    feature = np.arange(128)[:, None]
    masks = [feature // 32 == np.arange(4)[None], feature // 8 % 4 == np.arange(4)[None]]
    for name, src, extra in (("sa", "L1_attn", True), ("xa", "L1_xattn", False)):
        wq, wk = i[src + "_Wq"], i[src + "_Wk"]
        bq, bk = i[src + "_bq"], i[src + "_bk"]
        qk = [wq, wk] + ([wq[:, partner], wk[:, partner]] if extra else [])
        c[name + "_wqk"] = np.stack(qk, axis=1)
        c[name + "_wv"], c[name + "_wo"] = i[src + "_Wv"], i[src + "_Wo"]
        c[name + "_bo"] = np.tile(i[src + "_bo"], (128, 1))
        col = [bq, bk, bq[partner], bk[partner], i[src + "_bv"]]
        col += [i["L1_attn_ln_gamma"], i["L1_attn_ln_beta"], np.zeros(128, f32)]
        c[name + "_cols"] = np.concatenate([np.stack(col, axis=1)] + [m.astype(f32) for m in masks], axis=1)
    c["le_we"] = i["L1_ffn_We"].transpose(1, 0, 2).reshape(128, 5, 512)
    c["le_be"] = i["L1_ffn_be"]
    c["r0_gate"] = i["L0_ffn_gate_w"].T
    c["r1_gate"] = i["L1_ffn_wg2"][:, 0:20]
    c["r1_wg1"] = i["L1_ffn_wg1"]
    c["r1_bg1"] = i["L1_ffn_bg1"].reshape(32, 1)
    c["r1_bg2"] = np.tile(i["L1_ffn_bg2"][0:20], (128, 1))
    return {k: np.ascontiguousarray(v) for k, v in c.items()}


def kernel(**inputs):
    import numpy as _np
    import concourse.bacc as _bacc
    from concourse import mybir as _mybir
    from concourse.bass_utils import run_bass_kernel_spmd as _run

    inputs = {k: _np.asarray(v) for k, v in inputs.items()}
    nc = _bacc.Bacc("TRN2", target_bir_lowering=False, num_devices=1)
    arrays = {"x": inputs["x"], "ctx": inputs["ctx_1024"], **shape_constants(), **laid_out(inputs)}
    aps = {k: nc.dram_tensor(f"in_{k}", v.shape, _mybir.dt.from_np(v.dtype), kind="ExternalInput").ap()
           for k, v in arrays.items()}
    out = nc.dram_tensor("out", inputs["x"].shape, _mybir.dt.float32, kind="ExternalOutput").ap()
    decoder_kernel(nc, aps, aps["x"], aps["ctx"], out)
    r = _run(nc, [{f"in_{k}": _np.ascontiguousarray(v) for k, v in arrays.items()}], core_ids=[0])
    return r.results[0]["out"]
```

```python
import concourse.bass as bass
from concourse import mybir
from contextlib import ExitStack

fp32 = mybir.dt.float32
bf16 = mybir.dt.bfloat16
ALU = mybir.AluOpType
ACT = mybir.ActivationFunctionType
AX = mybir.AxisListType

P = 128
SEQ = 64
BPT = P // SEQ
D = 128
LN_EPS = 1e-5
STREAMS = 4


class Arena:

    def __init__(self, nc, stage):
        self.nc, self.stage, self.ctx, self.held = nc, stage, ExitStack(), []

    def __enter__(self):
        return self

    def __exit__(self, *a):
        self.ctx.__exit__(*a)
        if self.held:
            self.nc.clear_and_free_semaphores(self.held)
            self.nc.all_engine_barrier()

    def sb(self, name, shape, dt=fp32):
        return self.ctx.enter_context(self.nc.sbuf_tensor(f"{self.stage}_{name}", shape, dt))

    def ps(self, name, shape, dt=fp32):
        return self.ctx.enter_context(self.nc.psum_tensor(f"{self.stage}_{name}", shape, dt))

    def sem(self, name):
        self.held.append(self.nc.alloc_semaphore(f"{self.stage}_{name}"))
        return self.held[-1]


def wait_apart(eng, sem, value, mark):
    eng.wait_ge(sem, value)
    eng.sem_inc(mark, 1)


def ln_moments(dve, st, work, moments_step, done):
    even, odd = st[:, :, 1], st[:, :, 4]
    mean, var, diff = work[:, 0, :], work[:, 1, :], work[:, 2, :]
    dve.tensor_tensor(mean, even, odd, ALU.add).then_inc(moments_step, 1)
    dve.tensor_tensor(diff, even, odd, ALU.subtract).then_inc(moments_step, 1)
    dve.tensor_tensor(var, st[:, :, 2], st[:, :, 5], ALU.add).then_inc(moments_step, 1)
    dve.wait_ge(moments_step, done + 3)
    dve.tensor_scalar(mean, mean, 0.5, None, ALU.mult).then_inc(moments_step, 1)
    dve.scalar_tensor_tensor(out=diff, in0=diff, scalar=D / 4.0, in1=diff, op0=ALU.mult,
                             op1=ALU.mult).then_inc(moments_step, 1)
    dve.wait_ge(moments_step, done + 5)
    dve.tensor_tensor(var, var, diff, ALU.add).then_inc(moments_step, 1)


def pipelined(eng, steps, step):
    step(0, 0, True, True)
    if steps > 2:
        with eng.Fori(0, (steps - 2) // 2) as k:
            for s in range(2):
                step(2 * k + 1 + s, (1 + s) % 2, True, True)
    step(steps - 1, 1, True, False)
    step(steps, 0, False, False)


def linear_attention(nc, g, w, x_dram):
    ST = 8
    N = g.tiles // ST
    HD = 8
    NH = D // HD
    KVW = D + NH
    NB = 4
    PROJECT, ROPE, SUMS, OUT, WEIGH, TURN, FINAL, ADD = 1, 2, 3, 4, 5, 6, 7, 8
    S = range(ST)
    with Arena(nc, "la") as a:
        wqkv = a.sb("wqkv", [D, 3 * D])
        wo = a.sb("wo", [D, D])
        rope_c = a.sb("rope_c", [P, 2 * D])
        rope_s = a.sb("rope_s", [P, 2 * D])
        kv_mask = a.sb("kv_mask", [D, KVW])
        st0 = a.sb("st0", [P, 2, ST, 6])
        mom = a.sb("mom", [P, 2, 3, ST])
        lnv = a.sb("lnv", [P, 2, 2, ST])
        xn = a.sb("xn", [P, NB, D])
        xnT = a.sb("xnT", [D, NB, P])
        ra = a.sb("ra", [P, NB, 2 * D])
        rb = a.sb("rb", [P, NB, 2 * D])
        qk = a.sb("qk", [P, NB, 2 * D])
        vo = a.sb("vo", [P, NB, BPT, KVW])
        qT = a.sb("qT", [D, NB, P])
        kvm = a.sb("kvm", [D, NB, BPT, KVW])
        den = a.sb("den", [P, NB, NH])
        at = a.sb("at", [P, NB, D])
        atT = a.sb("atT", [D, NB, P])
        qkv_ps = [a.ps(f"qkv{u}", [P, 512])[:, 0:3 * D] for u in range(2)]
        xnT_ps, qT_ps, atT_ps, y_ps = (a.ps(name, [P, 512])[:, 0:D] for name in ("xnT_ps", "qT_ps", "atT_ps", "y_ps"))
        kv_ps = a.ps("kv_ps", [P, 512])[:, 0:BPT * KVW].rearrange("p (b n) -> p b n", b=BPT)
        o_ps = a.ps("o_ps", [P, 512])[:, 0:KVW]

        consts = a.sem("consts")
        x_in = a.sem("x_in")
        others = a.sem("others")
        bn_done = a.sem("bn_done")
        moments_step = a.sem("moments_step")
        ln_done = a.sem("ln_done")
        rstd_done = a.sem("rstd_done")
        ones_set = a.sem("ones_set")
        xn_done = a.sem("xn_done")
        xnT_ready = a.sem("xnT_ready")
        xnT_done = a.sem("xnT_done")
        qkv_done = a.sem("qkv_done")
        rope_ab = a.sem("rope_ab")
        rope_sum = a.sem("rope_sum")
        v_done = a.sem("v_done")
        qk_done = a.sem("qk_done")
        kv_sum = a.sem("kv_sum")
        kvm_done = a.sem("kvm_done")
        qT_ready = a.sem("qT_ready")
        qT_done = a.sem("qT_done")
        o_done = a.sem("o_done")
        den_step = a.sem("den_step")
        at_done = a.sem("at_done")
        atT_ready = a.sem("atT_ready")
        atT_done = a.sem("atT_done")
        y_done = a.sem("y_done")
        x_new = a.sem("x_new")
        bn2_done = a.sem("bn2_done")
        blk = a.ctx.enter_context(nc.Block())
        first = lambda j: isinstance(j, int) and j == 0

        def has(i, b, lag, new):
            return new if b >= lag else not first(i)

        @blk.sync
        def _(sp):
            sp.dma_start(g.x[:, 0:ST, :], x_dram[:, 0:ST, :]).then_inc(x_in, 16)
            with sp.Fori(0, N - 1) as k:
                sp.wait_ge(x_in, k * 16 + 16)
                s = bass.ds(k * ST + ST, ST)
                sp.dma_start(g.x[:, s, :], x_dram[:, s, :]).then_inc(x_in, 16)
            for key, tile in g.c.items():
                sp.dma_start(tile[(slice(None),) * len(w[key].shape)], w[key]).then_inc(others, 16)
            sp.wait_ge(x_in, 16 * N)
            sp.wait_ge(others, 16 * len(g.c))

        @blk.scalar
        def _(act):
            loads = [(wqkv[:, :], w["la_wqkv"]), (wo[:, :], w["la_wo"]), (g.ident[:, :], w["ident"]),
                     (rope_c[:, :], w["rope_c"]), (rope_s[:, :], w["rope_s"]), (kv_mask[:, :], w["kv_mask"])]
            for dst, src in loads:
                act.dma_start(dst, src).then_inc(consts, 16)
            act.wait_ge(consts, 16 * len(loads))
            act.wait_ge(ones_set, 2 + BPT)
            act.preload_act_table_set("natural_log_exp_and_others")

            def prepare(j, u, b):
                if b == 5:
                    act.wait_ge(moments_step, j * 6 + 6)
                    act.activation(lnv[:, u, 0, :], mom[:, u, 1, :], ACT.Ln, bias=g.ln_eps[:, :], scale=1.0 / D).then_inc(ln_done, 1)
                    act.wait_ge(ln_done, j + 1)
                    act.activation(lnv[:, u, 1, :], lnv[:, u, 0, :], ACT.Exp, scale=-0.5).then_inc(rstd_done, 1)

            def step(i, u, new, ahead):
                for b in S:
                    n = i * ST + b
                    if has(i, b, SUMS, new):
                        act.wait_ge(qT_ready, n - SUMS + 1)
                        act.activation(qT[:, (b - SUMS) % NB, :], qT_ps, ACT.Copy).then_inc(qT_done, 1)
                    if new:
                        act.wait_ge(xnT_ready, n + 1)
                        act.activation(xnT[:, b % NB, :], xnT_ps, ACT.Copy).then_inc(xnT_done, 1)
                    if has(i, b, TURN, new):
                        act.wait_ge(atT_ready, n - TURN + 1)
                        act.activation(atT[:, (b - TURN) % NB, :], atT_ps, ACT.Copy).then_inc(atT_done, 1)
                    if has(i, b, ROPE, new):
                        m, k = n - ROPE, (b - ROPE) % NB
                        act.wait_ge(rope_ab, 2 * m + 2)
                        for h in range(BPT):
                            r = slice(SEQ * h, SEQ * h + SEQ)
                            act.activation(vo[r, k, h, 0:D], qkv_ps[(b - ROPE) % 2][r, 2 * D:3 * D], ACT.Copy).then_inc(v_done, 1)
                        act.wait_ge(rope_sum, m + 1)
                        act.activation(qk[:, k, :], ra[:, k, :], ACT.Relu).then_inc(qk_done, 1)
                    if ahead:
                        prepare(i + 1, 1 - u, b)

            for b in S:
                prepare(0, 0, b)
            pipelined(act, N, step)

        @blk.tensor
        def _(pe):
            pe.wait_ge(ones_set, 2 + BPT)
            pe.wait_ge(consts, 16 * 6)

            def step(i, u, new, ahead):
                for b in S:
                    n = i * ST + b

                    def due(lag):
                        return n - lag, (b - lag) % NB, has(i, b, lag + 1, new or b < lag + 1)

                    if has(i, b, PROJECT, new):
                        m, k, later = due(PROJECT)
                        pe.wait_ge(xnT_done, m + 1)
                        if has(i, b, PROJECT + 2, new or b < PROJECT + 2):
                            pe.wait_ge(v_done, BPT * (m - 1))
                        pe.matmul(qkv_ps[(b - PROJECT) % 2], xnT[:, k, :], wqkv[:, :], start=True, stop=True).then_inc(qkv_done, 1)
                    if new:
                        m, k, later = due(0)
                        pe.wait_ge(xn_done, m + 1)
                        if later:
                            pe.wait_ge(xnT_done, m)
                        pe.transpose(xnT_ps, xn[:, k, :], g.ident[:, :]).then_inc(xnT_ready, 1)
                    if has(i, b, TURN, new):
                        m, k, later = due(TURN)
                        pe.wait_ge(at_done, m + 1)
                        if later:
                            pe.wait_ge(atT_done, m)
                        pe.transpose(atT_ps, at[:, k, :], g.ident[:, :]).then_inc(atT_ready, 1)
                    if has(i, b, SUMS, new):
                        m, k, later = due(SUMS)
                        pe.wait_ge(qk_done, m + 1)
                        if later:
                            pe.wait_ge(qT_done, m)
                        pe.transpose(qT_ps, qk[:, k, 0:D], g.ident[:, :]).then_inc(qT_ready, 1)
                        pe.wait_ge(v_done, BPT * (m + 1))
                        if later:
                            pe.wait_ge(kvm_done, m)
                        pe.matmul(kv_ps, qk[:, k, D:2 * D], vo[:, k, :, :], start=True, stop=True).then_inc(kv_sum, 1)
                    if has(i, b, OUT, new):
                        m, k, later = due(OUT)
                        pe.wait_ge(qT_done, m + 1)
                        pe.wait_ge(kvm_done, m + 1)
                        if later:
                            pe.wait_ge(at_done, m)
                        for h in range(BPT):
                            r = slice(SEQ * h, SEQ * h + SEQ)
                            mm = pe.matmul(o_ps[r, :], qT[:, k, r], kvm[:, k, h, :], start=True, stop=True)
                        mm.then_inc(o_done, 1)
                    if has(i, b, FINAL, new):
                        m, k, later = due(FINAL)
                        pe.wait_ge(atT_done, m + 1)
                        if later:
                            pe.wait_ge(x_new, m)
                        pe.matmul(y_ps, atT[:, k, :], wo[:, :], start=True, stop=True).then_inc(y_done, 1)

            pipelined(pe, N, step)

        @blk.gpsimd
        def _(pool):
            pool.memset(g.ln_eps[:, :], LN_EPS).then_inc(ones_set, 1)
            pool.memset(vo[:, :, :, :], 0.0).then_inc(ones_set, 1)
            pool.wait_ge(ones_set, 2)
            for b in range(BPT):
                pool.memset(vo[SEQ * b:SEQ * b + SEQ, :, b, D:KVW], 1.0).then_inc(ones_set, 1)
            pool.wait_ge(ones_set, 2 + BPT)

            def step(i, u, new, ahead):
                for b in S:
                    n = i * ST + b
                    if has(i, b, ROPE, new):
                        m, k = n - ROPE, (b - ROPE) % NB
                        pool.wait_ge(rope_ab, 2 * m + 2)
                        av = ra[:, k, :].rearrange("p (n two) -> p n two", two=2)
                        bv = rb[:, k, :].rearrange("p (n two) -> p n two", two=2)
                        pool.tensor_tensor(av, av, bv[:, :, ::-1], ALU.add).then_inc(rope_sum, 1)

            pipelined(pool, N, step)

        @blk.vector
        def _(dve):
            dve.wait_ge(consts, 16 * 6)
            dve.wait_ge(ones_set, 2 + BPT)

            def prepare(j, u, b):
                if b < 4:
                    if b == 0:
                        dve.wait_ge(x_in, j * 16 + 16)
                    for k in (2 * b, 2 * b + 1):
                        dve.wait_ge(consts, 16 * 6)
                        dve.bn_stats(st0[:, u, k, :], g.x[:, j * ST + k, :]).then_inc(bn_done, 1)
                if b == 4:
                    dve.wait_ge(bn_done, j * ST + ST)
                    ln_moments(dve, st0[:, u, :, :], mom[:, u, :, :], moments_step, j * 6)

            def step(i, u, new, ahead):
                for b in S:
                    n = i * ST + b
                    if new:
                        if b == 0:
                            dve.wait_ge(rstd_done, i + 1)
                        dve.tensor_scalar(xn[:, b % NB, :], g.x[:, n, :], mom[:, u, 0, b:b + 1], lnv[:, u, 1, b:b + 1],
                                          ALU.subtract, ALU.mult).then_inc(xn_done, 1)
                    if has(i, b, WEIGH, new):
                        m, k = n - WEIGH, (b - WEIGH) % NB
                        dve.wait_ge(o_done, m + 1)
                        dve.tensor_scalar(den[:, k, :], o_ps[:, D:KVW], 1e-6, None, ALU.add).then_inc(den_step, 1)
                    if has(i, b, ROPE, new):
                        m, k, bank = n - ROPE, (b - ROPE) % NB, qkv_ps[(b - ROPE) % 2]
                        dve.wait_ge(qkv_done, m + 1)
                        dve.tensor_tensor(ra[:, k, :], bank[:, 0:2 * D], rope_c[:, :], ALU.mult).then_inc(rope_ab, 1)
                        dve.tensor_tensor(rb[:, k, :], bank[:, 0:2 * D], rope_s[:, :], ALU.mult).then_inc(rope_ab, 1)
                    if has(i, b, WEIGH, new):
                        m, k = n - WEIGH, (b - WEIGH) % NB
                        dve.wait_ge(den_step, 2 * m + 1)
                        dve.reciprocal(den[:, k, :], den[:, k, :]).then_inc(den_step, 1)
                    if has(i, b, WEIGH, new):
                        m, k = n - WEIGH, (b - WEIGH) % NB
                        dve.wait_ge(den_step, 2 * m + 2)
                        dve.tensor_tensor(at[:, k, :].rearrange("p (h e) -> p h e", h=NH),
                                          o_ps[:, 0:D].rearrange("p (h e) -> p h e", h=NH),
                                          den[:, k, :].unsqueeze(2).to_broadcast([P, NH, HD]), ALU.mult).then_inc(at_done, 1)
                    if has(i, b, ADD, new):
                        m = n - ADD
                        dve.wait_ge(y_done, m + 1)
                        dve.tensor_tensor(g.x[:, m, :], g.x[:, m, :], y_ps, ALU.add).then_inc(x_new, 1)
                    if has(i, b, SUMS, new):
                        m, k = n - SUMS, (b - SUMS) % NB
                        dve.wait_ge(kv_sum, m + 1)
                        dve.tensor_tensor(kvm[:, k, :, :], kv_ps, kv_mask[:, :].unsqueeze(1).to_broadcast([D, BPT, KVW]),
                                          ALU.mult).then_inc(kvm_done, 1)
                    if has(i, b, ADD, new):
                        m = n - ADD
                        dve.wait_ge(x_new, m + 1)
                        dve.wait_ge(consts, 16 * 6)
                        dve.bn_stats(g.st[:, m, :], g.x[:, m, :]).then_inc(bn2_done, 1)
                    if ahead:
                        prepare(i + 1, 1 - u, b)

            for b in S:
                prepare(0, 0, b)
            pipelined(dve, N, step)
            dve.wait_ge(bn2_done, g.tiles)


def mlstm(nc, g, w, ctx_rows):
    TG = STREAMS
    TOK = TG * P
    NB = TG * BPT
    N = g.tiles // TG
    NH, HD = 8, 16
    HP = NH // 2
    VW = HD + 1
    T, B = range(TG), range(NB)
    VALUES = 3
    CB = VALUES + 1
    with Arena(nc, "ml") as a:
        wg = g.c["ml_wg"]
        wgc = a.sb("wgc", [D, 40])
        gate_b = g.c["ml_gate_b"]
        lns = g.c["ml_scale"]
        m_h2 = g.c["ml_m_h2"]
        m_pair = g.c["ml_m_pair"]
        keep = g.c["ml_keep"]
        restart = g.c["ml_restart"]
        m_par = g.c["ml_m_par"]
        m_hp = g.c["ml_m_hp"]
        causal = a.sb("causal", [P, SEQ], bf16)
        causal32 = g.c["ml_causal"]
        ident16 = a.sb("ident16", [P, P], bf16)
        xvar = a.sb("xvar", [P, 3, g.tiles])
        xr = a.sb("xr", [P, 2, g.tiles])
        q_tok = a.sb("q_tok", [P, TG, D])
        qT = a.sb("qT", [D, TOK])
        kT = a.sb("kT", [D, TOK])
        cx = a.sb("cx", [P, NB, D])
        qG = a.sb("qG", [D, 2, HP, TOK])
        kE = a.sb("kE", [D, 2, NB, 2, SEQ])
        vB = a.sb("vB", [P, 2, NB, HP, 2, VW])
        argL = a.sb("argL", [40, 2, NB, 2, SEQ])
        argR = a.sb("argR", [40, 2, NB, HP, SEQ])
        fl = a.sb("fl", [P, 2, TG, NH])
        h = a.sb("h", [P, 2, TG, D])
        st = a.sb("st", [P, 2, TG, 6])
        f_abs = a.sb("f_abs", [NH, TOK])
        f_min = a.sb("f_min", [NH, TOK])
        cs = a.sb("cs", [NH, TOK])
        gg = a.sb("gg", [NH, TOK])
        cm = a.sb("cm", [NH, TOK])
        floor = a.sb("floor", [NH, TOK])
        dE = a.sb("dE", [P, CB, HP, SEQ])
        cT = a.sb("cT", [P, CB, HP, SEQ])
        den = a.sb("den", [P, TG, NH])
        mom = a.sb("mom", [P, 3, TG])
        hr = a.sb("hr", [P, 2, TG])
        hn = a.sb("hn", [P, TG, D])
        row_ps = [a.ps(f"row{n}", [P, 512]) for n in range(CB)]
        f_ps = [a.ps(f"f{n}", [P, 512]) for n in range(2)]
        qT_ps, kT_ps = f_ps
        gate_ps = qT_ps
        fl_ps = kT_ps[:, 0:TG * NH].rearrange("p (t h) -> p t h", t=TG)
        out_ps = [a.ps(f"out{n}", [P, 512])[:, 0:NH * VW] for n in range(2)]
        s_ps = [b[:, 0:HP * SEQ].rearrange("p (h s) -> p h s", h=HP) for b in row_ps]
        e_ps = [b[:, HP * SEQ:2 * HP * SEQ].rearrange("p (h s) -> p h s", h=HP) for b in row_ps]

        consts = a.sem("consts")
        cx_in = a.sem("cx_in")
        setup = a.sem("setup")
        casts_done = a.sem("casts_done")
        pool_mark = a.sem("pool_mark")
        sp_mark = a.sem("sp_mark")
        pe_mark = a.sem("pe_mark")
        moments_step = a.sem("moments_step")
        xr_done = a.sem("xr_done")
        q_done = a.sem("q_done")
        qT_in_ps = a.sem("qT_in_ps")
        kT_in_ps = a.sem("kT_in_ps")
        qT_done = a.sem("qT_done")
        qG_done = a.sem("qG_done")
        kT_done = a.sem("kT_done")
        kE_done = a.sem("kE_done")
        vB_done = a.sem("vB_done")
        gates_ready = a.sem("gates_ready")
        f_step = a.sem("f_step")
        gate_step = a.sem("gate_step")
        arg_done = a.sem("arg_done")
        scores_ready = a.sem("scores_ready")
        exps_done = a.sem("exps_done")
        c_done = a.sem("c_done")
        fl_ready = a.sem("fl_ready")
        pv_done = a.sem("pv_done")
        fl_done = a.sem("fl_done")
        den_step = a.sem("den_step")
        h_done = a.sem("h_done")
        bn_done = a.sem("bn_done")
        hmom_step = a.sem("hmom_step")
        hr_done = a.sem("hr_done")
        hn_done = a.sem("hn_done")
        hs_done = a.sem("hs_done")
        x_new = a.sem("x_new")
        st_done = a.sem("st_done")
        blk = a.ctx.enter_context(nc.Block())
        loads = []
        for u in range(2):
            loads += [(argL[32:40, u, :, :, :], w["ml_argL"]), (argR[0:8, u, :, :, :], w["ml_argR"])]
        LOADED = 16 * len(loads)

        by_row = lambda m: m.rearrange("p (b t) -> p b t", b=NB)
        first = lambda j: isinstance(j, int) and j == 0

        def has(i, b, lag, new):
            return new if b >= lag else not first(i)

        @blk.sync
        def _(sp):
            sp.wait_ge(setup, 3)
            for dst, src in loads:
                sp.dma_start(dst, src).then_inc(consts, 16)
            for h2 in range(2):
                sp.dma_start(cx[SEQ * h2:SEQ * h2 + SEQ, :, :], ctx_rows[:, 0:NB, :]).then_inc(cx_in, 16)
            with sp.Fori(0, N - 1) as k:
                wait_apart(sp, cx_in, k * 32 + 32, sp_mark)
                wait_apart(sp, kT_in_ps, k + 1, sp_mark)
                wait_apart(sp, vB_done, k * 2 + 2, sp_mark)
                for h2 in range(2):
                    sp.dma_start(cx[SEQ * h2:SEQ * h2 + SEQ, :, :],
                                 ctx_rows[:, bass.ds(k * NB + NB, NB), :]).then_inc(cx_in, 16)
            sp.wait_ge(cx_in, 32 * N)

        @blk.gpsimd
        def _(pool):
            pool.memset(vB[:, :, :, :, :, :], 0.0).then_inc(setup, 1)
            pool.memset(argL[:, :, :, :, :], 0.0).then_inc(setup, 1)
            pool.memset(argR[:, :, :, :, :], 0.0).then_inc(setup, 1)
            pool.wait_ge(setup, 3)
            for u in range(2):
                for h2 in range(2):
                    pool.memset(vB[SEQ * h2:SEQ * h2 + SEQ, u, :, :, h2, HD:VW], 1.0).then_inc(setup, 1)
            pool.wait_ge(setup, 7)
            pool.wait_ge(consts, LOADED)

            def prepare(j, u, b):
                if b in (0, 1):
                    r = slice(SEQ * b, SEQ * b + SEQ)
                    if b == 0:
                        wait_apart(pool, cx_in, j * 32 + 32, pool_mark)
                    else:
                        wait_apart(pool, vB_done, j * 2 + 1, pool_mark)
                    pool.tensor_copy(vB[r, u, :, :, b, 0:HD],
                                     cx[r, :, :].rearrange("p b (hp two e) -> p b hp two e", two=2, e=HD)[:, :, :, b, :]
                                     ).then_inc(vB_done, 1)
                if 3 <= b < 7:
                    pool.wait_ge(vB_done, j * 2 + 2)
                    pool.wait_ge(qT_done, j + 1)
                    pool.tensor_tensor(qG[:, u, b - 3, :], qT[:, :], m_pair[:, b - 3:b - 2].to_broadcast([D, TOK]),
                                       ALU.mult).then_inc(qG_done, 1)

            def step(i, u, new, ahead):
                for b in B:
                    if ahead:
                        if b == 0 and not first(i):
                            wait_apart(pool, pv_done, i * NB, pool_mark)
                        prepare(i + 1, 1 - u, b)
                    if b == 7 and not first(i):
                        pool.wait_ge(hn_done, i * TG)
                        pool.tensor_tensor(hn[:, :, :], hn[:, :, :], lns[:, :].unsqueeze(1).to_broadcast([P, TG, D]),
                                           ALU.mult).then_inc(hs_done, 1)

            for b in B:
                prepare(0, 0, b)
            pipelined(pool, N, step)

        @blk.scalar
        def _(act):
            act.preload_act_table_set("natural_log_exp_and_others")
            act.wait_ge(moments_step, 6)
            act.activation(xr[:, 0, :], xvar[:, 1, :], ACT.Ln, bias=g.ln_eps[:, :], scale=1.0 / D).then_inc(xr_done, 1)
            act.wait_ge(xr_done, 1)
            act.activation(xr[:, 1, :], xr[:, 0, :], ACT.Exp, scale=-0.5).then_inc(xr_done, 1)
            act.wait_ge(consts, LOADED)

            def prepare(j, u, b):
                if b == 0:
                    if not first(j):
                        act.wait_ge(gates_ready, j)
                    act.wait_ge(kT_in_ps, j + 1)
                    act.activation(kT[:, :], kT_ps[:, :], ACT.Copy).then_inc(kT_done, 1)
                    for h2 in range(2):
                        act.activation(kE[:, u, :, h2, :], by_row(kT_ps[:, :]), ACT.Copy, scale=m_h2[:, h2:h2 + 1]).then_inc(kE_done, 1)
                if b == 2:
                    if not first(j):
                        act.wait_ge(qG_done, j * HP)
                    act.wait_ge(qT_in_ps, j + 1)
                    act.activation(qT[:, :], qT_ps[:, :], ACT.Copy).then_inc(qT_done, 1)
                if b == 3:
                    act.wait_ge(gates_ready, j + 1)
                    act.activation(f_abs[:, :], gate_ps[32:40, :], ACT.Abs, bias=gate_b[32:40, 1:2]).then_inc(f_step, 1)
                    act.wait_ge(f_step, j * 3 + 1)
                    act.activation(f_abs[:, :], f_abs[:, :], ACT.Exp, scale=-1.0).then_inc(f_step, 1)
                    act.wait_ge(f_step, j * 3 + 2)
                    act.activation(f_abs[:, :], f_abs[:, :], ACT.Ln, bias=1.0).then_inc(f_step, 1)
                if b == 6:
                    act.wait_ge(gate_step, j * 6 + 4)
                    for h2 in range(2):
                        act.activation(argL[0:8, u, :, h2, :], by_row(gg[:, :]), ACT.Copy,
                                       scale=m_par[:, h2:h2 + 1]).then_inc(arg_done, 1)
                if b == 6:
                    act.wait_ge(gate_step, j * 6 + 5)
                    for hp in range(HP):
                        act.activation(argR[32:40, u, :, hp, :], by_row(cm[:, :]), ACT.Copy,
                                       scale=m_hp[:, hp:hp + 1]).then_inc(arg_done, 1)

            def step(i, u, new, ahead):
                for b in B:
                    r = i * NB + b
                    if new:
                        act.wait_ge(scores_ready, r + 1)
                        act.activation(dE[:, b % CB, :, :], e_ps[b % CB], ACT.Exp).then_inc(exps_done, 1)
                    if b == 4 and not first(i):
                        act.wait_ge(hmom_step, i * 6)
                        act.activation(hr[:, 0, :], mom[:, 1, :], ACT.Ln, bias=g.ln_eps[:, :], scale=1.0 / D).then_inc(hr_done, 1)
                        act.wait_ge(hr_done, i * 2 - 1)
                        act.activation(hr[:, 1, :], hr[:, 0, :], ACT.Exp, scale=-0.5).then_inc(hr_done, 1)
                    if b == 2 and new:
                        act.wait_ge(fl_ready, i * TG + TG)
                        act.activation(fl[:, u, :, :], fl_ps, ACT.Exp, scale=-1.0).then_inc(fl_done, 1)
                    if ahead:
                        prepare(i + 1, 1 - u, b)

            for b in B:
                prepare(0, 0, b)
            pipelined(act, N, step)

        @blk.tensor
        def _(pe):
            pe.wait_ge(setup, 7)
            pe.wait_ge(casts_done, 3)
            pe.wait_ge(consts, LOADED)

            def prepare(j, u, b):
                if b == 0:
                    if not (isinstance(j, int) and j <= 1):
                        wait_apart(pe, fl_done, j - 1, pe_mark)
                    wait_apart(pe, cx_in, j * 32 + 32, pe_mark)
                    for k in B:
                        mm = pe.transpose(kT_ps[:, SEQ * k:SEQ * k + SEQ], cx[0:SEQ, k, :], g.ident[0:SEQ, 0:SEQ])
                    mm.then_inc(kT_in_ps, 1)
                if b == 1:
                    if not first(j):
                        pe.wait_ge(gate_step, j * 6)
                    for t in T:
                        pe.wait_ge(q_done, j * TG + t + 1)
                        mm = pe.transpose(qT_ps[:, P * t:P * t + P], q_tok[:, t, :], g.ident[:, :])
                    mm.then_inc(qT_in_ps, 1)
                if b == 3:
                    pe.wait_ge(qT_done, j + 1)
                    pe.matmul(gate_ps[0:40, :], wg[:, 0, :], qT[:, :], start=True, stop=False)
                    pe.wait_ge(kT_done, j + 1)
                    pe.matmul(gate_ps[0:40, :], wgc[:, :], kT[:, :], start=False, stop=True).then_inc(gates_ready, 1)

            def step(i, u, new, ahead):
                for b in B:
                    r = i * NB + b
                    if new:
                        if b == 0:
                            pe.wait_ge(qG_done, HP * i + HP)
                            pe.wait_ge(kE_done, 2 * i + 2)
                        if has(i, b, CB, new):
                            pe.wait_ge(c_done, r - CB + 1)
                        pe.matmul(s_ps[b % CB], kE[:, u, b, :, :], qG[:, u, :, SEQ * b:SEQ * b + SEQ], start=True, stop=True)
                        if b == 0:
                            pe.wait_ge(arg_done, 6 * i + 6)
                        pe.matmul(e_ps[b % CB], argL[:, u, b, :, :], argR[:, u, b, :, :], start=True, stop=False)
                        pe.matmul(e_ps[b % CB], ident16[:, :], causal[:, :].unsqueeze(1).to_broadcast([P, HP, SEQ]),
                                  start=False, stop=True).then_inc(scores_ready, 1)
                    if has(i, b, VALUES, new):
                        row, v = (b - VALUES) % NB, u if b >= VALUES else 1 - u
                        t, q = row // 2, slice(SEQ * (row % 2), SEQ * (row % 2) + SEQ)
                        pe.wait_ge(c_done, r - VALUES + 1)
                        if row % 2 == 0 and has(i, b, VALUES + 4, new or b < VALUES + 4):
                            pe.wait_ge(h_done, (r - VALUES) - 2)
                        for hp in range(HP):
                            mm = pe.matmul(out_ps[t % 2][q, 2 * VW * hp:2 * VW * hp + 2 * VW], cT[:, (b - VALUES) % CB, hp, :],
                                           vB[:, v, row, hp, :, :], start=True, stop=True)
                        mm.then_inc(pv_done, 1)
                    if b == 2 and new:
                        wait_apart(pe, gate_step, i * 6 + 6, pe_mark)
                        wait_apart(pe, kE_done, 2 * i + (4 if ahead else 2), pe_mark)
                        for t in T:
                            pe.transpose(fl_ps[:, t, :], floor[:, P * t:P * t + P], g.ident[0:NH, 0:NH]).then_inc(fl_ready, 1)
                    if ahead:
                        prepare(i + 1, 1 - u, b)

            for b in B:
                prepare(0, 0, b)
            pipelined(pe, N, step)

        @blk.vector
        def _(dve):
            ln_moments(dve, g.st, xvar, moments_step, 0)
            dve.wait_ge(consts, LOADED)
            dve.tensor_copy(causal[:, :], causal32[:, :]).then_inc(casts_done, 1)
            dve.tensor_copy(ident16[:, :], g.ident[:, :]).then_inc(casts_done, 1)
            dve.tensor_tensor(wgc[:, :], wg[:, 1, :], wg[:, 2, :], ALU.add).then_inc(casts_done, 1)
            dve.wait_ge(xr_done, 2)

            def prepare(j, u, b):
                if b == 0:
                    if not first(j):
                        dve.wait_ge(qT_in_ps, j)
                    for t in T:
                        n = j * TG + t
                        dve.tensor_scalar(q_tok[:, t, :], g.x[:, n, :], xvar[:, 0, bass.ds(n, 1)], xr[:, 1, bass.ds(n, 1)],
                                          ALU.subtract, ALU.mult).then_inc(q_done, 1)
                if b == 4:
                    dve.wait_ge(f_step, j * 3 + 1)
                    dve.tensor_scalar(f_min[:, :], gate_ps[32:40, :], gate_b[32:40, 1:2], 0.0,
                                      ALU.add, ALU.min).then_inc(gate_step, 1)
                    dve.wait_ge(f_step, j * 3 + 3)
                    dve.wait_ge(gate_step, j * 6 + 1)
                    dve.tensor_tensor(f_min[:, :], f_min[:, :], f_abs[:, :], ALU.subtract).then_inc(gate_step, 1)
                    dve.wait_ge(gate_step, j * 6 + 2)
                    dve.tensor_tensor_scan(cs[:, :], keep[:, :], f_min[:, :], 0.0, ALU.mult, ALU.add).then_inc(gate_step, 1)
                    if not first(j):
                        dve.wait_ge(arg_done, j * 6)
                    dve.wait_ge(gate_step, j * 6 + 3)
                    dve.scalar_tensor_tensor(out=gg[:, :], in0=gate_ps[0:8, :], scalar=gate_b[0:8, 0:1], in1=cs[:, :],
                                             op0=ALU.add, op1=ALU.subtract).then_inc(gate_step, 1)
                if b == 5:
                    dve.wait_ge(gate_step, j * 6 + 4)
                    dve.tensor_tensor_scan(cm[:, :], restart[:, :], gg[:, :], -1e30, ALU.add, ALU.max).then_inc(gate_step, 1)
                if b == 6:
                    if not first(j):
                        dve.wait_ge(fl_ready, j * TG)
                    dve.wait_ge(gate_step, j * 6 + 5)
                    dve.tensor_tensor(floor[:, :], cs[:, :], cm[:, :], ALU.add).then_inc(gate_step, 1)

            def normalise(i, u, t):
                n = i * TG + t
                k = n * 3
                o = out_ps[t % 2].rearrange("p (h v) -> p h v", v=VW)
                dve.wait_ge(pv_done, n * 2 + 2)
                dve.wait_ge(fl_done, i + 1)
                dve.scalar_tensor_tensor(out=den[:, t, :], in0=o[:, :, HD], scalar=-1.0, in1=fl[:, u, t, :],
                                         op0=ALU.mult, op1=ALU.max).then_inc(den_step, 1)
                dve.wait_ge(den_step, k + 1)
                dve.tensor_tensor(den[:, t, :], o[:, :, HD], den[:, t, :], ALU.max).then_inc(den_step, 1)
                dve.wait_ge(den_step, k + 2)
                dve.tensor_scalar(den[:, t, :], den[:, t, :], 1e-6, None, ALU.add).then_inc(den_step, 1)
                dve.wait_ge(den_step, k + 3)
                dve.reciprocal(den[:, t, :], den[:, t, :]).then_inc(h_done, 1)
                dve.wait_ge(h_done, n * 2 + 1)
                dve.tensor_tensor(h[:, u, t, :].rearrange("p (h e) -> p h e", h=NH), o[:, :, 0:HD],
                                  den[:, t, :].unsqueeze(2).to_broadcast([P, NH, HD]), ALU.mult).then_inc(h_done, 1)
                dve.wait_ge(h_done, n * 2 + 2)
                dve.wait_ge(consts, 16)
                dve.bn_stats(st[:, u, t, :], h[:, u, t, :]).then_inc(bn_done, 1)

            def step(i, u, new, ahead):
                for b in B:
                    r = i * NB + b
                    if new:
                        dve.wait_ge(exps_done, r + 1)
                        if has(i, b, CB, new):
                            dve.wait_ge(pv_done, r - CB + 1)
                        dve.tensor_tensor(cT[:, b % CB, :, :], s_ps[b % CB], dE[:, b % CB, :, :], ALU.mult).then_inc(c_done, 1)
                    if b == 4 and not first(i):
                        dve.wait_ge(bn_done, i * TG)
                        ln_moments(dve, st[:, 1 - u, :, :], mom, hmom_step, (i - 1) * 6)
                    if ahead:
                        prepare(i + 1, 1 - u, b)
                    if b % 2 and has(i, b, VALUES + 2, new):
                        t = (b - VALUES - 2) // 2
                        normalise(i if t >= 0 else i - 1, u if t >= 0 else 1 - u, t % TG)
                    if not first(i):
                        if b == 5:
                            dve.wait_ge(hr_done, i * 2)
                            for t in T:
                                dve.tensor_scalar(hn[:, t, :], h[:, 1 - u, t, :], mom[:, 0, t:t + 1], hr[:, 1, t:t + 1],
                                                  ALU.subtract, ALU.mult).then_inc(hn_done, 1)
                        if b == 7:
                            rows = g.x[:, bass.ds(i * TG - TG, TG), :]
                            dve.wait_ge(hs_done, i)
                            dve.tensor_tensor(rows, rows, hn[:, :, :], ALU.add).then_inc(x_new, 1)
                        if b == 7:
                            dve.wait_ge(x_new, i)
                            for t in T:
                                n = i * TG - TG + t
                                dve.wait_ge(consts, 16)
                                dve.bn_stats(g.st[:, n, :], g.x[:, n, :]).then_inc(st_done, 1)

            for b in B:
                prepare(0, 0, b)
            pipelined(dve, N, step)
            dve.wait_ge(st_done, g.tiles)


def normed_transposed(nc, g, w, name, hidden):
    TG, N, TOK = STREAMS, g.tiles // STREAMS, STREAMS * P
    E = 20 if hidden else 8
    F = 32
    T = range(TG)
    with Arena(nc, name) as a:
        wgate, first = g.c[name + "_gate"], g.c[name + "_first"]
        if hidden:
            wg1, bg1, bg2 = g.c[name + "_wg1"], g.c[name + "_bg1"], g.c[name + "_bg2"]
        xvar = a.sb("xvar", [P, 3, g.tiles])
        xr = a.sb("xr", [P, 2, g.tiles])
        xn = a.sb("xn", [P, 2, TG, D])
        xT = a.sb("xT", [D, 2, TOK])
        hT = a.sb("hT", [F, 2, TOK])
        lg = a.sb("lg", [P, g.tiles, E])
        top = a.sb("top", [P, 2, g.tiles])
        eq = a.sb("eq", [P, g.tiles, E])
        pre = a.sb("pre", [P, g.tiles, E])
        pick = a.sb("pick", [P, 2, g.tiles, E])
        ex = a.sb("ex", [P, g.tiles, E])
        tr_ps = [a.ps(f"tr{u}", [P, 512]) for u in range(2)]
        h_ps = [a.ps(f"h{u}", [F, 512]) for u in range(2)]
        lg_ps = [a.ps(f"lg{u}", [P, 512])[:, 0:TG * E].rearrange("p (t e) -> p t e", t=TG) for u in range(2)]
        moments_step = a.sem("moments_step")
        xr_done = a.sem("xr_done")
        xn_done = a.sem("xn_done")
        tr_ready = a.sem("tr_ready")
        xT_done = a.sem("xT_done")
        kept = a.sem("kept")
        h_ready = a.sem("h_ready")
        h_done = a.sem("h_done")
        lg_ready = a.sem("lg_ready")
        lg_done = a.sem("lg_done")
        top_step = a.sem("top_step")
        ex_done = a.sem("ex_done")
        pool_mark = a.sem("pool_mark")
        blk = a.ctx.enter_context(nc.Block())
        last = g.tiles
        first_step = lambda i: isinstance(i, int) and i == 0

        @blk.scalar
        def _(act):
            act.preload_act_table_set("natural_log_exp_and_others")
            act.wait_ge(moments_step, 6)
            act.activation(xr[:, 0, :], xvar[:, 1, :], ACT.Ln, bias=g.ln_eps[:, :], scale=1.0 / D).then_inc(xr_done, 1)
            act.wait_ge(xr_done, 1)
            act.activation(xr[:, 1, :], xr[:, 0, :], ACT.Exp, scale=-0.5).then_inc(xr_done, 1)
            if hidden:
                act.preload_act_table(ACT.Gelu)

            def step(i, u, new, ahead):
                if hidden and not first_step(i):
                    act.wait_ge(h_ready, i)
                    act.activation(hT[:, 1 - u, :], h_ps[1 - u][:, :], ACT.Gelu, bias=bg1[:, :]).then_inc(h_done, 1)
                if new:
                    act.wait_ge(tr_ready, i + 1)
                    if not first_step(i):
                        act.wait_ge(kept, i)
                    act.activation(xT[:, u, :], tr_ps[u][:, :], ACT.Copy).then_inc(xT_done, 1)

            pipelined(act, N, step)
            act.preload_act_table_set("natural_log_exp_and_others")
            act.wait_ge(ex_done, 1)
            act.activation(ex[:, :, :], ex[:, :, :], ACT.Exp).then_inc(ex_done, 1)

        @blk.gpsimd
        def _(pool):
            pool.sem_inc(kept, 1)

            def step(i, u, new, ahead):
                if new:
                    wait_apart(pool, xT_done, i + 1, pool_mark)
                    pool.tensor_copy(g.xT[:, bass.ds(i * TOK, TOK)], xT[:, u, :]).then_inc(kept, 1)

            pipelined(pool, N, step)

        @blk.tensor
        def _(pe):

            def logits(i, u):
                if hidden:
                    pe.wait_ge(h_done, i + 1)
                for t in T:
                    mm = pe.matmul(lg_ps[u][:, t, :], (hT if hidden else xT)[:, u, P * t:P * t + P], wgate[:, :],
                                   start=True, stop=True)
                mm.then_inc(lg_ready, 1)

            def step(i, u, new, ahead):
                before = not first_step(i)
                if before:
                    pe.wait_ge(xT_done, i)
                    if hidden:
                        pe.matmul(h_ps[1 - u][:, :], wg1[:, :], xT[:, 1 - u, :], start=True, stop=True).then_inc(h_ready, 1)
                    else:
                        logits(i - 1, 1 - u)
                if new:
                    for t in T:
                        pe.wait_ge(xn_done, i * TG + t + 1)
                        mm = pe.transpose(tr_ps[u][:, P * t:P * t + P], xn[:, u, t, :], g.ident[:, :])
                    mm.then_inc(tr_ready, 1)
                if before and hidden:
                    logits(i - 1, 1 - u)

            pipelined(pe, N, step)

        @blk.vector
        def _(dve):
            ln_moments(dve, g.st, xvar, moments_step, 0)
            dve.wait_ge(xr_done, 2)

            def step(i, u, new, ahead):
                for t in T if new else ():
                    n = i * TG + t
                    dve.tensor_scalar(xn[:, u, t, :], g.x[:, n, :], xvar[:, 0, bass.ds(n, 1)], xr[:, 1, bass.ds(n, 1)],
                                      ALU.subtract, ALU.mult).then_inc(xn_done, 1)
                if not first_step(i):
                    dst = lg[:, bass.ds(i * TG - TG, TG), :]
                    dve.wait_ge(lg_ready, i)
                    if hidden:
                        dve.tensor_tensor(dst, lg_ps[1 - u], bg2[:, :].unsqueeze(1).to_broadcast([P, TG, E]), ALU.add).then_inc(lg_done, 1)
                    else:
                        dve.tensor_copy(dst, lg_ps[1 - u]).then_inc(lg_done, 1)

            pipelined(dve, N, step)
            dve.wait_ge(lg_done, N)

            def over_experts(m):
                return m.unsqueeze(2).to_broadcast([P, last, E])

            flat = lambda m: m.rearrange("p t e -> p (t e)")
            step = 0
            src = lg
            for k in range(2):
                dve.tensor_reduce(top[:, k, :], src[:, :, :], AX.X, ALU.max).then_inc(top_step, 1)
                dve.wait_ge(top_step, step + 1)
                dve.tensor_tensor(eq[:, :, :], src[:, :, :], over_experts(top[:, k, :]), ALU.is_equal).then_inc(top_step, 1)
                dve.wait_ge(top_step, step + 2)
                dve.tensor_tensor_scan(flat(pre[:, :, :]), flat(first[:, 0:last, :]), flat(eq[:, :, :]), 0.0,
                                       ALU.mult, ALU.add).then_inc(top_step, 1)
                dve.wait_ge(top_step, step + 3)
                dve.scalar_tensor_tensor(out=pick[:, k, :, :], in0=pre[:, :, :], scalar=1.0, in1=eq[:, :, :],
                                         op0=ALU.is_equal, op1=ALU.mult).then_inc(top_step, 1)
                dve.wait_ge(top_step, step + 4)
                step += 4
                if k == 0:
                    dve.scalar_tensor_tensor(out=ex[:, :, :], in0=pick[:, 0, :, :], scalar=-3e38, in1=lg[:, :, :],
                                             op0=ALU.mult, op1=ALU.add).then_inc(top_step, 1)
                    dve.wait_ge(top_step, step + 1)
                    step += 1
                    src = ex
            dve.tensor_tensor(pick[:, 0, :, :], pick[:, 0, :, :], pick[:, 1, :, :], ALU.add).then_inc(top_step, 1)
            dve.tensor_tensor(ex[:, :, :], lg[:, :, :], over_experts(top[:, 0, :]), ALU.subtract).then_inc(ex_done, 1)
            dve.wait_ge(ex_done, 2)
            dve.tensor_reduce(top[:, 1, :], ex[:, :, :], AX.X, ALU.add).then_inc(top_step, 1)
            dve.wait_ge(top_step, step + 2)
            dve.reciprocal(top[:, 1, :], top[:, 1, :]).then_inc(top_step, 1)
            dve.tensor_tensor(pick[:, 0, :, :], pick[:, 0, :, :], ex[:, :, :], ALU.mult).then_inc(top_step, 1)
            dve.wait_ge(top_step, step + 4)
            dve.tensor_tensor(g.rw[:, 0:last, 0:E], pick[:, 0, :, :], over_experts(top[:, 1, :]), ALU.mult).then_inc(top_step, 1)
            dve.wait_ge(top_step, step + 5)


def silu_experts(nc, g, w):
    TG, N, TOK = STREAMS, g.tiles // STREAMS, STREAMS * P
    E, UNITS = 8, 8
    PARTS = [slice(32 * k, 32 * k + E + 1) for k in range(3)]
    PARTS_END = PARTS[2].stop
    T = range(TG)
    with Arena(nc, "se") as a:
        w1, w2, sel32 = g.c["se_w1"], g.c["se_w2"], g.c["se_sel"]
        sel = a.sb("sel", [PARTS_END, UNITS, P], bf16)
        rwx = a.sb("rwx", [P, TG, E + 1])
        rw = a.sb("rw", [PARTS_END, 2, TOK], bf16)
        rest = a.sb("rest", [E + 1, TOK])
        act_g = a.sb("act_g", [P, 2, TOK])
        hid = a.sb("hid", [P, 2, TOK])
        hw = a.sb("hw", [P, 2, TOK])
        yT = a.sb("yT", [D, TOK])
        y_ps = [a.ps(f"y{u}", [P, 512]) for u in range(2)]
        g_ps = [a.ps(f"g{u}", [P, 512]) for u in range(2)]
        b_ps = [a.ps(f"b{u}", [P, 512]) for u in range(2)]
        out_ps = a.ps("out", [P, 512])
        tr_ps = a.ps("tr", [P, 512])
        rwx_done = a.sem("rwx_done")
        casts_done = a.sem("casts_done")
        rwT_ready = a.sem("rwT_ready")
        rw_part = a.sem("rw_part")
        cleared = a.sem("cleared")
        up_ready = a.sem("up_ready")
        b_ready = a.sem("b_ready")
        silu_done = a.sem("silu_done")
        hid_done = a.sem("hid_done")
        hw_done = a.sem("hw_done")
        down_ready = a.sem("down_ready")
        yT_done = a.sem("yT_done")
        y_ready = a.sem("y_ready")
        x_new = a.sem("x_new")
        st_done = a.sem("st_done")
        blk = a.ctx.enter_context(nc.Block())
        first = lambda j: isinstance(j, int) and j == 0

        def has(i, s, lag, new):
            return new if s >= lag else not first(i)

        @blk.gpsimd
        def _(pool):
            pool.memset(rwx[:, :, :], 1.0).then_inc(casts_done, 1)
            pool.memset(rw[:, :, :], 0.0).then_inc(cleared, 1)
            pool.memset(sel[:, :, :], 0.0).then_inc(cleared, 1)

        @blk.scalar
        def _(act):
            act.preload_act_table(ACT.Silu)
            act.wait_ge(cleared, 2)

            def prepare(j, u, s):
                if s == 5:
                    act.wait_ge(rwT_ready, j + 1)
                    act.activation(rw[PARTS[0], u, :], tr_ps[0:E + 1, :], ACT.Copy).then_inc(rw_part, 1)
                if s == 6:
                    act.wait_ge(rw_part, j * 4 + 2)
                    act.activation(rw[PARTS[1], u, :], rest[:, :], ACT.Copy).then_inc(rw_part, 1)

            def step(i, u, new, ahead):
                for s in range(UNITS):
                    n = i * UNITS + s
                    if new:
                        act.wait_ge(up_ready, n + 1)
                        if has(i, s, 2, new):
                            act.wait_ge(hid_done, n - 1)
                        act.activation(act_g[:, s % 2, :], g_ps[s % 2][:, :], ACT.Silu).then_inc(silu_done, 1)
                    if s == 0 and not first(i):
                        act.wait_ge(down_ready, i)
                        act.activation(yT[:, :], out_ps[:, :], ACT.Copy).then_inc(yT_done, 1)
                    if ahead:
                        prepare(i + 1, 1 - u, s)

            for s in range(UNITS):
                prepare(0, 0, s)
            pipelined(act, N, step)

        @blk.tensor
        def _(pe):
            pe.wait_ge(casts_done, 4)

            def prepare(j, u, s):
                if s == 5:
                    pe.wait_ge(rwx_done, j + 1)
                    if not (isinstance(j, int) and j <= 1):
                        pe.wait_ge(x_new, j - 1)
                    for t in T:
                        mm = pe.transpose(tr_ps[0:E + 1, P * t:P * t + P], rwx[:, t, :], g.ident[:, :])
                    mm.then_inc(rwT_ready, 1)

            def step(i, u, new, ahead):
                for s in range(UNITS):
                    n = i * UNITS + s
                    if new:
                        if has(i, s, 2, new):
                            pe.wait_ge(hid_done, n - 1)
                        for k, bank in ((0, y_ps), (1, g_ps)):
                            mm = pe.matmul(bank[s % 2][:, :], w1[:, k, s, :], g.xT[:, bass.ds(i * TOK, TOK)], start=True, stop=True)
                        mm.then_inc(up_ready, 1)
                        if s == 0:
                            pe.wait_ge(rw_part, i * 4 + 4)
                        if has(i, s, 2, new):
                            pe.wait_ge(hw_done, n - 1)
                        pe.matmul(b_ps[s % 2][:, :], sel[:, s, :], rw[:, u, :], start=True, stop=True).then_inc(b_ready, 1)
                    if has(i, s, 1, new):
                        part = (s - 1) % UNITS
                        pe.wait_ge(hw_done, n)
                        if part == 0 and not first(i):
                            pe.wait_ge(yT_done, i)
                        mm = pe.matmul(out_ps[:, :], w2[:, part, :], hw[:, (s - 1) % 2, :], start=(part == 0),
                                       stop=(part == UNITS - 1))
                        if part == UNITS - 1:
                            mm.then_inc(down_ready, 1)
                    if s == 2 and not first(i):
                        pe.wait_ge(yT_done, i)
                        if ahead or new:
                            pe.wait_ge(rw_part, i * 4 + 4)
                        for t in T:
                            mm = pe.transpose(tr_ps[:, P * t:P * t + P], yT[:, P * t:P * t + P], g.ident[:, :])
                        mm.then_inc(y_ready, 1)
                    if ahead:
                        prepare(i + 1, 1 - u, s)

            for s in range(UNITS):
                prepare(0, 0, s)
            pipelined(pe, N, step)

        @blk.vector
        def _(dve):
            dve.wait_ge(cleared, 2)
            for rows in PARTS:
                dve.tensor_copy(sel[rows, :, :], sel32[:, :, :]).then_inc(casts_done, 1)
            dve.wait_ge(casts_done, 4)

            def prepare(j, u, s):
                if s == 4:
                    if not first(j):
                        dve.wait_ge(rwT_ready, j)
                    dve.tensor_copy(rwx[:, :, 0:E], g.rw[:, bass.ds(j * TG, TG), 0:E]).then_inc(rwx_done, 1)
                if s == 5:
                    dve.wait_ge(rw_part, j * 4 + 1)
                    dve.tensor_tensor(rest[:, :], tr_ps[0:E + 1, :], rw[PARTS[0], u, :], ALU.subtract).then_inc(rw_part, 1)
                if s == 6:
                    dve.wait_ge(rw_part, j * 4 + 3)
                    dve.tensor_tensor(rw[PARTS[2], u, :], rest[:, :], rw[PARTS[1], u, :], ALU.subtract).then_inc(rw_part, 1)

            def step(i, u, new, ahead):
                for s in range(UNITS):
                    n = i * UNITS + s
                    if new:
                        dve.wait_ge(silu_done, n + 1)
                        dve.tensor_tensor(hid[:, s % 2, :], y_ps[s % 2][:, :], act_g[:, s % 2, :], ALU.mult).then_inc(hid_done, 1)
                        dve.wait_ge(hid_done, n + 1)
                        dve.wait_ge(b_ready, n + 1)
                        dve.tensor_tensor(hw[:, s % 2, :], b_ps[s % 2][:, :], hid[:, s % 2, :], ALU.mult).then_inc(hw_done, 1)
                    if s == 3 and not first(i):
                        xs = g.x[:, bass.ds(i * TG - TG, TG), :]
                        dve.wait_ge(y_ready, i)
                        dve.tensor_tensor(xs, tr_ps[:, :].rearrange("p (t d) -> p t d", t=TG), xs, ALU.add).then_inc(x_new, 1)
                        dve.wait_ge(x_new, i)
                        for t in T:
                            m = i * TG - TG + t
                            dve.bn_stats(g.st[:, m, :], g.x[:, m, :]).then_inc(st_done, 1)
                    if ahead:
                        prepare(i + 1, 1 - u, s)

            for s in range(UNITS):
                prepare(0, 0, s)
            pipelined(dve, N, step)
            dve.wait_ge(st_done, g.tiles)


def linear_experts(nc, g, w, out_dram):
    TG, N, TOK = STREAMS, g.tiles // STREAMS, STREAMS * P
    E, C = 20, 4
    CH = E // C
    T = range(TG)
    BY_ACT, BY_DVE = (1, 3), (0, 2, 4)
    with Arena(nc, "le") as a:
        we, be = g.c["le_we"], g.c["le_be"]
        rws = a.sb("rws", [P, 2, TG, E])
        rwT = a.sb("rwT", [E, 2, TOK])
        xTs = a.sb("xTs", [D, 2, TOK])
        prod = a.sb("prod", [P, 2, CH, C * D])
        acc = a.sb("acc", [P, 2, C * D])
        part = a.sb("part", [P, 2, 2 * D])
        e_ps = [a.ps(f"e{k}", [P, 512]) for k in range(CH)]
        tr_ps = a.ps("tr", [E, 512])
        b_ps = [a.ps(f"b{k}", [P, 512]) for k in range(2)]
        xTs_done = a.sem("xTs_done")
        rws_done = a.sem("rws_done")
        rwT_ready = a.sem("rwT_ready")
        rwT_done = a.sem("rwT_done")
        e_ready = a.sem("e_ready")
        b_ready = a.sem("b_ready")
        act_prod = a.sem("act_prod")
        dve_prod = a.sem("dve_prod")
        pair_done = a.sem("pair_done")
        acc_done = a.sem("acc_done")
        fold_done = a.sem("fold_done")
        part_done = a.sem("part_done")
        x_new = a.sem("x_new")
        stored = a.sem("stored")
        sp_mark = a.sem("sp_mark")
        blk = a.ctx.enter_context(nc.Block())

        def at_least(n, lag):
            return not isinstance(n, int) or n >= lag

        @blk.sync
        def _(sp):
            with sp.Fori(0, N) as i:
                wait_apart(sp, x_new, i * TG + TG, sp_mark)
                sp.dma_start(out_dram[:, bass.ds(i * TG, TG), :], g.x[:, bass.ds(i * TG, TG), :]).then_inc(stored, 16)
            sp.wait_ge(stored, 16 * N)

        @blk.scalar
        def _(act):
            act.preload_act_table_set("natural_log_exp_and_others")

            def prepare(j, u, t):
                if t == 0:
                    act.activation(xTs[:, u, :], g.xT[:, bass.ds(j * TOK, TOK)], ACT.Copy).then_inc(xTs_done, 1)
                if t == 2:
                    act.wait_ge(rwT_ready, j + 1)
                    act.activation(rwT[:, u, :], tr_ps[:, :], ACT.Copy).then_inc(rwT_done, 1)

            def step(i, u, new, ahead):
                for t in T:
                    n = i * TG + t
                    if new:
                        for c in BY_ACT:
                            act.wait_ge(e_ready, n * CH + c + 1)
                            if c == BY_ACT[0] and at_least(n, 2):
                                act.wait_ge(acc_done, (n - 1) * 3)
                            for e in range(C):
                                s = slice(D * e, D * e + D)
                                op = act.activation(prod[:, t % 2, c, s], e_ps[c][:, s], ACT.Copy,
                                                    scale=rws[:, u, t, C * c + e:C * c + e + 1])
                            op.then_inc(act_prod, 1)
                    if ahead:
                        prepare(i + 1, 1 - u, t)

            for t in T:
                prepare(0, 0, t)
            act.wait_ge(rws_done, 1)
            pipelined(act, N, step)

        @blk.tensor
        def _(pe):

            def prepare(j, u, t):
                if t == 1:
                    pe.wait_ge(rws_done, j + 1)
                    for k in T:
                        mm = pe.transpose(tr_ps[:, P * k:P * k + P], rws[:, u, k, :], g.ident[:, :])
                    mm.then_inc(rwT_ready, 1)

            def step(i, u, new, ahead):
                for t in T if new else ():
                    n = i * TG + t
                    s = slice(P * t, P * t + P)
                    for c in range(CH):
                        if c == 0 and t == 0:
                            pe.wait_ge(xTs_done, i + 1)
                        if at_least(n, 1):
                            if c in BY_ACT:
                                pe.wait_ge(act_prod, (n - 1) * 2 + BY_ACT.index(c) + 1)
                            else:
                                pe.wait_ge(dve_prod, (n - 1) * 3 + BY_DVE.index(c) + 1)
                        pe.matmul(e_ps[c][:, :], xTs[:, u, s], we[:, c, :], start=True, stop=True).then_inc(e_ready, 1)
                    if t == 0:
                        pe.wait_ge(rwT_done, i + 1)
                    if at_least(n, 2):
                        pe.wait_ge(part_done, n - 1)
                    pe.matmul(b_ps[t % 2][:, 0:D], rwT[:, u, s], be[:, :], start=True, stop=True).then_inc(b_ready, 1)
                    if ahead:
                        prepare(i + 1, 1 - u, t)

            for t in T:
                prepare(0, 0, t)
            pipelined(pe, N, step)

        @blk.gpsimd
        def _(pool):
            def step(i, u, new, ahead):
                for t in T if new else ():
                    n = i * TG + t
                    p, sum_ = prod[:, t % 2, :, :], acc[:, t % 2, :]
                    if at_least(n, 2):
                        pool.wait_ge(fold_done, (n - 1) * 2)
                    pool.wait_ge(dve_prod, n * 3 + 1)
                    pool.wait_ge(act_prod, n * 2 + 1)
                    pool.tensor_tensor(sum_, p[:, 0, :], p[:, 1, :], ALU.add).then_inc(acc_done, 1)
                    pool.wait_ge(acc_done, n * 3 + 1)
                    pool.wait_ge(dve_prod, n * 3 + 2)
                    pool.tensor_tensor(sum_, sum_, p[:, 2, :], ALU.add).then_inc(acc_done, 1)
                    pool.wait_ge(acc_done, n * 3 + 2)
                    pool.wait_ge(pair_done, n + 1)
                    pool.tensor_tensor(sum_, sum_, p[:, 4, :], ALU.add).then_inc(acc_done, 1)

            pipelined(pool, N, step)

        @blk.vector
        def _(dve):
            def prepare(j, u, t):
                if t == 0:
                    dve.tensor_copy(rws[:, u, :, :], g.rw[:, bass.ds(j * TG, TG), 0:E]).then_inc(rws_done, 1)

            def step(i, u, new, ahead):
                for t in T:
                    n = i * TG + t
                    last = (new or t == 0) and at_least(n, 1)
                    q, sum_ = part[:, (t - 1) % 2, :], acc[:, (t - 1) % 2, :]

                    def weighted(k):
                        c = BY_DVE[k]
                        dve.wait_ge(e_ready, n * CH + c + 1)
                        dve.tensor_tensor(prod[:, t % 2, c, :].rearrange("p (e d) -> p e d", e=C),
                                          e_ps[c][:, :].rearrange("p (e d) -> p e d", e=C),
                                          rws[:, u, t, C * c:C * c + C].unsqueeze(2).to_broadcast([P, C, D]),
                                          ALU.mult).then_inc(dve_prod, 1)

                    if new:
                        if at_least(n, 2):
                            dve.wait_ge(acc_done, (n - 1) * 3)
                        weighted(0)
                        weighted(1)
                    if last:
                        dve.wait_ge(acc_done, n * 3)
                        dve.tensor_tensor(q, sum_[:, 0:2 * D], sum_[:, 2 * D:4 * D], ALU.add).then_inc(fold_done, 1)
                    if new:
                        weighted(2)
                    if last:
                        dve.wait_ge(fold_done, n * 2 - 1)
                        dve.tensor_tensor(q[:, 0:D], q[:, 0:D], q[:, D:2 * D], ALU.add).then_inc(fold_done, 1)
                    if new:
                        dve.wait_ge(act_prod, n * 2 + 2)
                        dve.wait_ge(dve_prod, n * 3 + 3)
                        dve.tensor_tensor(prod[:, t % 2, 4, :], prod[:, t % 2, 3, :], prod[:, t % 2, 4, :], ALU.add).then_inc(pair_done, 1)
                    if last:
                        dve.wait_ge(fold_done, n * 2)
                        dve.wait_ge(b_ready, n)
                        dve.tensor_tensor(q[:, 0:D], b_ps[(t - 1) % 2][:, 0:D], q[:, 0:D], ALU.add).then_inc(part_done, 1)
                        if ahead:
                            prepare(i + 1, 1 - u, t)
                        dve.wait_ge(part_done, n)
                        dve.tensor_tensor(g.x[:, n - 1, :], g.x[:, n - 1, :], q[:, 0:D], ALU.add).then_inc(x_new, 1)
                    elif ahead:
                        prepare(i + 1, 1 - u, t)

            for t in T:
                prepare(0, 0, t)
            pipelined(dve, N, step)


def softmax_attention(nc, g, w, name, ctx_dram):
    causal = ctx_dram is None
    TG, N, TOK = STREAMS, g.tiles // STREAMS, STREAMS * P
    NB = TG * BPT
    G, M, HD = 4, 4, 8
    H = 2 * M
    SCALE = 1.0 / HD ** 0.5
    T, B = range(TG), range(NB)
    TRANSPOSE, VALUES = 3, 4
    PB = 4
    with Arena(nc, name) as a:
        NQ = 4 if causal else 2
        wqk, wv, wo, bo = (g.c[name + k] for k in ("_wqk", "_wv", "_wo", "_bo"))
        cols = g.c[name + "_cols"]
        m_group, m_member = cols[:, 8:12], cols[:, 12:16]
        rope, cm32 = g.c["at_rope"], g.c["at_causal"]
        cm = a.sb("cm", [P, SEQ], bf16)
        ident16 = a.sb("ident16", [P, P], bf16)
        bvb = a.sb("bvb", [D, P])
        ybias = a.sb("ybias", [P, D])
        xvar = a.sb("xvar", [P, 3, g.tiles])
        xr = a.sb("xr", [P, 5, g.tiles])
        z = a.sb("z", [P, TG, D])
        an = a.sb("an", [P, TG, D])
        aT = a.sb("aT", [D, TOK])
        kv_in = a.sb("kv_in", [P, TG, D])
        cT = aT if causal else a.sb("cT", [D, TOK])
        ra = a.sb("ra", [D, 2, TOK])
        rb = a.sb("rb", [D, 2, TOK])
        qg = a.sb("qg", [D, 2, NB, G, SEQ])
        km = a.sb("km", [D, 2, NB, M, SEQ])
        vB = a.sb("vB", [P, 2, NB, 2, D])
        nm = a.sb("nm", [P, PB, H])
        rden = a.sb("rden", [P, PB, H])
        prob = a.sb("prob", [P, PB, H, SEQ])
        pT = a.sb("pT", [P, 2, TOK])
        atT = a.sb("atT", [D, TOK])
        s_ps = [a.ps(f"s{n}", [P, 512]) for n in range(2)]
        pT_ps = [a.ps(f"pT{n}", [P, 512]) for n in range(2)]
        at_ps = a.ps("at", [P, 512])
        f_ps = [a.ps(f"f{n}", [P, 512]) for n in range(3)]
        aT_ps, cT_ps, y_ps = f_ps[0], f_ps[1], f_ps[2]
        qk_ps = [f_ps[2], f_ps[0], f_ps[1], f_ps[2]]
        v_ps = f_ps[0]

        casts_done = a.sem("casts_done")
        cleared = a.sem("cleared")
        moments_step = a.sem("moments_step")
        ln_step = a.sem("ln_step")
        rr_done = a.sem("rr_done")
        bias_ready = a.sem("bias_ready")
        ybias_done = a.sem("ybias_done")
        kv_loaded = a.sem("kv_loaded")
        an_done = a.sem("an_done")
        z_done = a.sem("z_done")
        aT_ready = a.sem("aT_ready")
        cT_ready = a.sem("cT_ready")
        aT_done = a.sem("aT_done")
        cT_done = a.sem("cT_done")
        qk_ready = a.sem("qk_ready")
        qk_left = a.sem("qk_left")
        rope_done = a.sem("rope_done")
        v_ready = a.sem("v_ready")
        qg_done = a.sem("qg_done")
        km_done = a.sem("km_done")
        vB_done = a.sem("vB_done")
        base_done = a.sem("base_done")
        s_ready = a.sem("s_ready")
        nm_done = a.sem("nm_done")
        sub_done = a.sem("sub_done")
        exp_done = a.sem("exp_done")
        sum_done = a.sem("sum_done")
        rden_done = a.sem("rden_done")
        prob_done = a.sem("prob_done")
        pT_ready = a.sem("pT_ready")
        pT_done = a.sem("pT_done")
        pv_done = a.sem("pv_done")
        atT_done = a.sem("atT_done")
        y_ready = a.sem("y_ready")
        x_new = a.sem("x_new")
        st_done = a.sem("st_done")
        mark = a.sem("mark")
        blk = a.ctx.enter_context(nc.Block())
        by_row = lambda m: m.rearrange("p (b s) -> p b s", b=NB)
        step_rows = lambda i: g.x[:, bass.ds(i * TG, TG), :]

        def has(i, b, lag, new):
            return new if b >= lag else not (isinstance(i, int) and i == 0)

        @blk.sync
        def _(sp):
            if not causal:
                sp.dma_start(kv_in[:, :, :], ctx_dram[:, 0:TG, :]).then_inc(kv_loaded, 16)
                with sp.Fori(0, N - 1) as k:
                    wait_apart(sp, kv_loaded, k * 16 + 16, mark)
                    wait_apart(sp, cT_ready, k + 1, mark)
                    sp.dma_start(kv_in[:, :, :], ctx_dram[:, bass.ds(k * TG + TG, TG), :]).then_inc(kv_loaded, 16)
                sp.wait_ge(kv_loaded, 16 * N)

        @blk.gpsimd
        def _(pool):
            pool.memset(vB[:, :, :, :, :], 0.0).then_inc(cleared, 1)
            pool.wait_ge(ybias_done, 1)

            def prepare(j, u, b):
                bias = ybias[:, :].unsqueeze(1).to_broadcast([P, TG, D])
                if causal:
                    if b == 2:
                        pool.wait_ge(z_done, j * TG + TG)
                        pool.tensor_tensor(z[:, :, :], z[:, :, :], bias, ALU.add).then_inc(base_done, 1)
                    if b == 3:
                        pool.wait_ge(base_done, 2 * j + 1)
                        pool.wait_ge(an_done, j * TG + TG)
                        pool.tensor_tensor(step_rows(j), z[:, :, :], step_rows(j), ALU.add).then_inc(base_done, 1)
                    if b in (3, 4):
                        k = b - 3
                        pool.wait_ge(qk_left, j * NQ + 3 + k)
                        pool.tensor_tensor(ra[:, k, :], ra[:, k, :], rb[:, k, :], ALU.add).then_inc(rope_done, 1)
                elif b == 2:
                    pool.wait_ge(an_done, j * TG + TG)
                    pool.tensor_tensor(step_rows(j), bias, step_rows(j), ALU.add).then_inc(base_done, 2)
                if b in (4, 5):
                    pool.wait_ge(rope_done, j * 2 + (1 if causal else 2))
                    for k in (0, 1) if b == 4 else (2, 3):
                        pool.tensor_tensor(qg[:, u, :, k, :], by_row(ra[:, 0, :]),
                                           m_group[:, k:k + 1].unsqueeze(2).to_broadcast([D, NB, SEQ]),
                                           ALU.mult).then_inc(qg_done, 1)

            def step(i, u, new, ahead):
                for b in B:
                    r = i * NB + b
                    if has(i, b, 1, new):
                        pool.wait_ge(rden_done, r)
                        k = (b - 1) % PB
                        pool.tensor_tensor(prob[:, k, :, :], prob[:, k, :, :],
                                           rden[:, k, :].unsqueeze(2).to_broadcast([P, H, SEQ]), ALU.mult).then_inc(prob_done, 1)
                    if ahead:
                        prepare(i + 1, 1 - u, b)

            for b in B:
                prepare(0, 0, b)
            pipelined(pool, N, step)

        @blk.scalar
        def _(act):
            act.preload_act_table_set("natural_log_exp_and_others")
            act.wait_ge(moments_step, 6)
            act.activation(xr[:, 0, :], xvar[:, 1, :], ACT.Ln, bias=g.ln_eps[:, :], scale=1.0 / D).then_inc(ln_step, 1)
            act.wait_ge(ln_step, 1)
            act.activation(xr[:, 1, :], xr[:, 0, :], ACT.Exp, scale=-0.5).then_inc(ln_step, 1)
            if causal:
                act.wait_ge(rr_done, 2)
                act.activation(xr[:, 2, :], xr[:, 4, :], ACT.Ln, bias=g.ln_eps[:, :], scale=1.0 / D).then_inc(ln_step, 1)
                act.wait_ge(ln_step, 3)
                act.activation(xr[:, 2, :], xr[:, 2, :], ACT.Exp, scale=-0.5).then_inc(ln_step, 1)

            def prepare(j, u, b):
                if b == 1:
                    act.wait_ge(aT_ready, j + 1)
                    if causal:
                        act.activation(aT[:, :], aT_ps[:, :], ACT.Identity, bias=cols[:, 6:7], scale=cols[:, 5:6]).then_inc(aT_done, 1)
                    else:
                        act.activation(aT[:, :], aT_ps[:, :], ACT.Copy).then_inc(aT_done, 1)
                        act.wait_ge(cT_ready, j + 1)
                        act.activation(cT[:, :], cT_ps[:, :], ACT.Copy).then_inc(cT_done, 1)
                if b == 2 and not causal:
                    for k in range(2):
                        act.wait_ge(qk_ready, j * 2 + k + 1)
                        act.activation(ra[:, k, :], qk_ps[k][:, :], ACT.Identity, bias=cols[:, k:k + 1]).then_inc(rope_done, 1)
                if b in (4, 5, 6):
                    if b == 4:
                        act.wait_ge(rope_done, j * 2 + 2)
                    for m in ((0,), (1, 2), (3,))[b - 4]:
                        act.activation(km[:, u, :, m, :], by_row(ra[:, 1, :]), ACT.Copy,
                                       scale=m_member[:, m:m + 1]).then_inc(km_done, 1)
                if b in (5, 6):
                    h = b - 5
                    if h == 0:
                        act.wait_ge(v_ready, j + 1)
                    for half in range(2):
                        for p in range(2):
                            m = 2 * p + half
                            src = v_ps[SEQ * h:SEQ * h + SEQ, :].rearrange("p (t g m e) -> p t g m e", t=TG, g=G, m=M)
                            dst = vB[SEQ * half:SEQ * half + SEQ, u, :, p, :].rearrange("p (t h) (g m e) -> p t h g m e", h=2, g=G, m=M)
                            op = act.activation(dst[:, :, h, :, m, :], src[:, :, :, m, :], ACT.Copy)
                    op.then_inc(vB_done, 1)

            act.wait_ge(cleared, 1)

            def step(i, u, new, ahead):
                for b in B:
                    r = i * NB + b
                    if b == VALUES and has(i, 0, 1, new):
                        act.wait_ge(pv_done, r - VALUES)
                        act.activation(atT[:, :], at_ps[:, :], ACT.Copy).then_inc(atT_done, 1)
                    if has(i, b, TRANSPOSE, new):
                        act.wait_ge(pT_ready, r - TRANSPOSE + 1)
                        if has(i, b, TRANSPOSE + 2, new or b < TRANSPOSE + 2):
                            act.wait_ge(pv_done, r - TRANSPOSE - 1)
                        act.activation(pT[:, (b - TRANSPOSE) % 2, :], pT_ps[(b - TRANSPOSE) % 2][:, :], ACT.Copy).then_inc(pT_done, 1)
                    if new:
                        act.wait_ge(sub_done, r + 1)
                        act.activation(prob[:, b % PB, :, :], prob[:, b % PB, :, :], ACT.Exp, scale=SCALE).then_inc(exp_done, 1)
                    if ahead:
                        prepare(i + 1, 1 - u, b)

            for b in B:
                prepare(0, 0, b)
            pipelined(act, N, step)

        @blk.tensor
        def _(pe):
            pe.wait_ge(casts_done, 3 if causal else 2)
            pe.matmul(y_ps[:, 0:D], bvb[:, :], wo[:, :], start=True, stop=True).then_inc(bias_ready, 1)
            pe.wait_ge(ybias_done, 1)

            def project(j, k, left):
                if left is not None:
                    pe.wait_ge(qk_left, left)
                pe.matmul(qk_ps[k][:, :], wqk[:, k, :], (cT if k % 2 else aT)[:, :], start=True, stop=True).then_inc(qk_ready, 1)

            def prepare(j, u, b):
                if b == 1:
                    if not (isinstance(j, int) and j == 0):
                        pe.wait_ge(vB_done, 2 * j)
                    for t in T:
                        pe.wait_ge(an_done, j * TG + t + 1)
                        mm = pe.transpose(aT_ps[:, P * t:P * t + P], an[:, t, :], g.ident[:, :])
                    mm.then_inc(aT_ready, 1)
                    if not causal:
                        pe.wait_ge(kv_loaded, j * 16 + 16)
                        for t in T:
                            mm = pe.transpose(cT_ps[:, P * t:P * t + P], kv_in[:, t, :], g.ident[:, :])
                        mm.then_inc(cT_ready, 1)
                if b == 2:
                    pe.wait_ge(aT_done, j + 1)
                    project(j, 0, None)
                    if not causal:
                        pe.wait_ge(cT_done, j + 1)
                    project(j, 1, None)
                if causal and b == 3:
                    project(j, 2, None)
                    project(j, 3, j * NQ + 1)
                if b == 4:
                    if causal:
                        pe.wait_ge(qk_left, j * NQ + 2)
                    else:
                        pe.wait_ge(rope_done, 2 * j + 2)
                    for t in T:
                        mm = pe.matmul(v_ps[:, D * t:D * t + D], cT[:, P * t:P * t + P], wv[:, :], start=True, stop=True)
                    mm.then_inc(v_ready, 1)

            def step(i, u, new, ahead):
                for b in B:
                    r = i * NB + b
                    if new:
                        bank = s_ps[b % 2]
                        if b == 0:
                            pe.wait_ge(qg_done, i * G + G)
                            pe.wait_ge(km_done, i * M + M)
                        if has(i, b, 2, new):
                            pe.wait_ge(sub_done, r - 1)
                        if causal:
                            pe.matmul(bank[:, :], ident16[:, :], cm[:, :].unsqueeze(1).to_broadcast([P, H, SEQ]),
                                      start=True, stop=False, skip_group_check=True)
                        for half in range(2):
                            mm = pe.matmul(bank[:, 256 * half:256 * half + 256], qg[:, u, b, 2 * half:2 * half + 2, :],
                                           km[:, u, b, :, :], start=not causal, stop=True, skip_group_check=True)
                        mm.then_inc(s_ready, 1)
                    if has(i, b, TRANSPOSE, new):
                        k = (b - TRANSPOSE) % PB
                        pe.wait_ge(prob_done, r - TRANSPOSE + 1)
                        if has(i, b, TRANSPOSE + 2, new or b < TRANSPOSE + 2):
                            pe.wait_ge(pT_done, r - TRANSPOSE - 1)
                        for c in range(4):
                            mm = pe.transpose(pT_ps[(b - TRANSPOSE) % 2][:, P * c:P * c + P], prob[:, k, 2 * c:2 * c + 2, :], g.ident[:, :])
                        mm.then_inc(pT_ready, 1)
                    if has(i, b, VALUES, new):
                        pe.wait_ge(pT_done, r - VALUES + 1)
                        row, v = (b - VALUES) % NB, u if b >= VALUES else 1 - u
                        if row == 0:
                            pe.wait_ge(vB_done, 2 * i + 2)
                            if has(i, 0, 1, new):
                                pe.wait_ge(atT_done, i)
                        probs = pT[:, (b - VALUES) % 2, :].rearrange("p (h j g s) -> p h j g s", h=2, j=2, g=2)
                        for gr in range(G):
                            q = slice(32 * gr, 32 * gr + 32)
                            for j in range(2):
                                mm = pe.matmul(at_ps[q, SEQ * row:SEQ * row + SEQ], vB[:, v, row, j, q],
                                               probs[:, gr // 2, j, gr % 2, :], start=(j == 0), stop=(j == 1),
                                               tile_position=(0, 32 * gr), skip_group_check=True)
                        mm.then_inc(pv_done, 1)
                    if ahead:
                        prepare(i + 1, 1 - u, b)
                    if b == 5 and has(i, 0, 1, new):
                        pe.wait_ge(atT_done, i)
                        if ahead and causal:
                            pe.wait_ge(qk_left, i * NQ + 2 * NQ)
                        for t in T:
                            mm = pe.matmul(y_ps[:, D * t:D * t + D], atT[:, P * t:P * t + P], wo[:, :], start=True, stop=True)
                        mm.then_inc(y_ready, 1)

            for b in B:
                prepare(0, 0, b)
            pipelined(pe, N, step)

        @blk.vector
        def _(dve):
            ln_moments(dve, g.st, xvar, moments_step, 0)
            dve.tensor_copy(ident16[:, :], g.ident[:, :]).then_inc(casts_done, 1)
            dve.tensor_copy(bvb[:, :], cols[:, 4:5].to_broadcast([D, P])).then_inc(casts_done, 1)
            if causal:
                dve.tensor_copy(cm[:, :], cm32[:, :]).then_inc(casts_done, 1)
            dve.wait_ge(bias_ready, 1)
            dve.tensor_tensor(ybias[:, :], y_ps[:, 0:D], bo[:, :], ALU.add).then_inc(ybias_done, 1)
            dve.wait_ge(ln_step, 2)
            if causal:
                dve.tensor_tensor(xr[:, 4, :], xvar[:, 1, :], xr[:, 1, :], ALU.mult).then_inc(rr_done, 1)
                dve.wait_ge(rr_done, 1)
                dve.tensor_tensor(xr[:, 4, :], xr[:, 4, :], xr[:, 1, :], ALU.mult).then_inc(rr_done, 1)
                dve.wait_ge(ln_step, 4)
                dve.tensor_tensor(xr[:, 3, :], xr[:, 1, :], xr[:, 2, :], ALU.mult).then_inc(rr_done, 1)
                dve.wait_ge(rr_done, 3)

            def prepare(j, u, b):
                if b == 0:
                    if not (isinstance(j, int) and j == 0):
                        dve.wait_ge(aT_ready, j)
                    for t in T:
                        n = j * TG + t
                        dve.tensor_scalar(an[:, t, :], g.x[:, n, :], xvar[:, 0, bass.ds(n, 1)], xr[:, 3 if causal else 1, bass.ds(n, 1)],
                                          ALU.subtract, ALU.mult).then_inc(an_done, 1)
                if causal and b == 1:
                    if not (isinstance(j, int) and j == 0):
                        dve.wait_ge(base_done, 2 * j)
                    for t in T:
                        n = j * TG + t
                        dve.tensor_scalar(z[:, t, :], g.x[:, n, :], xvar[:, 0, bass.ds(n, 1)], xr[:, 1, bass.ds(n, 1)],
                                          ALU.subtract, ALU.mult).then_inc(z_done, 1)
                if causal and b in (2, 3):
                    if b == 2 and not (isinstance(j, int) and j == 0):
                        dve.wait_ge(km_done, j * M)
                        dve.wait_ge(qg_done, j * G)
                    for k in ((0, 1), (2, 3))[b - 2]:
                        dve.wait_ge(qk_ready, j * NQ + k + 1)
                        dve.scalar_tensor_tensor(out=by_row((rb if k >= 2 else ra)[:, k % 2, :]), in0=by_row(qk_ps[k][:, :]),
                                                 scalar=cols[:, k:k + 1],
                                                 in1=rope[:, k // 2, :].unsqueeze(1).to_broadcast([D, NB, SEQ]),
                                                 op0=ALU.add, op1=ALU.mult).then_inc(qk_left, 1)
            def step(i, u, new, ahead):
                for b in B:
                    r = i * NB + b
                    k = (b - 1) % PB
                    if new:
                        scores = s_ps[b % 2][:, :].rearrange("p (h t) -> p h t", t=SEQ)
                        dve.wait_ge(s_ready, r + 1)
                        dve.tensor_reduce(nm[:, b % PB, :], scores, AX.X, ALU.max).then_inc(nm_done, 1)
                    if has(i, b, 1, new):
                        dve.wait_ge(exp_done, r)
                        dve.tensor_reduce(rden[:, k, :], prob[:, k, :, :], AX.X, ALU.add).then_inc(sum_done, 1)
                    if new:
                        dve.wait_ge(nm_done, r + 1)
                        if has(i, b, PB, new):
                            dve.wait_ge(pT_ready, r - PB + 1)
                        dve.tensor_tensor(prob[:, b % PB, :, :], scores,
                                          nm[:, b % PB, :].unsqueeze(2).to_broadcast([P, H, SEQ]), ALU.subtract).then_inc(sub_done, 1)
                    if has(i, b, 1, new):
                        dve.wait_ge(sum_done, r)
                        dve.reciprocal(rden[:, k, :], rden[:, k, :]).then_inc(rden_done, 1)
                    if b in (6, 7) and has(i, 0, 1, new):
                        if b == 6:
                            dve.wait_ge(y_ready, i)
                            dve.wait_ge(base_done, 2 * i)
                            dve.tensor_tensor(step_rows(i - 1), y_ps[:, :].rearrange("p (t d) -> p t d", t=TG),
                                              step_rows(i - 1), ALU.add).then_inc(x_new, 1)
                        else:
                            dve.wait_ge(x_new, i)
                            for t in T:
                                n = i * TG - TG + t
                                dve.bn_stats(g.st[:, n, :], g.x[:, n, :]).then_inc(st_done, 1)
                    if ahead:
                        prepare(i + 1, 1 - u, b)

            for b in B:
                prepare(0, 0, b)
            pipelined(dve, N, step)
            dve.wait_ge(st_done, g.tiles)


class Shared:
    pass


RESIDENT = ("ml_wg", "ml_gate_b", "ml_scale", "ml_m_h2", "ml_m_pair", "ml_keep", "ml_restart", "ml_m_par", "ml_m_hp",
            "ml_causal", "r0_gate", "r0_first", "se_w1", "se_w2", "se_sel", "sa_wqk", "sa_wv", "sa_wo", "sa_bo",
            "sa_cols", "at_rope", "at_causal", "xa_wqk", "xa_wv", "xa_wo", "xa_bo", "xa_cols",
            "r1_gate", "r1_first", "r1_wg1", "r1_bg1", "r1_bg2", "le_we", "le_be")


def decoder_kernel(nc, w, x_dram, ctx_dram, out_dram, tiles=64):
    g = Shared()
    g.tiles = tiles
    with Arena(nc, "all") as a:
        g.x = a.sb("x", [P, tiles, D])
        g.st = a.sb("st", [P, tiles, 6])
        g.rw = a.sb("rw", [P, tiles, 20])
        g.ident = a.sb("ident", [P, P])
        g.c = {key: a.sb(key, list(w[key].shape)) for key in RESIDENT}
        g.ln_eps = a.sb("ln_eps", [P, 1])
        xv = x_dram.rearrange("b s d -> (b s) d").rearrange("(t p) d -> p t d", p=P)
        cv = ctx_dram.rearrange("b s d -> (b s) d").rearrange("(t p) d -> p t d", p=P)
        ctx_rows = ctx_dram.rearrange("b s d -> s b d")
        ov = out_dram.rearrange("b s d -> (b s) d").rearrange("(t p) d -> p t d", p=P)
        linear_attention(nc, g, w, xv)
        mlstm(nc, g, w, ctx_rows)
        with Arena(nc, "moe0") as e:
            g.xT = e.sb("xT", [D, tiles * P])
            normed_transposed(nc, g, w, "r0", hidden=False)
            silu_experts(nc, g, w)
        softmax_attention(nc, g, w, "sa", None)
        softmax_attention(nc, g, w, "xa", cv)
        with Arena(nc, "moe1") as e:
            g.xT = e.sb("xT", [D, tiles * P])
            normed_transposed(nc, g, w, "r1", hidden=True)
            linear_experts(nc, g, w, ov)


def shape_constants():
    import numpy as np
    hd = 8
    pos = np.arange(64, dtype=np.float32)[:, None]
    freq = (1.0 / 10000.0 ** (np.arange(0, hd, 2, dtype=np.float32) / hd)).astype(np.float32)
    ang = pos * freq[None]
    cos, sin = np.cos(ang).astype(np.float32), np.sin(ang).astype(np.float32)
    c = {}
    c["ident"] = np.eye(128, dtype=np.float32)
    c["rope_c"] = np.tile(np.repeat(cos, 2, axis=1), (2, 32))
    s = np.stack([sin, -sin], axis=-1).reshape(64, 8)
    c["rope_s"] = np.tile(s, (2, 32))
    head = np.arange(128) // 8
    same = (head[:, None] == head[None, :]).astype(np.float32)
    c["kv_mask"] = np.concatenate([same, (head[:, None] == np.arange(16)[None]).astype(np.float32)], axis=1)
    p, h8 = np.arange(128), np.arange(8)
    c["ml_m_h2"] = (p[:, None] // 16 % 2 == np.arange(2)[None])
    c["ml_m_pair"] = (p[:, None] // 32 == np.arange(4)[None]) / 16 ** 0.5
    first = np.arange(512) % 64 == 0
    c["ml_keep"] = np.tile(1.0 - first, (8, 1))
    c["ml_restart"] = np.tile(-1e30 * first, (8, 1))
    c["ml_m_par"] = (h8[:, None] % 2 == np.arange(2)[None])
    c["ml_m_hp"] = -1.0 * (h8[:, None] // 2 == np.arange(4)[None])
    t, s = np.arange(64)[:, None], np.arange(64)[None]
    c["ml_causal"] = np.tile(np.where(t <= s, 0.0, -1e30), (2, 1))
    c["ml_argL"] = np.broadcast_to((h8[:, None] % 2 == np.arange(2)[None])[:, None, :, None], (8, 8, 2, 64))
    c["ml_argR"] = np.broadcast_to((h8[:, None] // 2 == np.arange(4)[None])[:, None, :, None], (8, 8, 4, 64))
    for name, experts in (("r0_first", 8), ("r1_first", 20)):
        c[name] = np.broadcast_to(np.arange(experts) > 0, (128, 64, experts))
    unit = np.arange(1024)
    owner = np.where(unit < 768, unit // 96, 8)
    c["se_sel"] = (owner[None, :] == np.arange(9)[:, None]).reshape(9, 8, 128)
    c["at_rope"] = np.stack([np.tile(np.repeat(cos.T, 2, axis=0), (16, 1)),
                             np.tile(np.stack([-sin.T, sin.T], axis=1).reshape(8, 64), (16, 1))], axis=1)
    c["at_causal"] = np.tile(np.where(s <= t, 0.0, -1e30), (2, 1))
    return {k: np.ascontiguousarray(v, dtype=np.float32) for k, v in c.items()}


def laid_out(inputs):
    import numpy as np
    i = inputs
    c = {}
    c["la_wqkv"] = np.concatenate([i["L0_attn_Wq"], i["L0_attn_Wk"], i["L0_attn_Wv"]], axis=1)
    c["la_wo"] = i["L0_attn_Wo"]
    f32 = np.float32
    wg = np.zeros((128, 3, 40), f32)
    wg[:, :, 0:8] = i["L0_xattn_igate_w"].reshape(8, 3, 128).transpose(2, 1, 0)
    wg[:, :, 32:40] = i["L0_xattn_fgate_w"].reshape(8, 3, 128).transpose(2, 1, 0)
    c["ml_wg"] = wg
    gb = np.zeros((40, 2), f32)
    gb[0:8, 0] = i["L0_xattn_igate_b"]
    gb[32:40, 1] = i["L0_xattn_fgate_b"]
    c["ml_gate_b"] = gb
    c["ml_scale"] = np.tile(i["L0_xattn_ln_scale"], (128, 1))
    w1, ws1 = i["L0_ffn_W1"], i["L0_ffn_Ws1"]
    up = np.zeros((2, 1024, 128), f32)
    for k in range(2):
        up[k, 0:768] = w1[:, 96 * k:96 * k + 96].reshape(768, 128)
        up[k, 768:960] = ws1[192 * k:192 * k + 192]
    c["se_w1"] = up.transpose(2, 0, 1).reshape(128, 2, 8, 128)
    down = np.zeros((1024, 128), f32)
    down[0:768] = i["L0_ffn_W2"].transpose(0, 2, 1).reshape(768, 128)
    down[768:960] = i["L0_ffn_Ws2"].T
    c["se_w2"] = down.reshape(8, 128, 128).transpose(1, 0, 2)
    partner = np.arange(128) ^ 1
    feature = np.arange(128)[:, None]
    masks = [feature // 32 == np.arange(4)[None], feature // 8 % 4 == np.arange(4)[None]]
    for name, src, extra in (("sa", "L1_attn", True), ("xa", "L1_xattn", False)):
        wq, wk = i[src + "_Wq"], i[src + "_Wk"]
        bq, bk = i[src + "_bq"], i[src + "_bk"]
        qk = [wq, wk] + ([wq[:, partner], wk[:, partner]] if extra else [])
        c[name + "_wqk"] = np.stack(qk, axis=1)
        c[name + "_wv"], c[name + "_wo"] = i[src + "_Wv"], i[src + "_Wo"]
        c[name + "_bo"] = np.tile(i[src + "_bo"], (128, 1))
        col = [bq, bk, bq[partner], bk[partner], i[src + "_bv"]]
        col += [i["L1_attn_ln_gamma"], i["L1_attn_ln_beta"], np.zeros(128, f32)]
        c[name + "_cols"] = np.concatenate([np.stack(col, axis=1)] + [m.astype(f32) for m in masks], axis=1)
    c["le_we"] = i["L1_ffn_We"].transpose(1, 0, 2).reshape(128, 5, 512)
    c["le_be"] = i["L1_ffn_be"]
    c["r0_gate"] = i["L0_ffn_gate_w"].T
    c["r1_gate"] = i["L1_ffn_wg2"][:, 0:20]
    c["r1_wg1"] = i["L1_ffn_wg1"]
    c["r1_bg1"] = i["L1_ffn_bg1"].reshape(32, 1)
    c["r1_bg2"] = np.tile(i["L1_ffn_bg2"][0:20], (128, 1))
    return {k: np.ascontiguousarray(v) for k, v in c.items()}


def kernel(**inputs):
    import numpy as _np
    import concourse.bacc as _bacc
    from concourse import mybir as _mybir
    from concourse.bass_utils import run_bass_kernel_spmd as _run

    inputs = {k: _np.asarray(v) for k, v in inputs.items()}
    nc = _bacc.Bacc("TRN2", target_bir_lowering=False, num_devices=1)
    arrays = {"x": inputs["x"], "ctx": inputs["ctx_1024"], **shape_constants(), **laid_out(inputs)}
    aps = {k: nc.dram_tensor(f"in_{k}", v.shape, _mybir.dt.from_np(v.dtype), kind="ExternalInput").ap()
           for k, v in arrays.items()}
    out = nc.dram_tensor("out", inputs["x"].shape, _mybir.dt.float32, kind="ExternalOutput").ap()
    decoder_kernel(nc, aps, aps["x"], aps["ctx"], out)
    r = _run(nc, [{f"in_{k}": _np.ascontiguousarray(v) for k, v in arrays.items()}], core_ids=[0])
    return r.results[0]["out"]
```
